# Optimizing a Trainium2 kernel written in Bass

```python
import numpy as np
import jax
import jax.numpy as jnp

def _softmax(x, axis=-1):
    return jax.nn.softmax(x, axis=axis)

def _gelu(x):
    return jax.nn.gelu(x, approximate=True)

def _silu(x):
    return jax.nn.silu(x)

def _sigmoid(x):
    return jax.nn.sigmoid(x)

def _layernorm(x, axis=-1, eps=1e-05):
    m = jnp.mean(x, axis=axis, keepdims=True)
    v = jnp.var(x, axis=axis, keepdims=True)
    return (x - m) / jnp.sqrt(v + eps)

def _scatter_add(tgt, idx, src, axis=0):
    return tgt.at[idx].add(src)

def _segment_sum(src, seg, n):
    return jax.ops.segment_sum(src, seg, n)
kernel_name = 'mk_xattn_ffn_d2_seqx_r4_b1fe95'

def setup_inputs(seed: int=0):
    np.random.seed(seed)
    _w = jnp.asarray

    def _rec_inputs():
        import jax
        import jax.numpy as jnp
        _rk = jax.random.key(seed)
        x = -1.394e-06 + 0.9999 * jax.random.normal(jax.random.fold_in(_rk, 1), (4, 512, 256), jnp.float32)
        _lenS = 512 - jax.random.randint(jax.random.fold_in(_rk, 7), (4,), 0, max(1, 512 // 4) + 1, jnp.int32)
        _lenS2 = 1024 - jax.random.randint(jax.random.fold_in(_rk, 8), (4,), 0, max(1, 1024 // 4) + 1, jnp.int32)
        _ctx_1024P = jax.random.normal(jax.random.fold_in(_rk, 11), (4, 16, 256), jnp.float32)
        _ctx_1024c = jax.random.dirichlet(jax.random.fold_in(_rk, 511), 0.3 * jnp.ones((16,), jnp.float32), (4, 1024))
        _ctx_1024t = jnp.einsum('bsk,bkd->bsd', _ctx_1024c, _ctx_1024P)
        _ctx_1024t = _ctx_1024t * jax.lax.rsqrt(jnp.mean(jnp.square(_ctx_1024t)) + 1e-12) * 0.953939
        ctx_1024 = -0.000392918 + 0.999932 * (_ctx_1024t + 0.3 * jax.random.normal(jax.random.fold_in(_rk, 611), (4, 1024, 256), jnp.float32))
        _validS = jnp.arange(512)[None, :] < _lenS[:, None]
        _validS2 = jnp.arange(1024)[None, :] < _lenS2[:, None]
        _causal = jnp.tril(jnp.ones((512, 512), dtype=bool))
        mask_BxS2_bk0 = jnp.logical_not(jnp.broadcast_to(_validS2[:, :], (4, 1024)))
        return (x, ctx_1024, mask_BxS2_bk0)
    x, ctx_1024, mask_BxS2_bk0 = _rec_inputs()

    def _L0_xattn_setup():
        import jax, jax.numpy as jnp
        import numpy as np
        DIM = 256
        DIM_LATENT = 256
        DIM_HEAD = 64
        INNER = max(DIM, DIM_LATENT)
        HEADS = INNER // DIM_HEAD
        SCALE = DIM_HEAD ** (-0.5)
        LN_EPS = 1e-05
        RMS_EPS = 1e-08

        def layernorm(x, g, b):
            mu = jnp.mean(x, axis=-1, keepdims=True)
            var = jnp.mean(jnp.square(x - mu), axis=-1, keepdims=True)
            return (x - mu) * jax.lax.rsqrt(var + LN_EPS) * g + b

        def rmsnorm(x, gamma):
            n = jnp.linalg.norm(x, axis=-1, keepdims=True) * x.shape[-1] ** (-0.5)
            return x / jnp.maximum(n, RMS_EPS) * gamma
        key = jax.random.key(seed)
        ks = jax.random.split(key, 8)
        b, n, nl = (8, 512, 128)
        x = jax.random.normal(ks[0], (b, n, DIM), dtype=jnp.float32)
        latents = jax.random.normal(ks[1], (b, nl, DIM_LATENT), dtype=jnp.float32)
        mask = jax.random.randint(ks[2], (b, n), 0, 2).astype(bool)
        init = lambda k, shape, fan_in: jax.random.normal(k, shape, jnp.float32) * fan_in ** (-0.5)
        return {'x': x, 'latents': latents, 'mask': mask, 'ln_x_g': jnp.ones((DIM,), jnp.float32), 'ln_x_b': jnp.zeros((DIM,), jnp.float32), 'ln_l_g': jnp.ones((DIM_LATENT,), jnp.float32), 'ln_l_b': jnp.zeros((DIM_LATENT,), jnp.float32), 'q_gamma': jnp.ones((DIM_HEAD,), jnp.float32), 'k_gamma': jnp.ones((DIM_HEAD,), jnp.float32), 'W_q': init(ks[3], (DIM_LATENT, INNER), DIM_LATENT), 'W_kv': init(ks[4], (DIM, 2 * INNER), DIM), 'W_out': init(ks[5], (INNER, DIM_LATENT), INNER), 'b_out': jnp.zeros((DIM_LATENT,), jnp.float32)}
    _L0_xattn_all = _L0_xattn_setup()
    _L0_xattn_in = {k: v for k, v in _L0_xattn_all.items() if k in ('ln_x_g', 'ln_x_b', 'ln_l_g', 'ln_l_b', 'q_gamma', 'k_gamma', 'W_q', 'W_kv', 'W_out', 'b_out')}
    del _L0_xattn_all

    def _L0_ffn_setup():
        import jax, jax.numpy as jnp
        import numpy as np
        H = 256
        M = 128
        E = 16
        TOP_K = 2
        SCALE = 2.5
        NORM_TOPK = True
        B, S = (1, 256)

        def _moe(x, gate_w, w_gate, w_up, w_down, ws_gate, ws_up, ws_down):
            T = x.shape[0]
            shared = jax.nn.silu(x @ ws_gate) * (x @ ws_up) @ ws_down
            scores = jax.nn.sigmoid(x.astype(jnp.float32) @ gate_w.T.astype(jnp.float32))
            topk_w, topk_idx = jax.lax.top_k(scores, TOP_K)
            if NORM_TOPK and TOP_K > 1:
                topk_w = topk_w / (topk_w.sum(-1, keepdims=True) + 1e-20)
            topk_w = topk_w * SCALE
            route = jnp.zeros((T, E), topk_w.dtype).at[jnp.arange(T)[:, None], topk_idx].set(topk_w)
            g = jnp.einsum('th,ehm->etm', x, w_gate)
            u = jnp.einsum('th,ehm->etm', x, w_up)
            eo = jnp.einsum('etm,emh->eth', jax.nn.silu(g) * u, w_down)
            routed = jnp.einsum('te,eth->th', route.astype(x.dtype), eo)
            return routed + shared
        key = jax.random.key(seed)
        ks = jax.random.split(key, 8)
        std = 0.02
        return {'hidden_states': jax.random.normal(ks[0], (B, S, H), jnp.float32), 'gate_w': jax.random.normal(ks[1], (E, H), jnp.float32) * std, 'w_gate': jax.random.normal(ks[2], (E, H, M), jnp.float32) * std, 'w_up': jax.random.normal(ks[3], (E, H, M), jnp.float32) * std, 'w_down': jax.random.normal(ks[4], (E, M, H), jnp.float32) * std, 'ws_gate': jax.random.normal(ks[5], (H, M), jnp.float32) * std, 'ws_up': jax.random.normal(ks[6], (H, M), jnp.float32) * std, 'ws_down': jax.random.normal(ks[7], (M, H), jnp.float32) * std}
    _L0_ffn_all = _L0_ffn_setup()
    _L0_ffn_in = {k: v for k, v in _L0_ffn_all.items() if k in ('gate_w', 'w_gate', 'w_up', 'w_down', 'ws_gate', 'ws_up', 'ws_down')}
    del _L0_ffn_all

    def _L1_xattn_setup():
        import jax, jax.numpy as jnp
        import numpy as np
        HEADS = 16
        LOCAL_ATTN_CTX = 128

        def _strided_permute(x, local_attn_ctx):
            n, t, e = x.shape
            bT = t // local_attn_ctx
            return x.reshape(n, bT, local_attn_ctx, e).transpose(0, 2, 1, 3).reshape(n, t, e)

        def _strided_unpermute(a, local_attn_ctx):
            n, t, e = a.shape
            bT = t // local_attn_ctx
            return a.reshape(n, local_attn_ctx, bT, e).transpose(0, 2, 1, 3).reshape(n, t, e)
        key = jax.random.key(seed)
        k1, k2, k3 = jax.random.split(key, 3)
        shape = (4, 1024, 256)
        return {'q': jax.random.normal(k1, shape, dtype=jnp.float32), 'k': jax.random.normal(k2, shape, dtype=jnp.float32), 'v': jax.random.normal(k3, shape, dtype=jnp.float32)}
    _L1_xattn_all = _L1_xattn_setup()
    _L1_xattn_in = {k: v for k, v in _L1_xattn_all.items() if k in ()}
    del _L1_xattn_all

    def _L1_ffn_setup():
        import jax, jax.numpy as jnp
        import numpy as np
        S, B, H = (512, 2, 256)
        NUM_HEADS, NUM_KV_HEADS = (16, 4)
        HEAD_DIM = H // NUM_HEADS
        E, TOP_K, FFN = (16, 2, 512)
        CAP_FACTOR = 1.25
        EPS = 1e-05

        def _layernorm(x, w, b):
            mu = jnp.mean(x, axis=-1, keepdims=True)
            var = jnp.mean((x - mu) ** 2, axis=-1, keepdims=True)
            return (x - mu) * jax.lax.rsqrt(var + EPS) * w + b
        key = jax.random.key(seed)
        ks = jax.random.split(key, 6)
        qkv_out = (NUM_HEADS + 2 * NUM_KV_HEADS) * HEAD_DIM
        sdH = 1.0 / np.sqrt(H)
        sdF = 1.0 / np.sqrt(FFN)
        return {'hidden_states': jax.random.normal(ks[0], (S, B, H), jnp.float32), 'ln1_weight': jnp.ones((H,), jnp.float32), 'ln1_bias': jnp.zeros((H,), jnp.float32), 'ln2_weight': jnp.ones((H,), jnp.float32), 'ln2_bias': jnp.zeros((H,), jnp.float32), 'qkv_weight': jax.random.normal(ks[1], (qkv_out, H), jnp.float32) * sdH, 'proj_weight': jax.random.normal(ks[2], (H, H), jnp.float32) * sdH, 'router_weight': jax.random.normal(ks[3], (E, H), jnp.float32) * sdH, 'moe_w1': jax.random.normal(ks[4], (E, FFN, H), jnp.float32) * sdH, 'moe_w2': jax.random.normal(ks[5], (E, H, FFN), jnp.float32) * sdF}
    _L1_ffn_all = _L1_ffn_setup()
    _L1_ffn_in = {k: v for k, v in _L1_ffn_all.items() if k in ('ln1_weight', 'ln1_bias', 'ln2_weight', 'ln2_bias', 'qkv_weight', 'proj_weight', 'router_weight', 'moe_w1', 'moe_w2')}
    del _L1_ffn_all
    return {'x': x, 'ctx_1024': ctx_1024, 'mask_BxS2_bk0': mask_BxS2_bk0, 'L0_xattn_ln_x_g': _L0_xattn_in['ln_x_g'], 'L0_xattn_ln_x_b': _L0_xattn_in['ln_x_b'], 'L0_xattn_ln_l_g': _L0_xattn_in['ln_l_g'], 'L0_xattn_ln_l_b': _L0_xattn_in['ln_l_b'], 'L0_xattn_q_gamma': _L0_xattn_in['q_gamma'], 'L0_xattn_k_gamma': _L0_xattn_in['k_gamma'], 'L0_xattn_W_q': _L0_xattn_in['W_q'], 'L0_xattn_W_kv': _L0_xattn_in['W_kv'], 'L0_xattn_W_out': _L0_xattn_in['W_out'], 'L0_xattn_b_out': _L0_xattn_in['b_out'], 'L0_ffn_gate_w': _L0_ffn_in['gate_w'], 'L0_ffn_w_gate': _L0_ffn_in['w_gate'], 'L0_ffn_w_up': _L0_ffn_in['w_up'], 'L0_ffn_w_down': _L0_ffn_in['w_down'], 'L0_ffn_ws_gate': _L0_ffn_in['ws_gate'], 'L0_ffn_ws_up': _L0_ffn_in['ws_up'], 'L0_ffn_ws_down': _L0_ffn_in['ws_down'], 'L1_ffn_ln1_weight': _L1_ffn_in['ln1_weight'], 'L1_ffn_ln1_bias': _L1_ffn_in['ln1_bias'], 'L1_ffn_ln2_weight': _L1_ffn_in['ln2_weight'], 'L1_ffn_ln2_bias': _L1_ffn_in['ln2_bias'], 'L1_ffn_qkv_weight': _L1_ffn_in['qkv_weight'], 'L1_ffn_proj_weight': _L1_ffn_in['proj_weight'], 'L1_ffn_router_weight': _L1_ffn_in['router_weight'], 'L1_ffn_moe_w1': _L1_ffn_in['moe_w1'], 'L1_ffn_moe_w2': _L1_ffn_in['moe_w2']}

def reference(x, ctx_1024, mask_BxS2_bk0, L0_xattn_ln_x_g, L0_xattn_ln_x_b, L0_xattn_ln_l_g, L0_xattn_ln_l_b, L0_xattn_q_gamma, L0_xattn_k_gamma, L0_xattn_W_q, L0_xattn_W_kv, L0_xattn_W_out, L0_xattn_b_out, L0_ffn_gate_w, L0_ffn_w_gate, L0_ffn_w_up, L0_ffn_w_down, L0_ffn_ws_gate, L0_ffn_ws_up, L0_ffn_ws_down, L1_ffn_ln1_weight, L1_ffn_ln1_bias, L1_ffn_ln2_weight, L1_ffn_ln2_bias, L1_ffn_qkv_weight, L1_ffn_proj_weight, L1_ffn_router_weight, L1_ffn_moe_w1, L1_ffn_moe_w2):
    import jax
    import jax.numpy as jnp

    def _L0_xattn_ref(x, latents, mask, ln_x_g, ln_x_b, ln_l_g, ln_l_b, q_gamma, k_gamma, W_q, W_kv, W_out, b_out):
        import jax, jax.numpy as jnp
        import numpy as np
        DIM = 256
        DIM_LATENT = 256
        DIM_HEAD = 64
        INNER = max(DIM, DIM_LATENT)
        HEADS = INNER // DIM_HEAD
        SCALE = DIM_HEAD ** (-0.5)
        LN_EPS = 1e-05
        RMS_EPS = 1e-08

        def layernorm(x, g, b):
            mu = jnp.mean(x, axis=-1, keepdims=True)
            var = jnp.mean(jnp.square(x - mu), axis=-1, keepdims=True)
            return (x - mu) * jax.lax.rsqrt(var + LN_EPS) * g + b

        def rmsnorm(x, gamma):
            n = jnp.linalg.norm(x, axis=-1, keepdims=True) * x.shape[-1] ** (-0.5)
            return x / jnp.maximum(n, RMS_EPS) * gamma
        b, n, _ = x.shape
        nl = latents.shape[1]
        xn = layernorm(x, ln_x_g, ln_x_b)
        ln = layernorm(latents, ln_l_g, ln_l_b)
        q = ln @ W_q
        kv = jnp.concatenate([xn @ W_kv, ln @ W_kv], axis=1)
        k, v = (kv[..., :INNER], kv[..., INNER:])
        to_heads = lambda t: t.reshape(t.shape[0], t.shape[1], HEADS, DIM_HEAD).transpose(0, 2, 1, 3)
        q, k, v = (to_heads(q), to_heads(k), to_heads(v))
        qn = rmsnorm(q, q_gamma) * SCALE
        kn = rmsnorm(k, k_gamma)
        sim = jnp.einsum('bhid,bhjd->bhij', qn, kn)
        full_mask = jnp.pad(mask, ((0, 0), (0, nl)), constant_values=True)
        neg = -jnp.finfo(sim.dtype).max
        sim = jnp.where(full_mask[:, None, None, :], sim, neg)
        attn = jax.nn.softmax(sim.astype(jnp.float32), axis=-1).astype(sim.dtype)
        out = jnp.einsum('bhij,bhjd->bhid', attn, v)
        out = out.transpose(0, 2, 1, 3).reshape(b, nl, INNER)
        return out @ W_out + b_out

    def _L0_ffn_ref(hidden_states, gate_w, w_gate, w_up, w_down, ws_gate, ws_up, ws_down):
        import jax, jax.numpy as jnp
        import numpy as np
        H = 256
        M = 128
        E = 16
        TOP_K = 2
        SCALE = 2.5
        NORM_TOPK = True
        B, S = (1, 256)

        def _moe(x, gate_w, w_gate, w_up, w_down, ws_gate, ws_up, ws_down):
            T = x.shape[0]
            shared = jax.nn.silu(x @ ws_gate) * (x @ ws_up) @ ws_down
            scores = jax.nn.sigmoid(x.astype(jnp.float32) @ gate_w.T.astype(jnp.float32))
            topk_w, topk_idx = jax.lax.top_k(scores, TOP_K)
            if NORM_TOPK and TOP_K > 1:
                topk_w = topk_w / (topk_w.sum(-1, keepdims=True) + 1e-20)
            topk_w = topk_w * SCALE
            route = jnp.zeros((T, E), topk_w.dtype).at[jnp.arange(T)[:, None], topk_idx].set(topk_w)
            g = jnp.einsum('th,ehm->etm', x, w_gate)
            u = jnp.einsum('th,ehm->etm', x, w_up)
            eo = jnp.einsum('etm,emh->eth', jax.nn.silu(g) * u, w_down)
            routed = jnp.einsum('te,eth->th', route.astype(x.dtype), eo)
            return routed + shared
        b, s, h = hidden_states.shape
        x = hidden_states.reshape(-1, h)
        out = _moe(x, gate_w, w_gate, w_up, w_down, ws_gate, ws_up, ws_down)
        return out.reshape(b, s, h)

    def _L1_xattn_ref(q, k, v):
        import jax, jax.numpy as jnp
        import numpy as np
        HEADS = 16
        LOCAL_ATTN_CTX = 128

        def _strided_permute(x, local_attn_ctx):
            n, t, e = x.shape
            bT = t // local_attn_ctx
            return x.reshape(n, bT, local_attn_ctx, e).transpose(0, 2, 1, 3).reshape(n, t, e)

        def _strided_unpermute(a, local_attn_ctx):
            n, t, e = a.shape
            bT = t // local_attn_ctx
            return a.reshape(n, local_attn_ctx, bT, e).transpose(0, 2, 1, 3).reshape(n, t, e)
        qs = _strided_permute(q, LOCAL_ATTN_CTX)
        ks = _strided_permute(k, LOCAL_ATTN_CTX)
        vs = _strided_permute(v, LOCAL_ATTN_CTX)
        n_state = q.shape[-1] // HEADS
        scale = 1.0 / np.sqrt(n_state).astype(np.float32)
        w = jnp.einsum('nqe,nke->nqk', qs, ks)
        w = jax.nn.softmax(w * scale, axis=-1)
        a = jnp.einsum('nqk,nke->nqe', w, vs)
        return _strided_unpermute(a, LOCAL_ATTN_CTX)

    def _L1_ffn_ref(hidden_states, ln1_weight, ln1_bias, ln2_weight, ln2_bias, qkv_weight, proj_weight, router_weight, moe_w1, moe_w2):
        import jax, jax.numpy as jnp
        import numpy as np
        S, B, H = (512, 2, 256)
        NUM_HEADS, NUM_KV_HEADS = (16, 4)
        HEAD_DIM = H // NUM_HEADS
        E, TOP_K, FFN = (16, 2, 512)
        CAP_FACTOR = 1.25
        EPS = 1e-05

        def _layernorm(x, w, b):
            mu = jnp.mean(x, axis=-1, keepdims=True)
            var = jnp.mean((x - mu) ** 2, axis=-1, keepdims=True)
            return (x - mu) * jax.lax.rsqrt(var + EPS) * w + b
        S_, B_, H_ = hidden_states.shape
        dtype = hidden_states.dtype
        ln1 = _layernorm(hidden_states, ln1_weight, ln1_bias)
        qkv = jnp.einsum('sbh,oh->sbo', ln1, qkv_weight)
        q_sz = NUM_HEADS * HEAD_DIM
        kv_sz = NUM_KV_HEADS * HEAD_DIM
        q = qkv[..., :q_sz].reshape(S_, B_, NUM_HEADS, HEAD_DIM)
        k = qkv[..., q_sz:q_sz + kv_sz].reshape(S_, B_, NUM_KV_HEADS, HEAD_DIM)
        v = qkv[..., q_sz + kv_sz:].reshape(S_, B_, NUM_KV_HEADS, HEAD_DIM)
        rep = NUM_HEADS // NUM_KV_HEADS
        k = jnp.repeat(k, rep, axis=2)
        v = jnp.repeat(v, rep, axis=2)
        scale = 1.0 / np.sqrt(HEAD_DIM)
        scores = jnp.einsum('qbhd,kbhd->bhqk', q, k) * scale
        causal = jnp.tril(jnp.ones((S_, S_), bool))
        scores = jnp.where(causal, scores, jnp.asarray(-1e+30, dtype))
        attn = jax.nn.softmax(scores, axis=-1)
        attn_out = jnp.einsum('bhqk,kbhd->qbhd', attn, v).reshape(S_, B_, H_)
        proj_out = jnp.einsum('sbh,oh->sbo', attn_out, proj_weight)
        hidden_after_attn = hidden_states + proj_out
        ln2 = _layernorm(hidden_after_attn, ln2_weight, ln2_bias).reshape(-1, H_)
        T = ln2.shape[0]
        logits = ln2 @ router_weight.T
        probs = jax.nn.softmax(logits, axis=-1)
        top_p, top_i = jax.lax.top_k(probs, TOP_K)
        cap = int(np.ceil(T * TOP_K / E * CAP_FACTOR))
        exp_idx = top_i.reshape(-1)
        gate = top_p.reshape(-1).astype(dtype)
        tok = jnp.repeat(jnp.arange(T), TOP_K)
        onehot = jax.nn.one_hot(exp_idx, E, dtype=jnp.int32)
        pos = (jnp.cumsum(onehot, axis=0) * onehot).sum(-1) - 1
        keep = pos < cap
        pos_c = jnp.where(keep, pos, cap)
        buf = jnp.zeros((E, cap + 1, H_), dtype)
        buf = buf.at[exp_idx, pos_c].add(ln2[tok] * keep[:, None].astype(dtype))
        h1 = jax.nn.gelu(jnp.einsum('ech,efh->ecf', buf, moe_w1))
        h2 = jnp.einsum('ecf,ehf->ech', h1, moe_w2)
        out_ent = h2[exp_idx, pos_c] * (gate * keep.astype(dtype))[:, None]
        moe_out = jnp.zeros((T, H_), dtype).at[tok].add(out_ent)
        return hidden_after_attn + moe_out.reshape(S_, B_, H_)
    x = x + _L0_xattn_ref(ctx_1024, _layernorm(x, axis=-1), mask_BxS2_bk0, L0_xattn_ln_x_g, L0_xattn_ln_x_b, L0_xattn_ln_l_g, L0_xattn_ln_l_b, L0_xattn_q_gamma, L0_xattn_k_gamma, L0_xattn_W_q, L0_xattn_W_kv, L0_xattn_W_out, L0_xattn_b_out)
    x = x + _L0_ffn_ref(_layernorm(x, axis=-1), L0_ffn_gate_w, L0_ffn_w_gate, L0_ffn_w_up, L0_ffn_w_down, L0_ffn_ws_gate, L0_ffn_ws_up, L0_ffn_ws_down)
    x = x + _L1_xattn_ref(_layernorm(x, axis=-1), ctx_1024, ctx_1024)
    x = x + _L1_ffn_ref(_layernorm(x, axis=-1), L1_ffn_ln1_weight, L1_ffn_ln1_bias, L1_ffn_ln2_weight, L1_ffn_ln2_bias, L1_ffn_qkv_weight, L1_ffn_proj_weight, L1_ffn_router_weight, L1_ffn_moe_w1, L1_ffn_moe_w2)
    return x

_drawn_inputs = setup_inputs


def setup_inputs(seed=0):
    import zlib

    import numpy as np

    out = dict(_drawn_inputs(seed))
    spreads = {'L0_xattn_ln_x_g': (1.0, 0.2),
     'L0_xattn_ln_x_b': (0.0, 0.1),
     'L0_xattn_ln_l_g': (1.0, 0.2),
     'L0_xattn_ln_l_b': (0.0, 0.1),
     'L0_xattn_q_gamma': (1.0, 0.2),
     'L0_xattn_k_gamma': (1.0, 0.2),
     'L0_xattn_b_out': (0.0, 0.1),
     'L1_ffn_ln1_weight': (1.0, 0.2),
     'L1_ffn_ln1_bias': (0.0, 0.1),
     'L1_ffn_ln2_weight': (1.0, 0.2),
     'L1_ffn_ln2_bias': (0.0, 0.343)}
    factors = {'L0_ffn_ws_gate': 3.796,
     'L0_ffn_ws_up': 3.687,
     'L0_ffn_ws_down': 3.689,
     'L0_ffn_gate_w': 2.843,
     'L0_ffn_w_gate': 2.755,
     'L0_ffn_w_up': 2.693}
    for name, (base, spread) in spreads.items():
        noise = np.random.default_rng([zlib.crc32(name.encode()), seed]).standard_normal(out[name].shape)
        drawn = base * np.exp(spread * noise) if base else spread * noise
        out[name] = jnp.asarray(drawn.astype(out[name].dtype))
    for name, factor in factors.items():
        out[name] = (out[name] * factor).astype(out[name].dtype)
    return out
```

```python
from contextlib import ExitStack

import numpy as np

import concourse.bass as bass
from concourse import mybir

F32 = mybir.dt.float32
F32R = mybir.dt.float32r
F16 = mybir.dt.float16
I32 = mybir.dt.int32
U32 = mybir.dt.uint32
U8 = mybir.dt.uint8
ALU = mybir.AluOpType
ACT = mybir.ActivationFunctionType
AX = mybir.AxisListType

P = 128
B, S, D = 4, 512, 256
KC = D // P
TB = S // P
NT = B * TB
SC = 1024
CTB = SC // P
H0, DH0 = 4, 64
NPAIR = H0 // 2
KT0 = TB + CTB
NG = B * 3
E = 16
M0 = 128
F1 = 512
FC1 = F1 // P
NSLOT0 = (2 * NT * P + E * (P - 1)) // P
CAP1 = -(-(NT * P * 2 * 5) // (E * 4))
RT1 = -(-CAP1 // P)
NSLOT1 = E * RT1
H1, KV1, DH1 = 16, 4, 16
NRING = 6
NXG = 5
NYG = 4
RSQRT_SEED = float(0x5F3759DF)
BIG = 1e30

COLS = ("ln_x_g0", "ln_x_g1", "ln_x_b0", "ln_x_b1", "ln_l_g0", "ln_l_g1", "ln_l_b0", "ln_l_b1",
        "ln1_w0", "ln1_w1", "ln1_b0", "ln1_b1", "gamma_q", "gamma_k")
ROWS = {"b_out": (0, D), "ln2_w": (D, D), "ln2_b": (2 * D, D), "gamma_q": (3 * D, DH0), "gamma_k": (3 * D + DH0, DH0)}
NROW = 3 * D + 2 * DH0
NSTEP = NT + 10
CSCALE = 0.25
QKV = (H1 + 2 * KV1) * DH1
DVE_HOTS = 12
NW = 4


def bc(ap, axis, n):
    a = ap.unsqueeze(axis)
    shape = list(a.shape)
    shape[axis] = n
    return a.broadcast_to(shape)


class BankRing:

    def __init__(self, banks, n, unit_done, evacuated):
        self.banks, self.n, self.unit_done, self.evac = banks, n, unit_done, evacuated
        self.unit = {}

    def take(self, pe, key):
        u = len(self.unit)
        self.unit[key] = u
        if u >= self.n:
            pe.wait_ge(self.evac[u % self.n], u // self.n)
        return self.bank(key)

    def bank(self, key):
        return self.banks[:, self.unit[key] % self.n, :]

    def done(self, key):
        return self.unit[key] + 1

    def evacuated(self, key):
        return self.evac[self.unit[key] % self.n]

    def wait_done(self, eng, key):
        eng.wait_ge(self.unit_done, self.done(key))

    def wait_evacuated(self, eng, key):
        eng.wait_ge(self.evacuated(key), self.unit[key] // self.n + 1)


def build(nc, a, out):
    ctx = ExitStack()
    with ctx:
        def sb(name, shape, dt=F32):
            return ctx.enter_context(nc.sbuf_tensor(name, shape, dt))

        def sem(name):
            return ctx.enter_context(nc.semaphore(name))

        x = sb("x_res", [P, NT, D])
        ident = sb("ident", [P, P])
        ones = sb("ones", [P, P])
        headsel = sb("headsel", [P, 2])
        before = sb("before", [P, P], F16)
        ones16 = sb("ones16", [P, P], F16)
        iota = sb("iota", [P, P])
        token_id = sb("token_id", [P, NT])
        thresholds = sb("thresholds", [P, E])
        zero16 = sb("zero16", [P, E])
        cols = sb("cols", [P, len(COLS)])
        rows = sb("rows", [P, NROW])
        mv = sb("mv", [P, 4, TB, 2])
        st = sb("st", [P, TB, 6])
        rstd = sb("rstd", [P, 4, TB])
        nwt = sb("nwt", [P, 2, 3, 48])
        lnt = sb("lnt", [P, 2, TB])
        hid_rstd = sb("hid_rstd", [P, TB])
        kss = sb("kss", [P, TB * H0])
        weight2 = sb("weight2", [P, NT, 2])
        keep = sb("keep", [P, NT, 2])
        mask8 = sb("mask8", [P, B * CTB // 4], U32)
        pick = sb("pick", [P, 2, NT, E])
        weight = sb("weight", [P, NT, 2])
        chosen = sb("chosen", [P, NT, E], F16)
        earlier = sb("earlier", [P, NT + 1, E], F16)
        top8 = sb("top8", [P, TB, 8])
        idx8 = sb("idx8", [P, TB, 8], U32)
        idxf = sb("idxf", [P, TB, 2])
        score = sb("score", [P, TB, E])
        wtmp = sb("wtmp", [P, TB, 2])
        ptmp = sb("ptmp", [P, NT, E])
        rank = sb("rank", [P, NT, 2])
        rank_i = sb("rank_i", [P, NT, 2], I32)
        part_i = sb("part_i", [P, NT, 2], I32)
        rrow = sb("rrow", [P, NT, 2])
        rtile = sb("rtile", [P, NT, 2])
        rowhot = sb("rowhot", [P, NT, 2, P], F16)
        tilehot = sb("tilehot", [P, NT, 2, 48], F16)
        etiles = sb("etiles", [P, 3, E])
        ecmp = sb("ecmp", [P, 48, E])
        eslot = sb("eslot", [P, 48])
        eslot_i = sb("eslot_i", [P, 48], I32)
        slot_u = sb("slot_u", [P, NT, 2], U32)
        source = sb("source", [P, 48], U32)
        dest_f = sb("dest_f", [P, NT, 2])

        base = int(nc.sbuf_base) + 64
        arena = nc.sbuf_usable_end

        def place(at, name, shape, dt=F32):
            size = int(np.prod(shape[1:])) * {F16: 2, U8: 1}.get(dt, 4)
            t = nc.alloc_sbuf_tensor_at(name, shape, dt, offset=at[0])
            at[0] += -(-size // 32) * 32
            assert at[0] <= arena, (name, at[0], arena)
            return t

        at = [-(-base // 64) * 64]
        hT_at = at[0]
        hT = place(at, "hT", [P, KC, NT * P])
        gate_w = place(at, "gate_w", [P, KC, E])
        sh_gu = place(at, "sh_gu", [P, KC, 2 * M0])
        sh_dn = place(at, "sh_dn", [P, D])
        qkv_w = place(at, "qkv_w", [P, KC, QKV])
        proj_w = place(at, "proj_w", [P, KC, D])
        router_w = place(at, "router_w", [P, KC, E])
        hn = place(at, "hn", [P, 1, TB, D])
        rexp = place(at, "rexp", [P, TB * E])
        phase_at = at[0]
        wq = place(at, "wq", [P, KC, D])
        wkv = place(at, "wkv", [P, KC, 2 * D])
        wout = place(at, "wout", [P, KC, D])
        ctx_in = place(at, "ctx_in", [P, 2, TB, D])
        xn = place(at, "xn", [P, 2, TB, D])
        xnT = place(at, "xnT", [P, 2, KC, S])
        kstack = place(at, "kstack", [P, H0, KT0 * P], F32R)
        vals = place(at, "vals", [P, KT0, D])
        ksq = place(at, "ksq", [P, NPAIR, S])
        rkey = place(at, "rkey", [P, 2, KT0, H0])
        qn = place(at, "qn", [P, TB, D])
        qsq = place(at, "qsq", [P, TB, D])
        ssq = place(at, "ssq", [P, TB * H0])
        rq = place(at, "rq", [P, TB * H0])
        qdup = place(at, "qdup", [P, TB * H0, 2, DH0])
        qhi = place(at, "qhi", [P, H0, S], F32R)
        qlo = place(at, "qlo", [P, H0, S], F32R)
        gqk = place(at, "gqk", [P, 1])
        gbound = place(at, "gbound", [P, DH0 + 2])
        mbias = place(at, "mbias", [P, B, CTB])
        lbias = place(at, "lbias", [P, 1])
        probs = place(at, "probs", [P, 3, 2, S])
        psums = place(at, "psums", [P, 2, 2 * S])
        rden = place(at, "rden", [P, S])
        attnT = place(at, "attnT", [P, NPAIR, S])
        at = [phase_at]
        yg = place(at, "yg", [P, NYG, 2, D])
        ctx_at = at[0]
        ctx_n = place(at, "ctx_n", [P, B, CTB, D])
        ctx_t = place(at, "ctx_t", [P, KC, B, SC])
        work_at = at[0]
        at = [ctx_at]
        w1 = place(at, "w1", [P, NW, KC, F1])
        w2 = place(at, "w2", [P, NW, FC1, D])
        eT = place(at, "eT", [P, 2, KC, CAP1])
        h1 = place(at, "h1", [P, 2, FC1, CAP1])
        y2 = place(at, "y2", [P, 3, D])
        xg2 = place(at, "xg2", [P, NXG, D])
        assert at[0] <= work_at
        at = [work_at]
        un = place(at, "un", [P, B, D])
        uT = place(at, "uT", [P, KC, B * P])
        cprob = place(at, "cprob", [P, 2, SC])
        cprobT = place(at, "cprobT", [P, 2, SC])
        csum = place(at, "csum", [P, 3, 4])
        cmax = place(at, "cmax", [P, 2, 4])
        dn = place(at, "dn", [P, B, D])
        dT = place(at, "dT", [P, KC, B * P])
        hid = place(at, "hid", [P, 2, B, D])
        l_n = place(at, "l_n", [P, B, D])
        lT = place(at, "lT", [P, KC, B * P])
        qkv = place(at, "qkv", [P, B, QKV])
        prod = place(at, "prod", [P, B, D])
        at = [hT_at]
        att_s = place(at, "att_s", [P, B, H1, B])
        att_d = place(at, "att_d", [P, B, H1, B])
        att_e = place(at, "att_e", [P, B, H1, B])
        att_m = place(at, "att_m", [P, 2, B, H1])
        att_o = place(at, "att_o", [P, B, D])
        rl = place(at, "rl", [P, 2, B, E])
        rm = place(at, "rm", [P, 2, B])
        at = [work_at]
        e_gu = place(at, "e_gu", [P, KC, E, 2 * M0])
        e_dn = place(at, "e_dn", [P, E, D])
        xg = place(at, "xg", [P, NXG, D])
        xgT = place(at, "xgT", [P, 3, D])
        silu = place(at, "silu", [P, 2, M0])
        up = place(at, "up", [P, 2, M0])
        mid = place(at, "mid", [P, 2, M0])
        midT = place(at, "midT", [P, 2, P])
        ysb = place(at, "ysb", [P, 3, D])

        ring_psum = ctx.enter_context(nc.psum_tensor("ring_psum", [P, NRING, 512], F32))
        acc_psum = ctx.enter_context(nc.psum_tensor("acc_psum", [P, 2, 512], F32))

        h_rows = nc.dram_tensor("h_rows", (NT * P, D), F32).ap()
        l_rows = nc.dram_tensor("l_rows", (NT * P, D), F32).ap()
        y2_rows = nc.dram_tensor("y2_rows", (E * CAP1, D), F32).ap()
        y_rows = nc.dram_tensor("y_rows", (NSLOT0 * P, D), F32).ap()

        x_loaded = [sem(f"x_loaded{b}") for b in range(B)]
        ctx_loaded = [sem(f"ctx_loaded{i}") for i in range(2)]
        small_loaded = sem("small_loaded")
        wa_loaded = sem("wa_loaded")
        wb_loaded = sem("wb_loaded")
        consts_made = sem("consts_made")
        dve_step = sem("dve_step")
        pool_step = sem("pool_step")
        unit_done = sem("unit_done")
        evacuated = [sem(f"evacuated{i}") for i in range(NRING)]
        stats_ready = sem("stats_ready")
        ln_applied = sem("ln_applied")
        bias_added = sem("bias_added")
        khi_ready = sem("khi_ready")
        rkey_ready = sem("rkey_ready")
        rq_ready = sem("rq_ready")
        qdup_ready = sem("qdup_ready")
        qhi_ready = sem("qhi_ready")
        exp_consts_ready = sem("exp_consts_ready")
        pv_done = sem("pv_done")
        psums_added = sem("psums_added")
        attn_evacuated = sem("attn_evacuated")
        x_updated = sem("x_updated")
        hn_stored = sem("hn_stored")
        picks_ready = sem("picks_ready")
        rrow_ready = sem("rrow_ready")
        rowhot_ready = sem("rowhot_ready")
        out_stored = sem("out_stored")
        e_loaded = sem("e_loaded")
        shared_mid = sem("shared_mid")
        shared_added = sem("shared_added")
        tiles_placed = sem("tiles_placed")
        tilehot_ready = sem("tilehot_ready")
        eslot_ready = sem("eslot_ready")
        slots_ready = sem("slots_ready")
        gathered = [sem(f"gathered{i}") for i in range(NXG)]
        silu_ready = sem("silu_ready")
        y_stored = [sem(f"y_stored{i}") for i in range(3)]
        y_gathered = [sem(f"y_gathered{i}") for i in range(NYG)]
        combined = sem("combined")
        ctx_n_loaded = sem("ctx_n_loaded")
        ctx_t_loaded = sem("ctx_t_loaded")
        wd_loaded = sem("wd_loaded")
        cmax_ready = sem("cmax_ready")
        x2_done = sem("x2_done")
        att_diff = sem("att_diff")
        att_exp = sem("att_exp")
        att_done = sem("att_done")
        x3_done = sem("x3_done")
        l_stored = sem("l_stored")
        rl_diff = sem("rl_diff")
        rl_exp = sem("rl_exp")
        picks2_ready = sem("picks2_ready")
        places2_ready = sem("places2_ready")
        hots2_ready = sem("hots2_ready")
        slots2_ready = sem("slots2_ready")
        gathered2 = [sem(f"gathered2_{i}") for i in range(NXG)]
        w_loaded = [sem(f"w_loaded{i}") for i in range(NW)]
        y2_stored = [sem(f"y2_stored{i}") for i in range(3)]
        y2_gathered = [sem(f"y2_gathered{i}") for i in range(NYG)]
        finished = sem("finished")

        ring = BankRing(ring_psum, NRING, unit_done, evacuated)

        def col(name):
            i = COLS.index(name)
            return cols[:, i:i + 1]

        def row(name):
            o, n = ROWS[name]
            return rows[:, o:o + n]

        ln_order = [0, 1]
        for b in range(B):
            ln_order.append(3 * b + 2)
            if b + 1 < B:
                ln_order += [3 * b + 3, 3 * b + 4]
            ln_order.append(("h", b))
        ln_order.append(("c", 0))
        for i in range(NSTEP):
            if i % B == 2 and i // B + 1 < TB:
                ln_order.append(("c", i // B + 1))
            if i % B == 1 and 5 <= i < 5 + NT:
                ln_order.append(("d", (i - 5) // B))
            if i % B == 2 and 10 <= i:
                ln_order.append(("l", (i - 10) // B))
        ln_at = {k: i for i, k in enumerate(ln_order)}

        def step(b, p, j):
            return (b * NPAIR + p) * KT0 + j

        def tile_of(n):
            return n % B * TB + n // B

        def add_shared(pool, t):
            ring.wait_evacuated(pool, ("sy", t))
            pool.tensor_tensor(x[:, t, :], x[:, t, :], ysb[:, t % 2, :], ALU.add).then_inc(shared_added, 1)

        block = ctx.enter_context(nc.Block())

        @block.tensor
        def _(pe):
            def transposes(g):
                pe.wait_ge(ln_applied, ln_at[g] + 1)
                for k in range(KC):
                    bank = ring.take(pe, ("xT", g, k))
                    for t in range(TB):
                        last = pe.transpose(bank[:, t * P:(t + 1) * P], xn[:, g % 2, t, k * P:(k + 1) * P], ident[:, :])
                    last.then_inc(unit_done, 1)

            def projections(g):
                for k in range(KC):
                    ring.wait_evacuated(pe, ("xT", g, k))
                for p in range(NPAIR):
                    bank = ring.take(pe, ("kT", g, p))
                    for k in range(KC):
                        last = pe.matmul(bank, wkv[:, k, p * P:(p + 1) * P], xnT[:, g % 2, k, :],
                                         start=(k == 0), stop=(k == KC - 1))
                    last.then_inc(unit_done, 1)
                if g % 3 == 0:
                    for i in range(2):
                        token_major(("q", g, i), g, i, wq[:, :, :])
                for i in range(2):
                    token_major(("v", g, i), g, i, wkv[:, :, D:2 * D])

            def token_major(key, g, i, w):
                bank = ring.take(pe, key)
                for t in range(2):
                    for k in range(KC):
                        last = pe.matmul(bank[:, t * D:(t + 1) * D],
                                         xnT[:, g % 2, k, (2 * i + t) * P:(2 * i + t + 1) * P], w[:, k, :],
                                         start=(k == 0), stop=(k == KC - 1))
                last.then_inc(unit_done, 1)

            def key_squares(g):
                bank = ring.take(pe, ("ss", g))
                for p in range(NPAIR):
                    pe.wait_ge(khi_ready, g * NPAIR + p + 1)
                    for t in range(TB):
                        c = (t * NPAIR + p) * 2
                        last = pe.matmul(bank[:, c:c + 2], ksq[:, p, t * P:(t + 1) * P], headsel[:, :],
                                         start=True, stop=True)
                last.then_inc(unit_done, 1)

            def query_transposes(b):
                pe.wait_ge(qdup_ready, b + 1)
                for h in range(H0):
                    bank = ring.take(pe, ("qT", b, h))
                    for t in range(TB):
                        last = pe.transpose(bank[:, t * P:(t + 1) * P],
                                            qdup[:, t * H0 + h, :, :].rearrange("p a d -> p (a d)"), ident[:, :])
                    last.then_inc(unit_done, 1)

            def scores(b, p, j):
                for h in range(2):
                    hh = 2 * p + h
                    bank = ring.take(pe, ("s", b, p, j, h))
                    pe.matmul(bank, kstack[:, hh, j * P:(j + 1) * P], qhi[:, hh, :], start=True, stop=False)
                    pe.matmul(bank, kstack[:, hh, j * P:(j + 1) * P], qlo[:, hh, :],
                              start=False, stop=True).then_inc(unit_done, 1)

            def weigh(b, p, j):
                n, m = step(b, p, j), b * NPAIR + p
                if j == 0 and m >= 2:
                    pe.wait_ge(attn_evacuated, m - 1)
                for h in range(2):
                    ring.wait_evacuated(pe, ("s", b, p, j, h))
                    last = pe.matmul(acc_psum[h * DH0:(h + 1) * DH0, m % 2, :],
                                     vals[:, j, (2 * p + h) * DH0:(2 * p + h + 1) * DH0], probs[:, n % 3, h, :],
                                     start=(j == 0), stop=(j == KT0 - 1), skip_group_check=True)
                last.then_inc(pv_done, 1)

            def denominators(b, p):
                m = b * NPAIR + p
                pe.wait_ge(psums_added, KT0 * (m + 1))
                bank = ring.take(pe, ("den", b, p))
                for h in range(2):
                    last = pe.matmul(bank[h * DH0:(h + 1) * DH0, :], ones[:, 0:DH0], psums[:, m % 2, h * S:(h + 1) * S],
                                     start=True, stop=True, skip_group_check=True)
                last.then_inc(unit_done, 1)

            def out_projection(b):
                for i in range(2):
                    bank = ring.take(pe, ("wo", b, i))
                    pe.wait_ge(attn_evacuated, NPAIR * (b + 1))
                    for t in range(2):
                        for p in range(NPAIR):
                            last = pe.matmul(bank[:, t * D:(t + 1) * D], attnT[:, p, (2 * i + t) * P:(2 * i + t + 1) * P],
                                             wout[:, p, :], start=(p == 0), stop=(p == NPAIR - 1))
                    last.then_inc(unit_done, 1)

            def expert_norm_transposes(b):
                pe.wait_ge(ln_applied, ln_at["h", b] + 1)
                for k in range(KC):
                    bank = ring.take(pe, ("hT", b, k))
                    for t in range(TB):
                        last = pe.transpose(bank[:, t * P:(t + 1) * P], hn[:, 0, t, k * P:(k + 1) * P], ident[:, :])
                    last.then_inc(unit_done, 1)

            def router(b):
                for k in range(KC):
                    ring.wait_evacuated(pe, ("hT", b, k))
                bank = ring.take(pe, ("gate", b))
                for t in range(TB):
                    for k in range(KC):
                        last = pe.matmul(bank[:, t * E:(t + 1) * E], hT[:, k, (TB * b + t) * P:(TB * b + t + 1) * P],
                                         gate_w[:, k, :], start=(k == 0), stop=(k == KC - 1))
                last.then_inc(unit_done, 1)

            def ranks(b):
                pe.wait_ge(picks_ready, b + 1)
                bank = ring.take(pe, ("rank", b))
                n = TB * E
                pe.matmul(bank[:, 0:n], before[:, :], chosen[:, TB * b:TB * b + TB, :].rearrange("p t e -> p (t e)"),
                          start=True, stop=False)
                last = pe.matmul(bank[:, 0:n], ones16[:, :],
                                 earlier[:, TB * b:TB * b + TB, :].rearrange("p t e -> p (t e)"), start=False, stop=True)
                if b == B - 1:
                    last = pe.matmul(bank[:, n:n + E], ones16[:, :], earlier[:, NT, :], start=True, stop=True)
                last.then_inc(unit_done, 1)

            pe.wait_ge(consts_made, 1)
            transposes(0)
            pe.wait_ge(wa_loaded, 48)
            for b in range(B):
                g = 3 * b
                transposes(g + 1)
                projections(g)
                transposes(g + 2)
                key_squares(g)
                projections(g + 1)
                query_transposes(b)
                key_squares(g + 1)
                projections(g + 2)
                if b:
                    if b == 1:
                        pe.wait_ge(wb_loaded, 48)
                    expert_norm_transposes(b - 1)
                if b + 1 < B:
                    transposes(g + 3)
                key_squares(g + 2)
                if b:
                    router(b - 1)
                for p in range(NPAIR):
                    for j in range(KT0):
                        scores(b, p, j)
                        if j >= 2:
                            weigh(b, p, j - 2)
                        if j == 3 and p == 1:
                            denominators(b, 0)
                        if j == 6 and p == 1 and b:
                            ranks(b - 1)
                    weigh(b, p, KT0 - 2)
                    weigh(b, p, KT0 - 1)
                denominators(b, 1)
                out_projection(b)
            expert_norm_transposes(B - 1)
            router(B - 1)

            def shared_up(t):
                bank = ring.take(pe, ("sgu", t))
                for k in range(KC):
                    last = pe.matmul(bank[:, 0:2 * M0], hT[:, k, t * P:(t + 1) * P], sh_gu[:, k, :],
                                     start=(k == 0), stop=(k == KC - 1))
                last.then_inc(unit_done, 1)

            def shared_turn(t):
                pe.wait_ge(shared_mid, t + 1)
                bank = ring.take(pe, ("smT", t))
                pe.transpose(bank[:, 0:P], mid[:, t % 2, :], ident[:, :]).then_inc(unit_done, 1)

            def shared_down(t):
                ring.wait_evacuated(pe, ("smT", t))
                bank = ring.take(pe, ("sy", t))
                pe.matmul(bank[:, 0:D], midT[:, t % 2, :], sh_dn[:, :], start=True, stop=True).then_inc(unit_done, 1)

            for i in range(NT + 2):
                if i < NT:
                    shared_up(i)
                if i == 5:
                    ranks(B - 1)
                if 1 <= i <= NT:
                    shared_turn(i - 1)
                if i >= 2:
                    shared_down(i - 2)

            def slot_sources(key, n):
                bank = ring.take(pe, key)
                for t in range(NT):
                    for k in range(2):
                        last = pe.matmul(bank[:, 0:n], rowhot[:, t, k, :], tilehot[:, t, k, 0:n],
                                         start=(t == 0 and k == 0), stop=(t == NT - 1 and k == 1))
                last.then_inc(unit_done, 1)

            pe.wait_ge(rowhot_ready, B)
            pe.wait_ge(tilehot_ready, 2)
            slot_sources(("source", 0), NSLOT0)

            expert = {}

            def slot_turn(s):
                pe.wait_ge(gathered[s % NXG], 16 * (s // NXG + 1))
                bank = ring.take(pe, ("xgT", s))
                for k in range(KC):
                    last = pe.transpose(bank[:, k * P:(k + 1) * P], xg[:, s % NXG, k * P:(k + 1) * P], ident[:, :])
                last.then_inc(unit_done, 1)
                expert[s] = pe.value_load(eslot_i[0:1, s:s + 1], min_val=0, max_val=E - 1)

            def slot_up(s):
                ring.wait_evacuated(pe, ("xgT", s))
                bank = ring.take(pe, ("gu", s))
                for k in range(KC):
                    last = pe.matmul(bank[:, 0:2 * M0], xgT[:, s % 3, k * P:(k + 1) * P],
                                     e_gu[:, k, bass.ds(expert[s], 1), :], start=(k == 0), stop=(k == KC - 1))
                last.then_inc(unit_done, 1)

            def slot_mid_turn(s):
                ring.wait_evacuated(pe, ("gu", s))
                bank = ring.take(pe, ("mT", s))
                pe.transpose(bank[:, 0:P], mid[:, s % 2, :], ident[:, :]).then_inc(unit_done, 1)

            def slot_down(s):
                ring.wait_evacuated(pe, ("mT", s))
                bank = ring.take(pe, ("y", s))
                pe.matmul(bank[:, 0:D], midT[:, s % 2, :], e_dn[:, bass.ds(expert[s], 1), :],
                          start=True, stop=True).then_inc(unit_done, 1)

            pe.wait_ge(eslot_ready, 1)
            pe.wait_ge(e_loaded, 32)
            for i in range(NSLOT0 + 3):
                if i < NSLOT0:
                    slot_turn(i)
                if 1 <= i <= NSLOT0:
                    slot_up(i - 1)
                if 2 <= i <= NSLOT0 + 1:
                    slot_mid_turn(i - 2)
                if i >= 3:
                    slot_down(i - 3)

            def turn_tokens(key, ln_key, src):
                pe.wait_ge(ln_applied, ln_at[ln_key] + 1)
                for k in range(KC):
                    bank = ring.take(pe, key + (k,))
                    for s in range(B):
                        last = pe.transpose(bank[:, s * P:(s + 1) * P], src[:, s, k * P:(k + 1) * P], ident[:, :])
                    last.then_inc(unit_done, 1)

            def context_scores(n):
                c, s = divmod(n, B)
                if s == 0:
                    for k in range(KC):
                        ring.wait_evacuated(pe, ("uT", c, k))
                for half in range(2):
                    bank = ring.take(pe, ("cs", n, half))
                    for k in range(KC):
                        last = pe.matmul(bank, uT[:, k, s * P:(s + 1) * P], ctx_t[:, k, s, half * 512:(half + 1) * 512],
                                         start=(k == 0), stop=(k == KC - 1))
                    last.then_inc(unit_done, 1)

            def context_turn(n):
                for half in range(2):
                    ring.wait_evacuated(pe, ("cs", n, half))
                for half in range(2):
                    bank = ring.take(pe, ("cp", n, half))
                    for t in range(4):
                        o = half * 512 + t * P
                        last = pe.transpose(bank[:, t * P:(t + 1) * P], cprob[:, n % 2, o:o + P], ident[:, :])
                    last.then_inc(unit_done, 1)

            def context_values(n):
                for half in range(2):
                    ring.wait_evacuated(pe, ("cp", n, half))
                bank = ring.take(pe, ("co", n))
                for t in range(CTB):
                    last = pe.matmul(bank[:, 0:D], cprobT[:, n % 2, t * P:(t + 1) * P], ctx_n[:, n % B, t, :],
                                     start=(t == 0), stop=(t == CTB - 1))
                last.then_inc(unit_done, 1)

            def project_qkv(c):
                for k in range(KC):
                    ring.wait_evacuated(pe, ("dT", c, k))
                for s in range(B):
                    bank = ring.take(pe, ("qkv", c, s))
                    for k in range(KC):
                        last = pe.matmul(bank[:, 0:QKV], dT[:, k, s * P:(s + 1) * P], qkv_w[:, k, :],
                                         start=(k == 0), stop=(k == KC - 1))
                    last.then_inc(unit_done, 1)

            def turn_attention(c):
                pe.wait_ge(att_done, c + 1)
                for k in range(KC):
                    bank = ring.take(pe, ("oT", c, k))
                    for s in range(B):
                        last = pe.transpose(bank[:, s * P:(s + 1) * P], att_o[:, s, k * P:(k + 1) * P], ident[:, :])
                    last.then_inc(unit_done, 1)

            def project_out(c):
                for k in range(KC):
                    ring.wait_evacuated(pe, ("oT", c, k))
                for i in range(2):
                    bank = ring.take(pe, ("po", c, i))
                    for t in range(2):
                        for k in range(KC):
                            last = pe.matmul(bank[:, t * D:(t + 1) * D], dT[:, k, (2 * i + t) * P:(2 * i + t + 1) * P],
                                             proj_w[:, k, :], start=(k == 0), stop=(k == KC - 1))
                    last.then_inc(unit_done, 1)

            def router2(c):
                for k in range(KC):
                    ring.wait_evacuated(pe, ("lT", c, k))
                bank = ring.take(pe, ("rt", c))
                for s in range(B):
                    for k in range(KC):
                        last = pe.matmul(bank[:, s * E:(s + 1) * E], lT[:, k, s * P:(s + 1) * P], router_w[:, k, :],
                                         start=(k == 0), stop=(k == KC - 1))
                last.then_inc(unit_done, 1)

            turn_tokens(("uT", 0), ("c", 0), un)
            pe.wait_ge(ctx_t_loaded, 16)
            pe.wait_ge(ctx_n_loaded, 16)
            pe.wait_ge(wd_loaded, 48)
            for i in range(NSTEP):
                if i < NT:
                    context_scores(i)
                if 1 <= i <= NT:
                    context_turn(i - 1)
                if 2 <= i <= NT + 1:
                    context_values(i - 2)
                if i % B == 3 and i // B + 1 < TB:
                    turn_tokens(("uT", i // B + 1), ("c", i // B + 1), un)
                if i % B == 2 and 6 <= i < 6 + NT:
                    turn_tokens(("dT", (i - 6) // B), ("d", (i - 6) // B), dn)
                if i % B == 3 and 7 <= i < 7 + NT:
                    project_qkv((i - 7) // B)
                if i % B == 1 and 9 <= i < 9 + NT:
                    turn_attention((i - 9) // B)
                if i % B == 1 and 9 <= i < 9 + NT:
                    project_out((i - 9) // B)
                if i % B == 3 and 11 <= i < 11 + NT:
                    turn_tokens(("lT", (i - 11) // B), ("l", (i - 11) // B), l_n)
                if i % B == 3 and 11 <= i < 11 + NT:
                    router2((i - 11) // B)

            pe.wait_ge(picks2_ready, 1)
            bank = ring.take(pe, ("rank2", 0))
            pe.matmul(bank[:, 0:NT * E], before[:, :], chosen[:, :, :].rearrange("p t e -> p (t e)"), start=True, stop=False)
            pe.matmul(bank[:, 0:NT * E], ones16[:, :], earlier[:, 0:NT, :].rearrange("p t e -> p (t e)"),
                      start=False, stop=True).then_inc(unit_done, 1)
            pe.wait_ge(hots2_ready, 2)
            slot_sources(("source", 1), NSLOT1)

            def expert_turn(e):
                for k in range(KC):
                    bank = ring.take(pe, ("eT", e, k))
                    for r in range(RT1):
                        s, n = e * RT1 + r, min(P, CAP1 - r * P)
                        if k == 0:
                            pe.wait_ge(gathered2[s % NXG], 16 * (s // NXG + 1))
                        last = pe.transpose(bank[:, r * P:r * P + n], xg2[0:n, s % NXG, k * P:(k + 1) * P], ident[0:n, 0:n])
                    last.then_inc(unit_done, 1)

            def expert_up(e):
                for k in range(KC):
                    ring.wait_evacuated(pe, ("eT", e, k))
                pe.wait_ge(w_loaded[e % NW], 32 * (e // NW + 1))
                for f in range(FC1):
                    bank = ring.take(pe, ("h1", e, f))
                    for k in range(KC):
                        last = pe.matmul(bank[:, 0:CAP1], w1[:, e % NW, k, f * P:(f + 1) * P], eT[:, e % 2, k, :],
                                         start=(k == 0), stop=(k == KC - 1))
                    last.then_inc(unit_done, 1)

            def expert_down(e):
                for f in range(FC1):
                    ring.wait_evacuated(pe, ("h1", e, f))
                for r in range(RT1):
                    n = min(P, CAP1 - r * P)
                    bank = ring.take(pe, ("h2", e, r))
                    for f in range(FC1):
                        last = pe.matmul(bank[0:n, 0:D], h1[:, e % 2, f, r * P:r * P + n], w2[:, e % NW, f, :],
                                         start=(f == 0), stop=(f == FC1 - 1))
                    last.then_inc(unit_done, 1)

            expert_turn(0)
            for e in range(E):
                expert_up(e)
                if e + 1 < E:
                    expert_turn(e + 1)
                expert_down(e)

        @block.sync
        def _(sp):
            for b in range(B):
                sp.dma_start(x[:, TB * b:TB * b + TB, :], a["x"][b].rearrange("(t p) d -> p t d", p=P)).then_inc(x_loaded[b], 16)
                if b == 0:
                    sp.dma_start(cols[:, :], a["cols"]).then_inc(small_loaded, 16)
                    sp.dma_start(rows[:, :], a["rows"]).then_inc(small_loaded, 16)
                    sp.dma_start(mask8[:, :], a["mask"]).then_inc(small_loaded, 16)

            def load_ctx(c):
                if c >= 2:
                    g = (c - 2) // 2 * 3 + (c - 2) % 2 + 1
                    sp.wait_ge(ln_applied, ln_at[g] + 1)
                sp.dma_start(ctx_in[:, c % 2, :, :],
                             a["ctx"][c // 2, (c % 2) * S:(c % 2 + 1) * S, :].rearrange("(t p) d -> p t d", p=P)).then_inc(ctx_loaded[c % 2], 16)

            load_ctx(0)
            load_ctx(1)
            sp.dma_start(gate_w[:, :, :], a["gate_w"]).then_inc(wb_loaded, 16)
            sp.dma_start(sh_gu[:, :, :], a["sh_gu"]).then_inc(wb_loaded, 16)
            sp.dma_start(sh_dn[:, :], a["sh_dn"]).then_inc(wb_loaded, 16)
            sp.dma_start(qkv_w[:, :, :], a["qkv_w"]).then_inc(wd_loaded, 16)
            sp.dma_start(proj_w[:, :, :], a["proj_w"]).then_inc(wd_loaded, 16)
            sp.dma_start(router_w[:, :, :], a["router_w"]).then_inc(wd_loaded, 16)
            for b in range(B):
                if b + 1 < B:
                    load_ctx(2 * b + 2)
                    load_ctx(2 * b + 3)
                sp.wait_ge(ln_applied, ln_at["h", b] + 1)
                sp.dma_start(h_rows[b * S:(b + 1) * S, :].rearrange("(t p) d -> p t d", p=P), hn[:, 0, :, :]).then_inc(hn_stored, 16)
                if b == B - 1:
                    ring.wait_done(sp, ("wo", B - 1, 1))
                    sp.dma_start(e_gu[:, :, :, :], a["e_gu"]).then_inc(e_loaded, 16)
                    sp.dma_start(e_dn[:, :, :], a["e_dn"]).then_inc(e_loaded, 16)
                    sp.dma_start(ctx_t[:, :, :, :], a["ctxT"]).then_inc(ctx_t_loaded, 16)
                    sp.dma_start(ctx_n[:, :, :, :].rearrange("p b t d -> p (b t) d"),
                                 a["ctx"].rearrange("b (t p) d -> p (b t) d", p=P)).then_inc(ctx_n_loaded, 16)
            for s in range(NSLOT0):
                ring.wait_evacuated(sp, ("y", s))
                sp.dma_start(y_rows[s * P:(s + 1) * P, :], ysb[:, s % 3, :]).then_inc(y_stored[s % 3], 16)

            def load_expert(e):
                if e == 0:
                    ring.wait_done(sp, ("co", NT - 1))
                if e >= NW:
                    ring.wait_done(sp, ("h2", e - NW, RT1 - 1))
                sp.dma_start(w1[:, e % NW, :, :], a["w1"][e]).then_inc(w_loaded[e % NW], 16)
                sp.dma_start(w2[:, e % NW, :, :], a["w2"][e]).then_inc(w_loaded[e % NW], 16)

            for c in range(TB):
                if c == TB - 1:
                    for e in range(NW):
                        load_expert(e)
                sp.wait_ge(ln_applied, ln_at["l", c] + 1)
                sp.dma_start(l_rows.rearrange("(s c p) d -> p s c d", s=B, c=TB)[:, :, c, :], l_n[:, :, :]).then_inc(l_stored, 16)
            for e in range(E):
                for r in range(RT1):
                    n, j = min(P, CAP1 - r * P), e * RT1 + r
                    ring.wait_evacuated(sp, ("h2", e, r))
                    sp.dma_start(y2_rows[e * CAP1 + r * P:e * CAP1 + r * P + n, :], y2[0:n, j % 3, :]).then_inc(y2_stored[j % 3], 16)
                if e + NW < E:
                    load_expert(e + NW)
            for t in range(NT):
                sp.wait_ge(finished, t + 1)
                sp.dma_start(out[t // TB, t % TB * P:(t % TB + 1) * P, :], x[:, t, :]).then_inc(out_stored, 16)
            sp.wait_ge(out_stored, 16 * NT)

        @block.gpsimd
        def _(pool):
            count = [0]

            def link(ins):
                count[0] += 1
                ins.then_inc(pool_step, 1)
                pool.wait_ge(pool_step, count[0])

            link(pool.memset(ident[:, :], 0.0))
            link(pool.affine_select(out=ident[:, :], in_=ident[:, :], compare_op=ALU.not_equal, fill=1.0, base=0,
                                    pattern=[[-1, P]], channel_multiplier=1))
            pool.memset(ones[:, :], 1.0)
            pool.memset(ones16[:, :], 1.0)
            pool.memset(zero16[:, :], 0.0)
            pool.memset(earlier[:, 0, :], 0.0)
            link(pool.memset(headsel[:, :], 1.0))
            link(pool.affine_select(out=headsel[:, 0:1], in_=headsel[:, 0:1], compare_op=ALU.is_gt, fill=0.0, base=DH0,
                                    pattern=[[0, 1]], channel_multiplier=-1))
            link(pool.affine_select(out=headsel[:, 1:2], in_=headsel[:, 1:2], compare_op=ALU.is_ge, fill=0.0, base=-DH0,
                                    pattern=[[0, 1]], channel_multiplier=1))
            link(pool.affine_select(out=before[:, :], in_=ones16[:, :], compare_op=ALU.is_gt, fill=0.0, base=0,
                                    pattern=[[1, P]], channel_multiplier=-1))
            pool.iota(iota[:, :], pattern=[[1, P]], base=0, channel_multiplier=0, allow_small_or_imprecise_dtypes=True)
            pool.iota(token_id[:, :], pattern=[[P, NT]], base=0, channel_multiplier=1, allow_small_or_imprecise_dtypes=True)
            pool.iota(thresholds[:, :], pattern=[[P, E]], base=0, channel_multiplier=0, allow_small_or_imprecise_dtypes=True).then_inc(consts_made, 1)

            def apply_norm(key):
                i = ln_at[key]
                pool.wait_ge(stats_ready, i + 1)
                if isinstance(key, tuple) and key[0] != "h":
                    kind, c = key
                    src = hid[:, c % 2, :, :] if kind == "l" else x[:, c:NT:TB, :]
                    dst = {"c": un, "d": dn, "l": l_n}[kind]
                    if key == ("c", 0):
                        ring.wait_done(pool, ("y", NSLOT0 - 1))
                    if c:
                        ring.wait_done(pool, ({"c": "uT", "d": "dT", "l": "lT"}[kind], c - 1, KC - 1))
                        if kind == "l":
                            pool.wait_ge(l_stored, 16 * c)
                elif isinstance(key, tuple):
                    b = key[1]
                    src, dst = x[:, TB * b:TB * b + TB, :], hn[:, 0, :, :]
                    if b >= 1:
                        pool.wait_ge(hn_stored, 16 * b)
                        ring.wait_done(pool, ("hT", b - 1, 1))
                else:
                    g = key
                    if g >= 2:
                        ring.wait_done(pool, ("xT", g - 2, 1))
                    dst = xn[:, g % 2, :, :]
                    src = x[:, TB * (g // 3):TB * (g // 3) + TB, :] if g % 3 == 0 else ctx_in[:, (g % 3 - 1), :, :]
                for t in range(TB):
                    last = pool.tensor_scalar(dst[:, t, :], src[:, t, :], mv[:, i % 4, t, 0:1], rstd[:, i % 4, t:t + 1],
                                              ALU.subtract, ALU.mult)
                if isinstance(key, tuple) and key[0] == "l":
                    link(last)
                    link(pool.tensor_tensor(dst[:, :, :], dst[:, :, :], bc(row("ln2_w"), 1, B), ALU.mult))
                    last = pool.tensor_tensor(dst[:, :, :], dst[:, :, :], bc(row("ln2_b"), 1, B), ALU.add)
                last.then_inc(ln_applied, 1)
                if not isinstance(key, tuple) and key % 3 == 0:
                    b = key // 3
                    pool.wait_ge(ln_applied, i + 1)
                    pool.wait_ge(small_loaded, 48)
                    xs = x[:, TB * b:TB * b + TB, :]
                    pool.tensor_tensor(xs, xs, bc(row("b_out"), 1, TB), ALU.add).then_inc(bias_added, 1)

            def queries_twice(b):
                pool.wait_ge(rq_ready, b + 1)
                if b:
                    ring.wait_done(pool, ("qT", b - 1, H0 - 1))
                for d in range(2):
                    last = pool.tensor_tensor(qdup[:, :, d, :], qn[:, :, :].rearrange("p t (h e) -> p (t h) e", h=H0),
                                              bc(rq[:, :], 2, DH0), ALU.mult)
                last.then_inc(qdup_ready, 1)

            def row_onehots(b):
                pool.wait_ge(rrow_ready, b + 1)
                for t in range(TB * b, TB * b + TB):
                    for k in range(2):
                        last = pool.tensor_scalar(rowhot[:, t, k, :], iota[:, :], rrow[:, t, k:k + 1], None, ALU.is_equal)
                last.then_inc(rowhot_ready, 1)

            apply_norm(0)
            apply_norm(1)
            for b in range(B):
                queries_twice(b)
                apply_norm(3 * b + 2)
                if b + 1 < B:
                    apply_norm(3 * b + 3)
                    apply_norm(3 * b + 4)
                if b:
                    row_onehots(b - 1)
                apply_norm(("h", b))
            for t in range(NT):
                if t == 10:
                    row_onehots(B - 1)
                ring.wait_evacuated(pool, ("sgu", t))
                if t == 0:
                    ring.wait_done(pool, ("wo", B - 1, 1))
                if t >= 2:
                    ring.wait_done(pool, ("smT", t - 2))
                pool.tensor_tensor(mid[:, t % 2, :], silu[:, t % 2, :], up[:, t % 2, :], ALU.mult).then_inc(shared_mid, 1)
                if t >= 2:
                    add_shared(pool, t - 2)
            for t in (NT - 2, NT - 1):
                add_shared(pool, t)
            pool.wait_ge(tiles_placed, 1)
            for t in range(NT):
                last = pool.tensor_scalar(tilehot[:, t, 1, 0:NSLOT0], iota[:, 0:NSLOT0], rtile[:, t, 1:2], token_id[:, t:t + 1],
                                          ALU.is_equal, ALU.mult)
            last.then_inc(tilehot_ready, 1)

            pool.wait_ge(slots_ready, 1)
            pool.wait_ge(hn_stored, 16 * B)
            for s in range(NSLOT0):
                if s >= NXG:
                    ring.wait_done(pool, ("xgT", s - NXG))
                pool.indirect_dma_start(xg[:, s % NXG, :], None, h_rows,
                                        bass.IndirectOffsetOnAxis(ap=source[:, s:s + 1], axis=0)).then_inc(gathered[s % NXG], 16)
            for i in range(3):
                pool.wait_ge(y_stored[i], 16 * len(range(i, NSLOT0, 3)))

            def gather_results(n):
                if n >= NYG:
                    pool.wait_ge(combined, n - NYG + 1)
                for k in range(2):
                    pool.indirect_dma_start(yg[:, n % NYG, k, :], None, y_rows,
                                            bass.IndirectOffsetOnAxis(ap=slot_u[:, tile_of(n), k:k + 1], axis=0)).then_inc(y_gathered[n % NYG], 16)

            for n in range(B):
                gather_results(n)
            apply_norm(("c", 0))
            for i in range(NSTEP):
                if i % B == 1 and i // B + 1 < TB:
                    for n in range(B * (i // B + 1), B * (i // B + 2)):
                        gather_results(n)
                if i % B == 2 and i // B + 1 < TB:
                    apply_norm(("c", i // B + 1))
                if i % B == 1 and 5 <= i < 5 + NT:
                    apply_norm(("d", (i - 5) // B))
                if i % B == 2 and 10 <= i:
                    apply_norm(("l", (i - 10) // B))
            pool.wait_ge(places2_ready, 1)
            for t in range(DVE_HOTS, NT):
                for k in range(2):
                    pool.tensor_scalar(rowhot[:, t, k, :], iota[:, :], rrow[:, t, k:k + 1], None, ALU.is_equal)
                    last = pool.tensor_scalar(tilehot[:, t, k, :], iota[:, 0:NSLOT1], rtile[:, t, k:k + 1], token_id[:, t:t + 1],
                                              ALU.is_equal, ALU.mult)
            last.then_inc(hots2_ready, 1)
            pool.wait_ge(slots2_ready, 1)
            pool.wait_ge(l_stored, 16 * TB)
            for s in range(NSLOT1):
                if s >= NXG:
                    ring.wait_done(pool, ("eT", (s - NXG) // RT1, KC - 1))
                n = min(P, CAP1 - s % RT1 * P)
                pool.indirect_dma_start(xg2[0:n, s % NXG, :], None, l_rows,
                                        bass.IndirectOffsetOnAxis(ap=source[0:n, s:s + 1], axis=0)).then_inc(gathered2[s % NXG], 16)
            for i in range(3):
                pool.wait_ge(y2_stored[i], 16 * len(range(i, NSLOT1, 3)))
            for t in range(NT):
                if t >= NYG:
                    pool.wait_ge(finished, t - NYG + 1)
                else:
                    pool.wait_ge(combined, NT)
                for k in range(2):
                    pool.indirect_dma_start(yg[:, t % NYG, k, :], None, y2_rows,
                                            bass.IndirectOffsetOnAxis(ap=slot_u[:, t, k:k + 1], axis=0)).then_inc(y2_gathered[t % NYG], 16)

        @block.scalar
        def _(act):
            act.dma_start(wkv[:, :, :], a["wkv"]).then_inc(wa_loaded, 16)
            act.dma_start(wq[:, :, :], a["wq"]).then_inc(wa_loaded, 16)
            act.dma_start(wout[:, :, :], a["wout"]).then_inc(wa_loaded, 16)
            act.wait_ge(small_loaded, 48)
            act.wait_ge(exp_consts_ready, 1)

            def evac_turned(g):
                ring.wait_done(act, ("xT", g, 1))
                n = "ln_l" if g % 3 == 0 else "ln_x"
                if g >= 2:
                    ring.wait_done(act, ("v", g - 2, 1))
                act.activation(xnT[:, g % 2, 1, :], ring.bank(("xT", g, 1)), ACT.Identity, bias=col(n + "_b1"),
                               scale=col(n + "_g1")).then_inc(ring.evacuated(("xT", g, 1)), 1)

            def keys(g):
                b, gg = divmod(g, 3)
                for p in range(NPAIR):
                    bank = ring.bank(("kT", g, p))
                    ring.wait_done(act, ("kT", g, p))
                    if g:
                        ring.wait_done(act, ("ss", g - 1))
                    if gg == 0 and b:
                        ring.wait_done(act, ("s", b - 1, NPAIR - 1, KT0 - 1, 1))
                    act.activation(ksq[:, p, :], bank, ACT.Square)
                    span = slice(gg * S, (gg + 1) * S)
                    act.activation(kstack[0:DH0, 2 * p, span], bank[0:DH0, :], ACT.Copy)
                    act.activation(kstack[DH0:P, 2 * p + 1, span], bank[DH0:P, :], ACT.Copy).then_inc(khi_ready, 1)

            def copies(key, dst):
                ring.wait_done(act, key)
                act.activation(dst, ring.bank(key), ACT.Copy).then_inc(ring.evacuated(key), 1)

            def copies_part(key, dst, n):
                ring.wait_done(act, key)
                act.activation(dst, ring.bank(key)[:, 0:n], ACT.Copy).then_inc(ring.evacuated(key), 1)

            def values(g):
                b, gg = divmod(g, 3)
                if gg == 0 and b:
                    act.wait_ge(pv_done, step(b, 0, 0))
                for i in range(2):
                    copies(("v", g, i), vals[:, gg * TB + 2 * i:gg * TB + 2 * i + 2, :].rearrange("p t d -> p (t d)"))

            def queries(b):
                if b:
                    act.wait_ge(qdup_ready, b)
                for i in range(2):
                    copies(("q", 3 * b, i), qn[:, 2 * i:2 * i + 2, :].rearrange("p t d -> p (t d)"))

            def query_high(b):
                if b:
                    ring.wait_done(act, ("s", b - 1, NPAIR - 1, KT0 - 1, 1))
                for h in range(H0):
                    ring.wait_done(act, ("qT", b, h))
                    act.activation(qhi[:, h, :], ring.bank(("qT", b, h)), ACT.Copy, scale=gqk[:, :]).then_inc(qhi_ready, 1)

            def exps(b, p, j):
                n = step(b, p, j)
                if n >= 3:
                    act.wait_ge(pv_done, n - 2)
                    act.wait_ge(psums_added, n - 2)
                if p == 0 and j % TB == 0:
                    act.wait_ge(rkey_ready, 3 * b + j // TB + 1)
                for h in range(2):
                    key = ("s", b, p, j, h)
                    ring.wait_done(act, key)
                    act.activation(probs[:, n % 3, h, :], ring.bank(key), ACT.Exp,
                                   bias=lbias[:, :] if j < TB else mbias[:, b, j - TB:j - TB + 1],
                                   scale=rkey[:, b % 2, j, 2 * p + h:2 * p + h + 1]).then_inc(ring.evacuated(key), 1)

            def expert_norm_turned(b):
                for k in range(KC):
                    copies(("hT", b, k), hT[:, k, b * S:(b + 1) * S])

            def router_exp(b):
                key = ("gate", b)
                ring.wait_done(act, key)
                if b:
                    act.wait_ge(picks_ready, b)
                act.activation(rexp[:, :], ring.bank(key)[:, 0:TB * E], ACT.Exp, scale=-1.0).then_inc(ring.evacuated(key), 1)

            evac_turned(0)
            for b in range(B):
                g = 3 * b
                evac_turned(g + 1)
                keys(g)
                queries(b)
                values(g)
                evac_turned(g + 2)
                keys(g + 1)
                values(g + 1)
                query_high(b)
                keys(g + 2)
                values(g + 2)
                if b:
                    expert_norm_turned(b - 1)
                if b + 1 < B:
                    evac_turned(g + 3)
                if b:
                    router_exp(b - 1)
                for p in range(NPAIR):
                    for j in range(KT0):
                        exps(b, p, j)
            expert_norm_turned(B - 1)
            router_exp(B - 1)

            for i in range(NT + 2):
                if i < NT:
                    key = ("sgu", i)
                    ring.wait_done(act, key)
                    if i >= 2:
                        act.wait_ge(shared_mid, i - 1)
                    act.activation(up[:, i % 2, :], ring.bank(key)[:, M0:2 * M0], ACT.Copy)
                    act.activation(silu[:, i % 2, :], ring.bank(key)[:, 0:M0], ACT.Silu).then_inc(ring.evacuated(key), 1)
                if 1 <= i <= NT:
                    t = i - 1
                    if t >= 2:
                        ring.wait_done(act, ("sy", t - 2))
                    copies_part(("smT", t), midT[:, t % 2, :], P)
                if i >= 2:
                    t = i - 2
                    if t >= 2:
                        act.wait_ge(shared_added, t - 1)
                    copies_part(("sy", t), ysb[:, t % 2, :], D)
            for i in range(NSLOT0 + 3):
                if 1 <= i <= NSLOT0:
                    s = i - 1
                    key = ("gu", s)
                    ring.wait_done(act, key)
                    if s >= 2:
                        ring.wait_evacuated(act, ("gu", s - 2))
                    act.activation(silu[:, s % 2, :], ring.bank(key)[:, 0:M0], ACT.Silu).then_inc(silu_ready, 1)
                if i >= 3:
                    s = i - 3
                    if s >= 3:
                        act.wait_ge(y_stored[s % 3], 16 * (s // 3))
                    copies_part(("y", s), ysb[:, s % 3, :], D)

            for k in range(KC):
                copies(("uT", 0, k), uT[:, k, :])
            for i in range(NSTEP):
                if i < NT:
                    if i >= 2:
                        ring.wait_done(act, ("cp", i - 2, 1))
                        if i >= 3:
                            act.wait_ge(x2_done, i - 2)
                    act.wait_ge(cmax_ready, i + 1)
                    for half in range(2):
                        key = ("cs", i, half)
                        act.activation(cprob[:, i % 2, half * 512:(half + 1) * 512], ring.bank(key), ACT.Exp,
                                       bias=cmax[:, i % 2, 3:4], scale=CSCALE,
                                       accum_out=csum[:, i % 3, half:half + 1]).then_inc(ring.evacuated(key), 1)
                if 1 <= i <= NT:
                    if i >= 3:
                        ring.wait_done(act, ("co", i - 3))
                    copies(("cp", i - 1, 0), cprobT[:, (i - 1) % 2, 0:512])
                c, phase = divmod(i, B)
                if phase == 3 and c + 1 < TB:
                    for k in range(KC):
                        ring.wait_done(act, ("cs", i, 1))
                        copies(("uT", c + 1, k), uT[:, k, :])
                if phase == 2 and 0 <= c - 1 < TB:
                    for k in range(KC):
                        key = ("dT", c - 1, k)
                        if c >= 2:
                            ring.wait_done(act, ("po", c - 2, 1))
                        ring.wait_done(act, key)
                        act.activation(dT[:, k, :], ring.bank(key), ACT.Identity, bias=col(f"ln1_b{k}"),
                                       scale=col(f"ln1_w{k}")).then_inc(ring.evacuated(key), 1)
                if phase == 3 and 0 <= c - 1 < TB:
                    if c >= 2:
                        act.wait_ge(att_done, c - 1)
                    for s in range(B):
                        copies_part(("qkv", c - 1, s), qkv[:, s, :], QKV)
                if phase == 0 and 0 <= c - 2 < TB:
                    act.wait_ge(att_diff, c - 1)
                    act.activation(att_e[:, :, :, :].rearrange("p s h k -> p (s h k)"), att_d[:, :, :, :].rearrange("p s h k -> p (s h k)"),
                                   ACT.Exp, scale=DH1 ** -0.5).then_inc(att_exp, 1)
                if phase == 1 and 0 <= c - 2 < TB:
                    for k in range(KC):
                        copies(("oT", c - 2, k), dT[:, k, :])
                if phase == 3 and 0 <= c - 2 < TB:
                    for k in range(KC):
                        if c >= 3:
                            ring.wait_done(act, ("rt", c - 3))
                        copies(("lT", c - 2, k), lT[:, k, :])
                if phase == 0 and 0 <= c - 3 < TB:
                    act.wait_ge(rl_diff, c - 2)
                    act.activation(rl[:, 1, :, :].rearrange("p s e -> p (s e)"), rl[:, 0, :, :].rearrange("p s e -> p (s e)"),
                                   ACT.Exp).then_inc(rl_exp, 1)

            def expert_turned(e):
                key = ("eT", e, 0)
                if e >= 2:
                    ring.wait_done(act, ("h1", e - 2, FC1 - 1))
                copies_part(key, eT[:, e % 2, 0, :], CAP1)

            expert_turned(0)
            for e in range(E):
                for j in range(FC1):
                    key = ("h1", e, j)
                    if e >= 2:
                        ring.wait_done(act, ("h2", e - 2, RT1 - 1))
                    ring.wait_done(act, key)
                    act.activation(h1[:, e % 2, j, :], ring.bank(key)[:, 0:CAP1], ACT.Gelu_apprx_tanh).then_inc(ring.evacuated(key), 1)
                if e + 1 < E:
                    expert_turned(e + 1)

        @block.vector
        def _(dve):
            count = [0]
            turn = [0]

            def link(ins):
                count[0] += 1
                ins.then_inc(dve_step, 1)
                dve.wait_ge(dve_step, count[0])

            def rsqrt(dst, var, n, scale, floor, add):
                v, t, y = (nwt[:, turn[0], i, 0:n] for i in range(3))
                turn[0] ^= 1
                link(dve.tensor_scalar(v, var, scale, floor, ALU.mult, ALU.add if add else ALU.max))
                link(dve.tensor_scalar(y.bitcast(I32), v.bitcast(I32), -0.5, RSQRT_SEED, ALU.mult, ALU.add))
                for i in range(3):
                    link(dve.tensor_tensor(t, y, y, ALU.mult))
                    link(dve.scalar_tensor_tensor(t, t, -0.5, v, ALU.mult, ALU.mult))
                    last = dve.scalar_tensor_tensor(dst if i == 2 else y, t, 1.5, y, ALU.add, ALU.mult)
                    if i < 2:
                        link(last)
                return last

            def norm_stats(key):
                i = ln_at[key]
                if i >= 4:
                    dve.wait_ge(ln_applied, i - 3)
                if isinstance(key, tuple) and key[0] == "l":
                    src = hid[:, key[1] % 2, :, :]
                elif isinstance(key, tuple) and key[0] != "h":
                    src = x[:, key[1]:NT:TB, :]
                elif isinstance(key, tuple):
                    src = x[:, TB * key[1]:TB * key[1] + TB, :]
                elif key % 3 == 0:
                    b = key // 3
                    dve.wait_ge(x_loaded[b], 16)
                    src = x[:, TB * b:TB * b + TB, :]
                else:
                    b, gg = divmod(key, 3)
                    dve.wait_ge(ctx_loaded[gg - 1], 16 * (b + 1))
                    src = ctx_in[:, gg - 1, :, :]
                for t in range(TB):
                    last = dve.bn_stats(st[:, t, :], src[:, t, :])
                link(last)
                for t in range(TB):
                    last = dve.bn_aggr(mv[:, i % 4, t, :], st[:, t, :])
                link(last)
                var, r = mv[:, i % 4, :, 1], rstd[:, i % 4, :]
                if isinstance(key, tuple) and key[0] == "d" or not isinstance(key, tuple) and key % 3 == 0:
                    link(rsqrt(r, var, TB, 1.0, 1e-5, True))
                    t = lnt[:, 0, :]
                    if isinstance(key, tuple):
                        dve.tensor_copy(hid_rstd[:, :], r)
                    link(dve.tensor_tensor(t, r, r, ALU.mult))
                    link(dve.tensor_tensor(t, t, var, ALU.mult))
                    link(rsqrt(lnt[:, 1, :], t, TB, 1.0, 1e-5, True))
                    dve.tensor_tensor(r, r, lnt[:, 1, :], ALU.mult).then_inc(stats_ready, 1)
                else:
                    rsqrt(r, var, TB, 1.0, 1e-5, True).then_inc(stats_ready, 1)

            def evac_turned(g):
                key = ("xT", g, 0)
                ring.wait_done(dve, key)
                n = "ln_l" if g % 3 == 0 else "ln_x"
                if g >= 2:
                    ring.wait_done(dve, ("v", g - 2, 1))
                dve.tensor_scalar(xnT[:, g % 2, 0, :], ring.bank(key), col(n + "_g0"), col(n + "_b0"),
                                  ALU.mult, ALU.add).then_inc(ring.evacuated(key), 1)

            def key_low(g):
                gg = g % 3
                span = slice(gg * S, (gg + 1) * S)
                for p in range(NPAIR):
                    bank = ring.bank(("kT", g, p))
                    dve.wait_ge(khi_ready, g * NPAIR + p + 1)
                    dve.tensor_tensor(kstack[DH0:P, 2 * p, span], bank[0:DH0, :],
                                      kstack[0:DH0, 2 * p, span].bitcast(F32), ALU.subtract)
                    dve.tensor_tensor(kstack[0:DH0, 2 * p + 1, span], bank[DH0:P, :],
                                      kstack[DH0:P, 2 * p + 1, span].bitcast(F32),
                                      ALU.subtract).then_inc(ring.evacuated(("kT", g, p)), 1)

            def key_norms(g):
                key = ("ss", g)
                b, gg = divmod(g, 3)
                ring.wait_done(dve, key)
                n = TB * H0
                t = kss[:, :]
                ins = dve.tensor_copy(t, ring.bank(key)[:, 0:n])
                ins.then_inc(ring.evacuated(key), 1)
                ring.wait_evacuated(dve, key)
                dst = rkey[:, b % 2, gg * TB:(gg + 1) * TB, :].rearrange("p t h -> p (t h)")
                rsqrt(dst, t, n, 1.0 / DH0, 1e-16, False).then_inc(rkey_ready, 1)

            def query_norms(b):
                for i in range(2):
                    ring.wait_evacuated(dve, ("q", 3 * b, i))
                link(dve.tensor_tensor(qsq[:, :, :], qn[:, :, :], qn[:, :, :], ALU.mult))
                link(dve.tensor_reduce(ssq[:, :], qsq[:, :, :].rearrange("p t (h e) -> p (t h) e", h=H0), AX.X, ALU.add))
                rsqrt(rq[:, :], ssq[:, :], TB * H0, 1.0 / DH0, 1e-16, False).then_inc(rq_ready, 1)

            def query_low(b):
                for h in range(H0):
                    key = ("qT", b, h)
                    dve.wait_ge(qhi_ready, b * H0 + h + 1)
                    dve.scalar_tensor_tensor(qlo[:, h, :], ring.bank(key), gqk[:, 0:1], qhi[:, h, :].bitcast(F32),
                                             ALU.mult, ALU.subtract).then_inc(ring.evacuated(key), 1)

            def add_probs(b, p, j):
                n, m = step(b, p, j), b * NPAIR + p
                for h in range(2):
                    ring.wait_evacuated(dve, ("s", b, p, j, h))
                if j == 0:
                    if m >= 2:
                        ring.wait_done(dve, ("den",) + divmod(m - 2, NPAIR))
                else:
                    dve.wait_ge(psums_added, n)
                src = probs[:, n % 3, :, :].rearrange("p h q -> p (h q)")
                dst = psums[:, m % 2, :]
                if j == 0:
                    dve.tensor_copy(dst, src).then_inc(psums_added, 1)
                else:
                    dve.tensor_tensor(dst, dst, src, ALU.add).then_inc(psums_added, 1)

            def normalize_attention(b, p):
                key, m = ("den", b, p), b * NPAIR + p
                ring.wait_done(dve, key)
                dve.wait_ge(attn_evacuated, m) if m else None
                dve.reciprocal(rden[:, :], ring.bank(key)).then_inc(ring.evacuated(key), 1)
                ring.wait_evacuated(dve, key)
                dve.wait_ge(pv_done, KT0 * (m + 1))
                if b and p == 0:
                    ring.wait_done(dve, ("wo", b - 1, 1))
                dve.tensor_tensor(attnT[:, p, :], acc_psum[:, m % 2, :], rden[:, :], ALU.mult).then_inc(attn_evacuated, 1)

            def add_attention(b):
                dve.wait_ge(bias_added, b + 1)
                for i in range(2):
                    key = ("wo", b, i)
                    ring.wait_done(dve, key)
                    xs = x[:, TB * b + 2 * i:TB * b + 2 * i + 2, :].rearrange("p t d -> p (t d)")
                    dve.tensor_tensor(xs, ring.bank(key), xs, ALU.add).then_inc(ring.evacuated(key), 1)
                for i in range(2):
                    ring.wait_evacuated(dve, ("wo", b, i))

            def choose(b):
                key = ("gate", b)
                ring.wait_evacuated(dve, key)
                flat = score[:, :, :].rearrange("p t e -> p (t e)")
                link(dve.tensor_scalar(flat, rexp[:, :], 1.0, None, ALU.add))
                link(dve.reciprocal(flat, flat))
                for t in range(TB):
                    last = dve.max(top8[:, t, :], score[:, t, :])
                link(last)
                for t in range(TB):
                    last = dve.max_index(idx8[:, t, :], top8[:, t, :], score[:, t, :])
                link(last)
                link(dve.tensor_copy(idxf[:, :, :], idx8[:, :, 0:2]))
                ts = slice(TB * b, TB * b + TB)
                link(dve.tensor_tensor(wtmp[:, :, 0], top8[:, :, 0], top8[:, :, 1], ALU.add))
                link(dve.tensor_scalar(wtmp[:, :, 0], wtmp[:, :, 0], 1e-20, None, ALU.add))
                link(dve.reciprocal(wtmp[:, :, 1], wtmp[:, :, 0]))
                link(dve.scalar_tensor_tensor(weight[:, ts, :], top8[:, :, 0:2], 2.5, bc(wtmp[:, :, 1], 2, 2), ALU.mult, ALU.mult))
                pick_experts(b)

            def pick_experts(b):
                ts = slice(TB * b, TB * b + TB)
                for k in range(2):
                    last = dve.tensor_tensor(pick[:, k, ts, :], bc(iota[:, 0:E], 1, TB), bc(idxf[:, :, k], 2, E), ALU.is_equal)
                link(last)
                link(dve.tensor_tensor(chosen[:, ts, :], pick[:, 0, ts, :], pick[:, 1, ts, :], ALU.add))
                for t in range(TB * b, TB * b + TB):
                    last = dve.tensor_tensor(earlier[:, t + 1, :], earlier[:, t, :], chosen[:, t, :], ALU.add)
                    if t < TB * b + TB - 1:
                        link(last)
                last.then_inc(picks_ready, 1)

            def place_choices(b):
                key = ("rank", b)
                ts = slice(TB * b, TB * b + TB)
                ring.wait_done(dve, key)
                counted = ring.bank(key)[:, 0:TB * E].rearrange("p (t e) -> p t e", e=E)
                for k in range(2):
                    tmp = ptmp[:, k * TB:(k + 1) * TB, :]
                    ins = dve.tensor_tensor(tmp, pick[:, k, ts, :], counted, ALU.mult)
                    if k == 1 and b < B - 1:
                        ins.then_inc(ring.evacuated(key), 1)
                        ring.wait_evacuated(dve, key)
                    else:
                        link(ins)
                    link(dve.tensor_reduce(rank[:, ts, k], tmp, AX.X, ALU.add))
                if b == B - 1:
                    dve.tensor_copy(etiles[:, 0, :], ring.bank(key)[:, TB * E:(TB + 1) * E]).then_inc(ring.evacuated(key), 1)
                link(dve.tensor_copy(rank_i[:, ts, :], rank[:, ts, :]))
                link(dve.tensor_scalar(part_i[:, ts, :], rank_i[:, ts, :], P - 1, None, ALU.bitwise_and))
                link(dve.tensor_copy(rrow[:, ts, :], part_i[:, ts, :]))
                link(dve.tensor_scalar(part_i[:, ts, :], rank_i[:, ts, :], P.bit_length() - 1, None, ALU.arith_shift_right))
                dve.tensor_copy(rtile[:, ts, :], part_i[:, ts, :]).then_inc(rrow_ready, 1)

            dve.wait_ge(small_loaded, 48)
            dve.wait_ge(consts_made, 1)
            norm_stats(0)
            link(dve.tensor_tensor(gqk[:, :], col("gamma_q"), col("gamma_k"), ALU.mult))
            link(dve.tensor_scalar(gqk[:, :], gqk[:, :], DH0 ** -0.5, None, ALU.mult))
            link(dve.tensor_tensor(gbound[:, 0:DH0], row("gamma_q"), row("gamma_k"), ALU.mult))
            link(dve.tensor_reduce(gbound[:, DH0:DH0 + 1], gbound[:, 0:DH0], AX.X, ALU.max, apply_absolute_value=True))
            link(dve.tensor_scalar(gbound[:, DH0 + 1:DH0 + 2], gbound[:, DH0:DH0 + 1], -(DH0 ** 0.5), 80.0, ALU.mult, ALU.add))
            link(dve.tensor_scalar(lbias[:, :], gbound[:, DH0 + 1:DH0 + 2], 0.0, None, ALU.min))
            flat = mbias[:, :, :].rearrange("p b t -> p (b t)")
            link(dve.tensor_scalar(flat, mask8[:, :].bitcast(U8), BIG, -BIG, ALU.mult, ALU.add))
            dve.tensor_scalar(flat, flat, lbias[:, 0:1], None, ALU.add).then_inc(exp_consts_ready, 1)
            norm_stats(1)
            evac_turned(0)
            for b in range(B):
                g = 3 * b
                evac_turned(g + 1)
                key_low(g)
                query_norms(b)
                norm_stats(g + 2)
                evac_turned(g + 2)
                key_norms(g)
                key_low(g + 1)
                query_low(b)
                key_norms(g + 1)
                key_low(g + 2)
                if b + 1 < B:
                    norm_stats(g + 3)
                    norm_stats(g + 4)
                    evac_turned(g + 3)
                key_norms(g + 2)
                for p in range(NPAIR):
                    for j in range(KT0):
                        add_probs(b, p, j)
                        if j == 4 and p == 1:
                            normalize_attention(b, 0)
                        if j == 1 and p == 0 and b:
                            choose(b - 1)
                        if j == 7 and p == 1 and b:
                            place_choices(b - 1)
                normalize_attention(b, 1)
                add_attention(b)
                norm_stats(("h", b))
            choose(B - 1)
            place_choices(B - 1)

            link(dve.tensor_tensor(ecmp[:, 0:E, :], bc(etiles[:, 0, :], 2, E), bc(thresholds[:, :], 1, E), ALU.is_gt))
            link(dve.tensor_reduce(etiles[:, 1, :], ecmp[:, 0:E, :], AX.X, ALU.add))
            link(dve.tensor_tensor_scan(etiles[:, 2, :], etiles[:, 1, :], zero16[:, :], 0.0, ALU.add, ALU.add))
            link(dve.tensor_tensor(etiles[:, 0, :], etiles[:, 2, :], etiles[:, 1, :], ALU.subtract))
            for k in range(2):
                link(dve.tensor_tensor(ptmp[:, :, :], pick[:, k, :, :], bc(etiles[:, 0, :], 1, NT), ALU.mult))
                link(dve.tensor_reduce(dest_f[:, :, k], ptmp[:, :, :], AX.X, ALU.add))
            link(dve.tensor_tensor(rtile[:, :, :], rtile[:, :, :], dest_f[:, :, :], ALU.add))
            ins = dve.tensor_scalar(dest_f[:, :, :], rtile[:, :, :], float(P), None, ALU.mult)
            ins.then_inc(tiles_placed, 1)
            for t in range(NT):
                last = dve.tensor_scalar(tilehot[:, t, 0, 0:NSLOT0], iota[:, 0:NSLOT0], rtile[:, t, 0:1], token_id[:, t:t + 1],
                                         ALU.is_equal, ALU.mult)
            last.then_inc(tilehot_ready, 1)
            link(dve.tensor_tensor(ecmp[:, 0:NSLOT0, :], bc(etiles[:, 2, :], 1, NSLOT0), bc(iota[:, 0:NSLOT0], 2, E), ALU.is_le))
            link(dve.tensor_reduce(eslot[:, 0:NSLOT0], ecmp[:, 0:NSLOT0, :], AX.X, ALU.add))
            dve.tensor_scalar(eslot_i[:, 0:NSLOT0], eslot[:, 0:NSLOT0], float(E - 1), None, ALU.min).then_inc(eslot_ready, 1)
            dve.tensor_tensor(slot_u[:, :, :], dest_f[:, :, :], rrow[:, :, :], ALU.add)
            ring.wait_done(dve, ("source", 0))
            dve.tensor_copy(source[:, 0:NSLOT0], ring.bank(("source", 0))[:, 0:NSLOT0]).then_inc(ring.evacuated(("source", 0)), 1)
            ring.wait_evacuated(dve, ("source", 0))
            link_to = dve.tensor_copy(eslot[:, 0:1], eslot_i[:, 0:1])
            link_to.then_inc(slots_ready, 1)

            def copy_out(key, dst, n):
                ring.wait_done(dve, key)
                dve.tensor_copy(dst, ring.bank(key)[:, 0:n]).then_inc(ring.evacuated(key), 1)

            for i in range(NSLOT0 + 3):
                if i < NSLOT0:
                    if i >= 3:
                        ring.wait_done(dve, ("gu", i - 3))
                    copy_out(("xgT", i), xgT[:, i % 3, :], D)
                if 1 <= i <= NSLOT0:
                    s = i - 1
                    key = ("gu", s)
                    dve.wait_ge(silu_ready, s + 1)
                    if s >= 2:
                        ring.wait_done(dve, ("mT", s - 2))
                    dve.tensor_tensor(mid[:, s % 2, :], silu[:, s % 2, :], ring.bank(key)[:, M0:2 * M0],
                                      ALU.mult).then_inc(ring.evacuated(key), 1)
                if 2 <= i <= NSLOT0 + 1:
                    s = i - 2
                    if s >= 2:
                        ring.wait_done(dve, ("y", s - 2))
                    copy_out(("mT", s), midT[:, s % 2, :], P)

            def combine(n):
                t = tile_of(n)
                dve.wait_ge(y_gathered[n % NYG], 32 * (n // NYG + 1))
                if n == 0:
                    dve.wait_ge(shared_added, NT)
                link(dve.scalar_tensor_tensor(x[:, t, :], yg[:, n % NYG, 0, :], weight[:, t, 0:1], x[:, t, :], ALU.mult, ALU.add))
                dve.scalar_tensor_tensor(x[:, t, :], yg[:, n % NYG, 1, :], weight[:, t, 1:2], x[:, t, :], ALU.mult,
                                         ALU.add).then_inc(combined, 1)

            for n in range(B):
                combine(n)
            dve.wait_ge(combined, B)
            norm_stats(("c", 0))
            link(dve.memset(att_s[:, :, :, :], -BIG))

            def context_max(n):
                if n >= 2:
                    for half in range(2):
                        ring.wait_evacuated(dve, ("cs", n - 2, half))
                for half in range(2):
                    ring.wait_done(dve, ("cs", n, half))
                    last = dve.tensor_reduce(cmax[:, n % 2, half:half + 1], ring.bank(("cs", n, half)), AX.X, ALU.max)
                link(last)
                link(dve.tensor_tensor(cmax[:, n % 2, 2:3], cmax[:, n % 2, 0:1], cmax[:, n % 2, 1:2], ALU.max))
                dve.tensor_scalar(cmax[:, n % 2, 3:4], cmax[:, n % 2, 2:3], -CSCALE, None, ALU.mult).then_inc(cmax_ready, 1)

            def add_context(n):
                t, key = tile_of(n), ("co", n)
                link(dve.tensor_tensor(csum[:, n % 3, 2:3], csum[:, n % 3, 0:1], csum[:, n % 3, 1:2], ALU.add))
                link(dve.reciprocal(csum[:, n % 3, 3:4], csum[:, n % 3, 2:3]))
                ring.wait_done(dve, key)
                dve.scalar_tensor_tensor(x[:, t, :], ring.bank(key)[:, 0:D], csum[:, n % 3, 3:4], x[:, t, :],
                                         ALU.mult, ALU.add).then_inc(ring.evacuated(key), 1)
                ring.wait_evacuated(dve, key)
                dve.tensor_copy(csum[:, n % 3, 2:3], csum[:, n % 3, 3:4]).then_inc(x2_done, 1)

            def attend_scores(c):
                for s in range(B):
                    ring.wait_evacuated(dve, ("qkv", c, s))
                if c:
                    dve.wait_ge(att_diff, c)
                for k in range(B):
                    n = B - k
                    q = qkv[:, k:B, 0:H1 * DH1].rearrange("p s (g r d) -> p s g r d", g=KV1, d=DH1)
                    key = bc(bc(qkv[:, k, H1 * DH1:(H1 + KV1) * DH1].rearrange("p (g d) -> p g d", d=DH1), 2, H1 // KV1), 1, n)
                    pr = prod[:, 0:n, :].rearrange("p s (g r d) -> p s g r d", g=KV1, d=DH1)
                    for s in range(n):
                        last = dve.tensor_tensor(pr[:, s], q[:, s], key[:, s], ALU.mult)
                    link(last)
                    last = dve.tensor_reduce(att_s[:, k:B, :, k], prod[:, 0:n, :].rearrange("p s (h d) -> p s h d", d=DH1), AX.X, ALU.add)
                    link(last)
                link(dve.tensor_reduce(att_m[:, 0, :, :], att_s[:, :, :, :], AX.X, ALU.max))
                if c:
                    dve.wait_ge(att_exp, c)
                dve.tensor_tensor(att_d[:, :, :, :], att_s[:, :, :, :], bc(att_m[:, 0, :, :], 3, B), ALU.subtract).then_inc(att_diff, 1)

            def attend_values(c):
                dve.wait_ge(att_exp, c + 1)
                link(dve.tensor_reduce(att_m[:, 1, :, :], att_e[:, :, :, :], AX.X, ALU.add))
                link(dve.reciprocal(att_m[:, 1, :, :], att_m[:, 1, :, :]))
                link(dve.tensor_tensor(att_e[:, :, :, :], att_e[:, :, :, :], bc(att_m[:, 1, :, :], 3, B), ALU.mult))
                if c:
                    ring.wait_done(dve, ("oT", c - 1, KC - 1))
                for k in range(B):
                    n = B - k
                    v = bc(qkv[:, k, (H1 + KV1) * DH1:QKV].rearrange("p (g d) -> p g d", d=DH1), 2, H1 // KV1)
                    dst = att_o if k == 0 else prod
                    for s in range(n):
                        last = dve.tensor_tensor(dst[:, s, :].rearrange("p (g r d) -> p g r d", g=KV1, d=DH1), v,
                                                 bc(att_e[:, k + s, :, k].rearrange("p (g r) -> p g r", g=KV1), 3, DH1), ALU.mult)
                    link(last)
                    if k:
                        last = dve.tensor_tensor(att_o[:, k:B, :], att_o[:, k:B, :], prod[:, 0:n, :], ALU.add)
                        if k < B - 1:
                            link(last)
                last.then_inc(att_done, 1)

            def start_hidden(c):
                i = ln_at["d", c]
                if c >= 2:
                    dve.wait_ge(ln_applied, ln_at["l", c - 2] + 1)
                dve.wait_ge(stats_ready, i + 1)
                for s in range(B):
                    last = dve.tensor_scalar(hid[:, c % 2, s, :], x[:, c + s * TB, :], mv[:, i % 4, s, 0:1], hid_rstd[:, s:s + 1],
                                             ALU.subtract, ALU.mult)
                link(last)

            def add_hidden(c):
                dve.wait_ge(ln_applied, ln_at["d", c] + 1)
                dve.tensor_tensor(x[:, c:NT:TB, :], x[:, c:NT:TB, :], hid[:, c % 2, :, :], ALU.add).then_inc(x3_done, 1)

            def add_projection(c):
                for i in range(2):
                    key = ("po", c, i)
                    ring.wait_done(dve, key)
                    xs = hid[:, c % 2, 2 * i:2 * i + 2, :]
                    dve.tensor_tensor(xs, ring.bank(key).rearrange("p (t d) -> p t d", t=2), xs, ALU.add).then_inc(ring.evacuated(key), 1)
                for i in range(2):
                    ring.wait_evacuated(dve, ("po", c, i))

            def router_diff(c):
                key = ("rt", c)
                ring.wait_done(dve, key)
                logits = ring.bank(key)[:, 0:B * E].rearrange("p (s e) -> p s e", e=E)
                link(dve.tensor_reduce(rm[:, 0, :], logits, AX.X, ALU.max))
                dve.tensor_tensor(rl[:, 0, :, :], logits, bc(rm[:, 0, :], 2, E), ALU.subtract).then_inc(ring.evacuated(key), 1)
                ring.wait_evacuated(dve, key)
                dve.tensor_copy(rm[:, 1, :], rm[:, 0, :]).then_inc(rl_diff, 1)

            def choose2(c):
                ts = slice(c, NT, TB)
                dve.wait_ge(rl_exp, c + 1)
                link(dve.tensor_reduce(rm[:, 0, :], rl[:, 1, :, :], AX.X, ALU.add))
                link(dve.reciprocal(rm[:, 1, :], rm[:, 0, :]))
                link(dve.tensor_tensor(score[:, :, :], rl[:, 1, :, :], bc(rm[:, 1, :], 2, E), ALU.mult))
                for s in range(B):
                    last = dve.max(top8[:, s, :], score[:, s, :])
                link(last)
                for s in range(B):
                    last = dve.max_index(idx8[:, s, :], top8[:, s, :], score[:, s, :])
                link(last)
                link(dve.tensor_copy(idxf[:, :, :], idx8[:, :, 0:2]))
                dve.tensor_copy(weight2[:, ts, :], top8[:, :, 0:2])
                for k in range(2):
                    last = dve.tensor_tensor(pick[:, k, ts, :], bc(iota[:, 0:E], 1, B), bc(idxf[:, :, k], 2, E), ALU.is_equal)
                link(last)
                link(dve.tensor_tensor(chosen[:, ts, :], pick[:, 0, ts, :], pick[:, 1, ts, :], ALU.add))

            for i in range(NSTEP):
                c, phase = divmod(i, B)
                if i < NT:
                    context_max(i)
                if phase == 2 and 0 <= c - 2 < TB:
                    add_projection(c - 2)
                if 1 <= i <= NT:
                    if i >= 3:
                        ring.wait_done(dve, ("co", i - 3))
                    copy_out(("cp", i - 1, 1), cprobT[:, (i - 1) % 2, 512:1024], 512)
                if 2 <= i <= NT + 1:
                    add_context(i - 2)
                if phase == 2 and c + 1 < TB:
                    for n in range(B * (c + 1), B * (c + 2)):
                        combine(n)
                    dve.wait_ge(combined, B * (c + 2))
                    norm_stats(("c", c + 1))
                if phase == 1 and 0 <= c - 1 < TB:
                    norm_stats(("d", c - 1))
                    start_hidden(c - 1)
                if phase == 3 and 0 <= c - 1 < TB:
                    attend_scores(c - 1)
                if phase == 0 and 0 <= c - 2 < TB:
                    attend_values(c - 2)
                if phase == 2 and 0 <= c - 2 < TB:
                    norm_stats(("l", c - 2))
                if phase == 3 and 0 <= c - 2 < TB:
                    router_diff(c - 2)
                    add_hidden(c - 2)
                if phase == 0 and 0 <= c - 3 < TB:
                    choose2(c - 3)

            for t in range(NT):
                last = dve.tensor_tensor(earlier[:, t + 1, :], earlier[:, t, :], chosen[:, t, :], ALU.add)
                if t < NT - 1:
                    link(last)
            last.then_inc(picks2_ready, 1)
            key = ("rank2", 0)
            ring.wait_done(dve, key)
            counted = ring.bank(key)[:, 0:NT * E].rearrange("p (t e) -> p t e", e=E)
            for k in range(2):
                link(dve.tensor_tensor(ptmp[:, :, :], pick[:, k, :, :], counted, ALU.mult))
                link(dve.tensor_reduce(rank[:, :, k], ptmp[:, :, :], AX.X, ALU.add))
            dve.tensor_copy(etiles[:, 1, :], ring.bank(key)[:, 0:E]).then_inc(ring.evacuated(key), 1)
            for k in range(2):
                link(dve.tensor_tensor(ptmp[:, :, :], pick[:, k, :, :], bc(iota[:, 0:E], 1, NT), ALU.mult))
                link(dve.tensor_reduce(dest_f[:, :, k], ptmp[:, :, :], AX.X, ALU.add))
            link(dve.tensor_scalar(keep[:, :, :], rank[:, :, :], float(CAP1), None, ALU.is_lt))
            link(dve.tensor_copy(rank_i[:, :, :], rank[:, :, :]))
            link(dve.tensor_scalar(part_i[:, :, :], rank_i[:, :, :], P - 1, None, ALU.bitwise_and))
            link(dve.tensor_copy(rrow[:, :, :], part_i[:, :, :]))
            link(dve.tensor_scalar(part_i[:, :, :], rank_i[:, :, :], P.bit_length() - 1, None, ALU.arith_shift_right))
            link(dve.tensor_copy(rtile[:, :, :], part_i[:, :, :]))
            link(dve.scalar_tensor_tensor(rtile[:, :, :], dest_f[:, :, :], float(RT1), rtile[:, :, :], ALU.mult, ALU.add))
            link(dve.scalar_tensor_tensor(rtile[:, :, :], keep[:, :, :], -1000.0, rtile[:, :, :], ALU.mult, ALU.add))
            dve.tensor_scalar(rtile[:, :, :], rtile[:, :, :], 1000.0, None, ALU.add).then_inc(places2_ready, 1)
            dve.wait_ge(places2_ready, 1)
            for t in range(DVE_HOTS):
                for k in range(2):
                    dve.tensor_scalar(rowhot[:, t, k, :], iota[:, :], rrow[:, t, k:k + 1], None, ALU.is_equal)
                    last = dve.tensor_scalar(tilehot[:, t, k, :], iota[:, 0:NSLOT1], rtile[:, t, k:k + 1], token_id[:, t:t + 1],
                                             ALU.is_equal, ALU.mult)
            last.then_inc(hots2_ready, 1)
            link(dve.scalar_tensor_tensor(dest_f[:, :, :], dest_f[:, :, :], float(CAP1), rank[:, :, :], ALU.mult, ALU.add))
            dve.tensor_tensor(slot_u[:, :, :], dest_f[:, :, :], keep[:, :, :], ALU.mult)
            link(dve.tensor_tensor(weight2[:, :, :], weight2[:, :, :], keep[:, :, :], ALU.mult))
            ring.wait_done(dve, ("source", 1))
            dve.tensor_copy(source[:, 0:NSLOT1], ring.bank(("source", 1))[:, 0:NSLOT1]).then_inc(ring.evacuated(("source", 1)), 1)
            ring.wait_evacuated(dve, ("source", 1))
            dve.tensor_copy(eslot[:, 0:1], source[:, 0:1]).then_inc(slots2_ready, 1)

            def expert_turned(e):
                if e >= 2:
                    ring.wait_done(dve, ("h1", e - 2, FC1 - 1))
                copy_out(("eT", e, 1), eT[:, e % 2, 1, :], CAP1)

            expert_turned(0)
            for e in range(E):
                if e + 1 < E:
                    expert_turned(e + 1)
                for r in range(RT1):
                    n, j = min(P, CAP1 - r * P), e * RT1 + r
                    key = ("h2", e, r)
                    if j >= 3:
                        dve.wait_ge(y2_stored[j % 3], 16 * (j // 3))
                    ring.wait_done(dve, key)
                    dve.tensor_copy(y2[0:n, j % 3, :], ring.bank(key)[0:n, 0:D]).then_inc(ring.evacuated(key), 1)
            dve.wait_ge(x3_done, TB)
            for t in range(NT):
                dve.wait_ge(y2_gathered[t % NYG], 32 * (t // NYG + 1))
                link(dve.scalar_tensor_tensor(x[:, t, :], yg[:, t % NYG, 0, :], weight2[:, t, 0:1], x[:, t, :], ALU.mult, ALU.add))
                dve.scalar_tensor_tensor(x[:, t, :], yg[:, t % NYG, 1, :], weight2[:, t, 1:2], x[:, t, :], ALU.mult,
                                         ALU.add).then_inc(finished, 1)


def lay_out(inputs):
    f = {k: np.asarray(v) for k, v in inputs.items()}

    def chunks(w):
        return np.ascontiguousarray(w.reshape(-1, P, w.shape[-1]).transpose(1, 0, 2))

    def halves(v):
        return [v[:P], v[P:]]

    gq, gk = f["L0_xattn_q_gamma"], f["L0_xattn_k_gamma"]
    cols = []
    for n in ("L0_xattn_ln_x_g", "L0_xattn_ln_x_b", "L0_xattn_ln_l_g", "L0_xattn_ln_l_b", "L1_ffn_ln1_weight", "L1_ffn_ln1_bias"):
        cols += halves(f[n])
    cols += [np.concatenate([gq, gq]), np.concatenate([gk, gk])]
    rows = np.concatenate([f["L0_xattn_b_out"], f["L1_ffn_ln2_weight"], f["L1_ffn_ln2_bias"], gq, gk])
    wg, wu, wd = f["L0_ffn_w_gate"], f["L0_ffn_w_up"], f["L0_ffn_w_down"]
    gu = np.concatenate([wg, wu], axis=2)
    return {
        "x": f["x"],
        "ctx": f["ctx_1024"],
        "ctxT": np.ascontiguousarray(f["ctx_1024"].transpose(2, 0, 1)).reshape(KC, P, B, SC).transpose(1, 0, 2, 3).copy(),
        "mask": np.ascontiguousarray(f["mask_BxS2_bk0"].reshape(B, CTB, P).transpose(2, 0, 1).reshape(P, B * CTB)).view(np.uint32),
        "cols": np.ascontiguousarray(np.stack(cols, axis=1)),
        "rows": np.ascontiguousarray(np.broadcast_to(rows, (P, NROW))),
        "wq": chunks(f["L0_xattn_W_q"]),
        "wkv": chunks(f["L0_xattn_W_kv"]),
        "wout": chunks(f["L0_xattn_W_out"]),
        "gate_w": chunks(f["L0_ffn_gate_w"].T),
        "sh_gu": chunks(np.concatenate([f["L0_ffn_ws_gate"], f["L0_ffn_ws_up"]], axis=1)),
        "sh_dn": f["L0_ffn_ws_down"],
        "e_gu": np.ascontiguousarray(gu.reshape(E, KC, P, 2 * M0).transpose(2, 1, 0, 3)),
        "e_dn": np.ascontiguousarray(wd.transpose(1, 0, 2)),
        "qkv_w": chunks(f["L1_ffn_qkv_weight"].T),
        "proj_w": chunks(f["L1_ffn_proj_weight"].T),
        "router_w": chunks(f["L1_ffn_router_weight"].T),
        "w1": np.ascontiguousarray(f["L1_ffn_moe_w1"].transpose(0, 2, 1).reshape(E, KC, P, F1).transpose(0, 2, 1, 3)),
        "w2": np.ascontiguousarray(f["L1_ffn_moe_w2"].transpose(0, 2, 1).reshape(E, FC1, P, D).transpose(0, 2, 1, 3)),
    }


def kernel(**inputs):
    import concourse.bacc as bacc
    from concourse.bass_utils import run_bass_kernel_spmd as run

    nc = bacc.Bacc("TRN2", target_bir_lowering=False, num_devices=1)
    arrays = lay_out(inputs)
    a = {n: nc.dram_tensor(f"in_{n}", v.shape, mybir.dt.from_np(v.dtype), kind="ExternalInput").ap() for n, v in arrays.items()}
    out = nc.dram_tensor("out", (B, S, D), F32, kind="ExternalOutput").ap()
    build(nc, a, out)
    r = run(nc, [{f"in_{n}": v for n, v in arrays.items()}], core_ids=[0])
    return r.results[0]["out"]
```

```python
from contextlib import ExitStack

import numpy as np

import concourse.bass as bass
from concourse import mybir

F32 = mybir.dt.float32
F32R = mybir.dt.float32r
F16 = mybir.dt.float16
I32 = mybir.dt.int32
U32 = mybir.dt.uint32
U8 = mybir.dt.uint8
ALU = mybir.AluOpType
ACT = mybir.ActivationFunctionType
AX = mybir.AxisListType

P = 128
B, S, D = 4, 512, 256
KC = D // P
TB = S // P
NT = B * TB
SC = 1024
CTB = SC // P
H0, DH0 = 4, 64
NPAIR = H0 // 2
KT0 = TB + CTB
NG = B * 3
E = 16
M0 = 128
F1 = 512
FC1 = F1 // P
NSLOT0 = (2 * NT * P + E * (P - 1)) // P
CAP1 = -(-(NT * P * 2 * 5) // (E * 4))
RT1 = -(-CAP1 // P)
NSLOT1 = E * RT1
H1, KV1, DH1 = 16, 4, 16
NRING = 6
NXG = 4
NYG = 4
RSQRT_SEED = float(0x5F3759DF)
BIG = 1e30

COLS = ("ln_x_g0", "ln_x_g1", "ln_x_b0", "ln_x_b1", "ln_l_g0", "ln_l_g1", "ln_l_b0", "ln_l_b1",
        "ln1_w0", "ln1_w1", "ln1_b0", "ln1_b1", "gamma_q", "gamma_k")
ROWS = {"b_out": (0, D), "ln2_w": (D, D), "ln2_b": (2 * D, D), "gamma_q": (3 * D, DH0), "gamma_k": (3 * D + DH0, DH0)}
NROW = 3 * D + 2 * DH0
NSTEP = NT + 12
CSCALE = 0.25
QKV = (H1 + 2 * KV1) * DH1
VALUES_DVE = [(), (), (0, 3), (0, 3)]
VALUES_POOL = [(0, 1, 2, 3), (0, 1, 2, 3), (1, 2), (1, 2)]
NW = 4


def bc(ap, axis, n):
    a = ap.unsqueeze(axis)
    shape = list(a.shape)
    shape[axis] = n
    return a.broadcast_to(shape)


class BankRing:

    def __init__(self, banks, n, unit_done, evacuated):
        self.banks, self.n, self.unit_done, self.evac = banks, n, unit_done, evacuated
        self.place = {}
        self.uses = [0] * len(banks)
        self.next = 0

    def take(self, pe, key):
        b = self.next
        self.next = (b + 1) % self.n
        self.place[key] = len(self.place), b, self.uses[b]
        if self.uses[b]:
            pe.wait_ge(self.evac[b], self.uses[b])
        self.uses[b] += 1
        return self.banks[b]

    def grow(self):
        self.n = len(self.banks)

    def bank(self, key):
        return self.banks[self.place[key][1]]

    def evacuated(self, key):
        return self.evac[self.place[key][1]]

    def wait_done(self, eng, key):
        eng.wait_ge(self.unit_done, self.place[key][0] + 1)

    def wait_evacuated(self, eng, key):
        _, b, uses = self.place[key]
        eng.wait_ge(self.evac[b], uses + 1)


def build(nc, a, out):
    ctx = ExitStack()
    with ctx:
        def sb(name, shape, dt=F32):
            return ctx.enter_context(nc.sbuf_tensor(name, shape, dt))

        def sem(name):
            return ctx.enter_context(nc.semaphore(name))

        x = sb("x_res", [P, NT, D])
        ident = sb("ident", [P, P])
        ones = sb("ones", [P, P])
        headsel = sb("headsel", [P, 2])
        before = sb("before", [P, P], F16)
        ones16 = sb("ones16", [P, P], F16)
        iota = sb("iota", [P, P])
        iota16 = sb("iota16", [P, P], F16)
        token16 = sb("token16", [P, NT, 2], F16)
        rrow16 = sb("rrow16", [P, NT, 2], F16)
        rtile16 = sb("rtile16", [P, NT, 2], F16)
        thresholds = sb("thresholds", [P, E])
        zero16 = sb("zero16", [P, E])
        cols = sb("cols", [P, len(COLS)])
        rows = sb("rows", [P, NROW])
        mv = sb("mv", [P, 4, TB, 2])
        st = sb("st", [P, TB, 6])
        rstd = sb("rstd", [P, 4, TB])
        nwt = sb("nwt", [P, 2, 3, 48])
        lnt = sb("lnt", [P, 2, TB])
        hid_rstd = sb("hid_rstd", [P, TB])
        kss = sb("kss", [P, 3, TB * H0])
        weight2 = sb("weight2", [P, NT, 2])
        keep = sb("keep", [P, NT, 2])
        mask8 = sb("mask8", [P, B * CTB // 4], U32)
        pick = sb("pick", [P, 2, NT, E])
        weight = sb("weight", [P, NT, 2])
        chosen = sb("chosen", [P, NT, E], F16)
        earlier = sb("earlier", [P, NT + 1, E], F16)
        top8 = sb("top8", [P, TB, 8])
        idx8 = sb("idx8", [P, TB, 8], U32)
        idxf = sb("idxf", [P, TB, 2])
        score = sb("score", [P, TB, E])
        wtmp = sb("wtmp", [P, TB, 2])
        ptmp = sb("ptmp", [P, NT, E])
        rank = sb("rank", [P, NT, 2])
        rank_i = sb("rank_i", [P, NT, 2], I32)
        part_i = sb("part_i", [P, NT, 2], I32)
        rrow = sb("rrow", [P, NT, 2])
        rtile = sb("rtile", [P, NT, 2])
        rowhot = sb("rowhot", [P, NT, 2, P], F16)
        tilehot = sb("tilehot", [P, NT, 2, 48], F16)
        etiles = sb("etiles", [P, 3, E])
        ecmp = sb("ecmp", [P, 48, E])
        eslot = sb("eslot", [P, 48])
        eslot_i = sb("eslot_i", [P, 48], I32)
        slot_u = sb("slot_u", [P, NT, 2], U32)
        source = sb("source", [P, 48], U32)
        dest_f = sb("dest_f", [P, NT, 2])

        base = int(nc.sbuf_base) + 64
        arena = nc.sbuf_usable_end

        def place(at, name, shape, dt=F32):
            size = int(np.prod(shape[1:])) * {F16: 2, U8: 1}.get(dt, 4)
            t = nc.alloc_sbuf_tensor_at(name, shape, dt, offset=at[0])
            at[0] += -(-size // 32) * 32
            assert at[0] <= arena, (name, at[0], arena)
            return t

        at = [-(-base // 64) * 64]
        hT_at = at[0]
        hT = place(at, "hT", [P, KC, NT * P])
        gate_w = place(at, "gate_w", [P, KC, E])
        sh_gu = place(at, "sh_gu", [P, KC, 2 * M0])
        sh_dn = place(at, "sh_dn", [P, D])
        qkv_w = place(at, "qkv_w", [P, KC, QKV])
        proj_w = place(at, "proj_w", [P, KC, D])
        router_w = place(at, "router_w", [P, KC, E])
        hn = place(at, "hn", [P, 1, TB, D])
        rexp = place(at, "rexp", [P, TB * E])
        phase_at = at[0]
        wq = place(at, "wq", [P, KC, D])
        wkv = place(at, "wkv", [P, KC, 2 * D])
        wout = place(at, "wout", [P, KC, D])
        ctx_in = place(at, "ctx_in", [P, 2, TB, D])
        xn = place(at, "xn", [P, 2, TB, D])
        xnT = place(at, "xnT", [P, 2, KC, S])
        kstack = place(at, "kstack", [P, H0, KT0 * P], F32R)
        vals = place(at, "vals", [P, KT0, D])
        ksq = place(at, "ksq", [P, NPAIR, S])
        rkey = place(at, "rkey", [P, 2, KT0, H0])
        qn = place(at, "qn", [P, TB, D])
        qsq = place(at, "qsq", [P, TB, D])
        ssq = place(at, "ssq", [P, TB * H0])
        rq = place(at, "rq", [P, TB * H0])
        qdup = place(at, "qdup", [P, TB * H0, 2, DH0])
        qhi = place(at, "qhi", [P, H0, S], F32R)
        qlo = place(at, "qlo", [P, H0, S], F32R)
        gqk = place(at, "gqk", [P, 1])
        gbound = place(at, "gbound", [P, DH0 + 2])
        mbias = place(at, "mbias", [P, B, CTB])
        lbias = place(at, "lbias", [P, 1])
        probs = place(at, "probs", [P, 3, 2, S])
        psums = place(at, "psums", [P, 2, 2 * S])
        rden = place(at, "rden", [P, S])
        attnT = place(at, "attnT", [P, NPAIR, S])
        at = [phase_at]
        yg = place(at, "yg", [P, NYG, 2, D])
        ctx_at = at[0]
        ctx_n = place(at, "ctx_n", [P, B, CTB, D])
        ctx_t = place(at, "ctx_t", [P, KC, B, SC])
        work_at = at[0]
        at = [ctx_at]
        w1 = place(at, "w1", [P, NW, KC, F1])
        w2 = place(at, "w2", [P, NW, FC1, D])
        eT = place(at, "eT", [P, 2, KC, CAP1])
        h1 = place(at, "h1", [P, 2, FC1, CAP1])
        y2 = place(at, "y2", [P, 3, D])
        xg2 = place(at, "xg2", [P, NXG, D])
        assert at[0] <= work_at
        at = [work_at]
        un = place(at, "un", [P, B, D])
        uT = place(at, "uT", [P, KC, B * P])
        cprob = place(at, "cprob", [P, 2, SC])
        cprobT = place(at, "cprobT", [P, 2, SC])
        csum = place(at, "csum", [P, 3, 4])
        cmax = place(at, "cmax", [P, 2, 4])
        dn = place(at, "dn", [P, B, D])
        dT = place(at, "dT", [P, KC, B * P])
        hid = place(at, "hid", [P, 2, B, D])
        l_n = place(at, "l_n", [P, B, D])
        lT = place(at, "lT", [P, KC, B * P])
        qkv = place(at, "qkv", [P, B, QKV])
        prod = place(at, "prod", [P, B, D])
        at = [hT_at]
        att_s = place(at, "att_s", [P, B, H1, B])
        att_d = place(at, "att_d", [P, B, H1, B])
        att_e = place(at, "att_e", [P, B, H1, B])
        att_m = place(at, "att_m", [P, 2, B, H1])
        att_o = place(at, "att_o", [P, B, D])
        value_prod = place(at, "value_prod", [P, B, D])
        rl = place(at, "rl", [P, 2, B, E])
        rm = place(at, "rm", [P, 2, B])
        at = [work_at]
        e_gu = place(at, "e_gu", [P, KC, E, 2 * M0])
        e_dn = place(at, "e_dn", [P, E, D])
        xg = place(at, "xg", [P, NXG, D])
        xgT = place(at, "xgT", [P, 3, D])
        silu = place(at, "silu", [P, 2, M0])
        up = place(at, "up", [P, 2, M0])
        mid = place(at, "mid", [P, 2, M0])
        midT = place(at, "midT", [P, 2, P])
        ysb = place(at, "ysb", [P, 3, D])

        ring_psum = ctx.enter_context(nc.psum_tensor("ring_psum", [P, NRING, 512], F32))
        acc_psum = ctx.enter_context(nc.psum_tensor("acc_psum", [P, 2, 512], F32))

        h_rows = nc.dram_tensor("h_rows", (NT * P, D), F32).ap()
        l_rows = nc.dram_tensor("l_rows", (NT * P, D), F32).ap()
        y2_rows = nc.dram_tensor("y2_rows", (E * CAP1, D), F32).ap()
        y_rows = nc.dram_tensor("y_rows", (NSLOT0 * P, D), F32).ap()

        x_loaded = [sem(f"x_loaded{b}") for b in range(B)]
        ctx_loaded = [sem(f"ctx_loaded{i}") for i in range(2)]
        small_loaded = sem("small_loaded")
        wa_loaded = sem("wa_loaded")
        wb_loaded = sem("wb_loaded")
        consts_made = sem("consts_made")
        dve_step = sem("dve_step")
        pool_step = sem("pool_step")
        unit_done = sem("unit_done")
        evacuated = [sem(f"evacuated{i}") for i in range(NRING + 2)]
        ln_applied = sem("ln_applied")
        bias_added = sem("bias_added")
        khi_ready = sem("khi_ready")
        rkey_ready = sem("rkey_ready")
        rq_ready = sem("rq_ready")
        qdup_ready = sem("qdup_ready")
        qhi_ready = sem("qhi_ready")
        exp_consts_ready = sem("exp_consts_ready")
        pv_done = sem("pv_done")
        psums_added = sem("psums_added")
        attn_evacuated = sem("attn_evacuated")
        x_updated = sem("x_updated")
        hn_stored = sem("hn_stored")
        picks_ready = sem("picks_ready")
        rrow_ready = sem("rrow_ready")
        rowhot_ready = sem("rowhot_ready")
        out_stored = sem("out_stored")
        e_loaded = sem("e_loaded")
        shared_mid = sem("shared_mid")
        shared_added = sem("shared_added")
        tilehot_ready = sem("tilehot_ready")
        eslot_ready = sem("eslot_ready")
        slots_ready = sem("slots_ready")
        gathered = [sem(f"gathered{i}") for i in range(NXG)]
        silu_ready = sem("silu_ready")
        y_stored = [sem(f"y_stored{i}") for i in range(3)]
        y_gathered = [sem(f"y_gathered{i}") for i in range(NYG)]
        combined = sem("combined")
        combined_later = sem("combined_later")
        ctx_n_loaded = sem("ctx_n_loaded")
        ctx_t_loaded = sem("ctx_t_loaded")
        wd_loaded = sem("wd_loaded")
        cmax_ready = sem("cmax_ready")
        x2_done = sem("x2_done")
        att_diff = sem("att_diff")
        att_exp = sem("att_exp")
        att_weights = sem("att_weights")
        att_done = sem("att_done")
        att_done_pool = sem("att_done_pool")
        x3_done = sem("x3_done")
        l_stored = sem("l_stored")
        rl_diff = sem("rl_diff")
        rl_exp = sem("rl_exp")
        picks2_ready = sem("picks2_ready")
        hots2_ready = sem("hots2_ready")
        slots2_ready = sem("slots2_ready")
        gathered2 = [sem(f"gathered2_{i}") for i in range(NXG)]
        w_loaded = [sem(f"w_loaded{i}") for i in range(NW)]
        y2_stored = [sem(f"y2_stored{i}") for i in range(3)]
        y2_gathered = [sem(f"y2_gathered{i}") for i in range(NYG)]
        finished = sem("finished")

        banks = [ring_psum[:, i, :] for i in range(NRING)] + [acc_psum[:, i, :] for i in range(2)]
        ring = BankRing(banks, NRING, unit_done, evacuated)

        def col(name):
            i = COLS.index(name)
            return cols[:, i:i + 1]

        def row(name):
            o, n = ROWS[name]
            return rows[:, o:o + n]

        ln_order = [0, 1]
        for b in range(B):
            ln_order.append(3 * b + 2)
            if b + 1 < B:
                ln_order.append(3 * b + 3)
            if b:
                ln_order.append(("h", b - 1))
            if b + 1 < B:
                ln_order.append(3 * b + 4)
        ln_order.append(("h", B - 1))
        ln_order.append(("c", 0))
        for i in range(NSTEP):
            if i % B == 2 and i // B + 1 < TB:
                ln_order.append(("c", i // B + 1))
            if i % B == 1 and 5 <= i < 5 + NT:
                ln_order.append(("d", (i - 5) // B))
            if i % B == 3 and 11 <= i < 11 + NT:
                ln_order.append(("l", (i - 11) // B))
        ln_at = {k: i for i, k in enumerate(ln_order)}

        def step(b, p, j):
            return (b * NPAIR + p) * KT0 + j

        def tile_of(n):
            return n % B * TB + n // B

        def add_shared(pool, t):
            ring.wait_evacuated(pool, ("sy", t))
            pool.tensor_tensor(x[:, t, :], x[:, t, :], ysb[:, t % 2, :], ALU.add).then_inc(shared_added, 1)

        def combine(eng, link, n):
            t = tile_of(n)
            eng.wait_ge(y_gathered[n % NYG], 32 * (n // NYG + 1))
            if n == 0:
                eng.wait_ge(shared_added, NT)
            both = yg[:, n % NYG, :, :]
            link(eng.tensor_tensor(both, both, bc(weight[:, t, :], 2, D), ALU.mult))
            link(eng.tensor_tensor(x[:, t, :], x[:, t, :], both[:, 0, :], ALU.add))
            eng.tensor_tensor(x[:, t, :], x[:, t, :], both[:, 1, :], ALU.add).then_inc(combined if n < B else combined_later, 1)

        def wait_values(eng, c):
            eng.wait_ge(att_done_pool, c + 1)
            if VALUES_DVE[c]:
                eng.wait_ge(att_done, sum(1 for q in VALUES_DVE[:c + 1] if q))

        def attend_values(eng, link, c, queries, product, done):
            eng.wait_ge(att_weights, c + 1)
            if c:
                ring.wait_done(eng, ("oT", c - 1, KC - 1))
            for k in range(queries[-1] + 1):
                v = bc(qkv[:, k, (H1 + KV1) * DH1:QKV].rearrange("p (g d) -> p g d", d=DH1), 2, H1 // KV1)
                seen_by = [s for s in queries if s >= k]
                for s in seen_by:
                    dst = att_o if k == 0 else product
                    last = eng.tensor_tensor(dst[:, s, :].rearrange("p (g r d) -> p g r d", g=KV1, d=DH1), v,
                                             bc(att_e[:, s, :, k].rearrange("p (g r) -> p g r", g=KV1), 3, DH1), ALU.mult)
                link(last)
                if k:
                    for s in seen_by:
                        last = eng.tensor_tensor(att_o[:, s, :], att_o[:, s, :], product[:, s, :], ALU.add)
                    if k < queries[-1]:
                        link(last)
            last.then_inc(done, 1)

        assert CAP1 - (RT1 - 1) * P == P // 2 and E % 2 == 0
        down_units = []
        for e in range(E):
            down_units += [(e, [(slice(0, P), e, r * P)]) for r in range(RT1 - 1)]
            if e % 2:
                down_units.append((e, [(slice(0, P // 2), e - 1, (RT1 - 1) * P), (slice(P // 2, P), e, (RT1 - 1) * P)]))

        def last_down(e):
            return max(j for j, (_, parts) in enumerate(down_units) if e in [p[1] for p in parts])

        def stores_before(j):
            return sum(len(parts) for _, parts in down_units[j % 3:j:3])

        block = ctx.enter_context(nc.Block())

        @block.tensor
        def _(pe):
            def transposes(g):
                pe.wait_ge(ln_applied, ln_at[g] + 1)
                for k in range(KC):
                    bank = ring.take(pe, ("xT", g, k))
                    for t in range(TB):
                        last = pe.transpose(bank[:, t * P:(t + 1) * P], xn[:, g % 2, t, k * P:(k + 1) * P], ident[:, :])
                    last.then_inc(unit_done, 1)

            def projections(g):
                project_keys(g)
                project_rows(g)

            def project_keys(g):
                for k in range(KC):
                    ring.wait_evacuated(pe, ("xT", g, k))
                for p in range(NPAIR):
                    bank = ring.take(pe, ("kT", g, p))
                    for k in range(KC):
                        last = pe.matmul(bank, wkv[:, k, p * P:(p + 1) * P], xnT[:, g % 2, k, :],
                                         start=(k == 0), stop=(k == KC - 1))
                    last.then_inc(unit_done, 1)

            def project_rows(g):
                if g % 3 == 0:
                    for i in range(2):
                        token_major(("q", g, i), g, i, wq[:, :, :])
                for i in range(2):
                    token_major(("v", g, i), g, i, wkv[:, :, D:2 * D])

            def token_major(key, g, i, w):
                bank = ring.take(pe, key)
                for t in range(2):
                    for k in range(KC):
                        last = pe.matmul(bank[:, t * D:(t + 1) * D],
                                         xnT[:, g % 2, k, (2 * i + t) * P:(2 * i + t + 1) * P], w[:, k, :],
                                         start=(k == 0), stop=(k == KC - 1))
                last.then_inc(unit_done, 1)

            def key_squares(g):
                bank = ring.take(pe, ("ss", g))
                for p in range(NPAIR):
                    pe.wait_ge(khi_ready, g * NPAIR + p + 1)
                    for t in range(TB):
                        c = (t * NPAIR + p) * 2
                        last = pe.matmul(bank[:, c:c + 2], ksq[:, p, t * P:(t + 1) * P], headsel[:, :],
                                         start=True, stop=True)
                last.then_inc(unit_done, 1)

            def query_transposes(b):
                pe.wait_ge(qdup_ready, 2 * (b + 1))
                for h in range(H0):
                    bank = ring.take(pe, ("qT", b, h))
                    for t in range(TB):
                        last = pe.transpose(bank[:, t * P:(t + 1) * P],
                                            qdup[:, t * H0 + h, :, :].rearrange("p a d -> p (a d)"), ident[:, :])
                    last.then_inc(unit_done, 1)

            def scores(b, p, j):
                for h in range(2):
                    hh = 2 * p + h
                    bank = ring.take(pe, ("s", b, p, j, h))
                    pe.matmul(bank, kstack[:, hh, j * P:(j + 1) * P], qhi[:, hh, :], start=True, stop=False)
                    pe.matmul(bank, kstack[:, hh, j * P:(j + 1) * P], qlo[:, hh, :],
                              start=False, stop=True).then_inc(unit_done, 1)

            def weigh(b, p, j):
                n, m = step(b, p, j), b * NPAIR + p
                if j == 0 and m >= 2:
                    pe.wait_ge(attn_evacuated, m - 1)
                for h in range(2):
                    ring.wait_evacuated(pe, ("s", b, p, j, h))
                    last = pe.matmul(acc_psum[h * DH0:(h + 1) * DH0, m % 2, :],
                                     vals[:, j, (2 * p + h) * DH0:(2 * p + h + 1) * DH0], probs[:, n % 3, h, :],
                                     start=(j == 0), stop=(j == KT0 - 1), skip_group_check=True)
                last.then_inc(pv_done, 1)

            def denominators(b, p):
                m = b * NPAIR + p
                pe.wait_ge(psums_added, KT0 * (m + 1))
                bank = ring.take(pe, ("den", b, p))
                for h in range(2):
                    last = pe.matmul(bank[h * DH0:(h + 1) * DH0, :], ones[:, 0:DH0], psums[:, m % 2, h * S:(h + 1) * S],
                                     start=True, stop=True, skip_group_check=True)
                last.then_inc(unit_done, 1)

            def out_projection(b):
                for i in range(2):
                    bank = ring.take(pe, ("wo", b, i))
                    pe.wait_ge(attn_evacuated, NPAIR * (b + 1))
                    for t in range(2):
                        for p in range(NPAIR):
                            last = pe.matmul(bank[:, t * D:(t + 1) * D], attnT[:, p, (2 * i + t) * P:(2 * i + t + 1) * P],
                                             wout[:, p, :], start=(p == 0), stop=(p == NPAIR - 1))
                    last.then_inc(unit_done, 1)

            def expert_norm_transposes(b):
                pe.wait_ge(ln_applied, ln_at["h", b] + 1)
                for k in range(KC):
                    bank = ring.take(pe, ("hT", b, k))
                    for t in range(TB):
                        last = pe.transpose(bank[:, t * P:(t + 1) * P], hn[:, 0, t, k * P:(k + 1) * P], ident[:, :])
                    last.then_inc(unit_done, 1)

            def router(b):
                for k in range(KC):
                    ring.wait_evacuated(pe, ("hT", b, k))
                bank = ring.take(pe, ("gate", b))
                for t in range(TB):
                    for k in range(KC):
                        last = pe.matmul(bank[:, t * E:(t + 1) * E], hT[:, k, (TB * b + t) * P:(TB * b + t + 1) * P],
                                         gate_w[:, k, :], start=(k == 0), stop=(k == KC - 1))
                last.then_inc(unit_done, 1)

            def ranks(b):
                pe.wait_ge(picks_ready, b + 1)
                bank = ring.take(pe, ("rank", b))
                n = TB * E
                pe.matmul(bank[:, 0:n], before[:, :], chosen[:, TB * b:TB * b + TB, :].rearrange("p t e -> p (t e)"),
                          start=True, stop=False)
                last = pe.matmul(bank[:, 0:n], ones16[:, :],
                                 earlier[:, TB * b:TB * b + TB, :].rearrange("p t e -> p (t e)"), start=False, stop=True)
                if b == B - 1:
                    last = pe.matmul(bank[:, n:n + E], ones16[:, :], earlier[:, NT, :], start=True, stop=True)
                last.then_inc(unit_done, 1)

            pe.wait_ge(consts_made, 1)
            transposes(0)
            pe.wait_ge(wa_loaded, 48)
            for b in range(B):
                g = 3 * b
                if b == 0:
                    project_keys(g)
                project_rows(g)
                if b == 0:
                    transposes(g + 1)
                transposes(g + 2)
                key_squares(g)
                projections(g + 1)
                query_transposes(b)
                key_squares(g + 1)
                projections(g + 2)
                if b + 1 < B:
                    transposes(g + 3)
                key_squares(g + 2)
                for p in range(NPAIR):
                    for j in range(KT0):
                        scores(b, p, j)
                        if j >= 2:
                            weigh(b, p, j - 2)
                        if j == 6 and p == 0 and b:
                            if b == 1:
                                pe.wait_ge(wb_loaded, 48)
                            expert_norm_transposes(b - 1)
                        if j == 8 and p == 0 and b:
                            router(b - 1)
                        if j == 3 and p == 1:
                            denominators(b, 0)
                        if j == 10 and p == 1 and b:
                            ranks(b - 1)
                    weigh(b, p, KT0 - 2)
                    weigh(b, p, KT0 - 1)
                denominators(b, 1)
                if b + 1 < B:
                    transposes(g + 4)
                    project_keys(g + 3)
                out_projection(b)
            ring.grow()
            expert_norm_transposes(B - 1)
            router(B - 1)

            def shared_up(t):
                bank = ring.take(pe, ("sgu", t))
                for k in range(KC):
                    last = pe.matmul(bank[:, 0:2 * M0], hT[:, k, t * P:(t + 1) * P], sh_gu[:, k, :],
                                     start=(k == 0), stop=(k == KC - 1))
                last.then_inc(unit_done, 1)

            def shared_turn(t):
                pe.wait_ge(shared_mid, t + 1)
                bank = ring.take(pe, ("smT", t))
                pe.transpose(bank[:, 0:P], mid[:, t % 2, :], ident[:, :]).then_inc(unit_done, 1)

            def shared_down(t):
                ring.wait_evacuated(pe, ("smT", t))
                bank = ring.take(pe, ("sy", t))
                pe.matmul(bank[:, 0:D], midT[:, t % 2, :], sh_dn[:, :], start=True, stop=True).then_inc(unit_done, 1)

            for i in range(NT + 2):
                if i < NT:
                    shared_up(i)
                if i == 5:
                    ranks(B - 1)
                if 1 <= i <= NT:
                    shared_turn(i - 1)
                if i >= 2:
                    shared_down(i - 2)

            def slot_sources(key, n):
                bank = ring.take(pe, key)
                for t in range(NT):
                    for k in range(2):
                        last = pe.matmul(bank[:, 0:n], rowhot[:, t, k, :], tilehot[:, t, k, 0:n],
                                         start=(t == 0 and k == 0), stop=(t == NT - 1 and k == 1))
                last.then_inc(unit_done, 1)

            pe.wait_ge(rowhot_ready, B)
            pe.wait_ge(tilehot_ready, 1)
            slot_sources(("source", 0), NSLOT0)

            expert = {}

            def slot_turn(s):
                pe.wait_ge(gathered[s % NXG], 16 * (s // NXG + 1))
                bank = ring.take(pe, ("xgT", s))
                for k in range(KC):
                    last = pe.transpose(bank[:, k * P:(k + 1) * P], xg[:, s % NXG, k * P:(k + 1) * P], ident[:, :])
                last.then_inc(unit_done, 1)
                expert[s] = pe.value_load(eslot_i[0:1, s:s + 1], min_val=0, max_val=E - 1)

            def slot_up(s):
                ring.wait_evacuated(pe, ("xgT", s))
                bank = ring.take(pe, ("gu", s))
                for k in range(KC):
                    last = pe.matmul(bank[:, 0:2 * M0], xgT[:, s % 3, k * P:(k + 1) * P],
                                     e_gu[:, k, bass.ds(expert[s], 1), :], start=(k == 0), stop=(k == KC - 1))
                last.then_inc(unit_done, 1)

            def slot_mid_turn(s):
                ring.wait_evacuated(pe, ("gu", s))
                bank = ring.take(pe, ("mT", s))
                pe.transpose(bank[:, 0:P], mid[:, s % 2, :], ident[:, :]).then_inc(unit_done, 1)

            def slot_down(s):
                ring.wait_evacuated(pe, ("mT", s))
                bank = ring.take(pe, ("y", s))
                pe.matmul(bank[:, 0:D], midT[:, s % 2, :], e_dn[:, bass.ds(expert[s], 1), :],
                          start=True, stop=True).then_inc(unit_done, 1)

            pe.wait_ge(eslot_ready, 1)
            pe.wait_ge(e_loaded, 32)
            for i in range(NSLOT0 + 3):
                if i < NSLOT0:
                    slot_turn(i)
                if 1 <= i <= NSLOT0:
                    slot_up(i - 1)
                if 2 <= i <= NSLOT0 + 1:
                    slot_mid_turn(i - 2)
                if i >= 3:
                    slot_down(i - 3)

            def turn_tokens(key, ln_key, src):
                pe.wait_ge(ln_applied, ln_at[ln_key] + 1)
                for k in range(KC):
                    bank = ring.take(pe, key + (k,))
                    for s in range(B):
                        last = pe.transpose(bank[:, s * P:(s + 1) * P], src[:, s, k * P:(k + 1) * P], ident[:, :])
                    last.then_inc(unit_done, 1)

            def context_scores(n):
                c, s = divmod(n, B)
                if s == 0:
                    for k in range(KC):
                        ring.wait_evacuated(pe, ("uT", c, k))
                for half in range(2):
                    bank = ring.take(pe, ("cs", n, half))
                    for k in range(KC):
                        last = pe.matmul(bank, uT[:, k, s * P:(s + 1) * P], ctx_t[:, k, s, half * 512:(half + 1) * 512],
                                         start=(k == 0), stop=(k == KC - 1))
                    last.then_inc(unit_done, 1)

            def context_turn(n):
                for half in range(2):
                    ring.wait_evacuated(pe, ("cs", n, half))
                for half in range(2):
                    bank = ring.take(pe, ("cp", n, half))
                    for t in range(4):
                        o = half * 512 + t * P
                        last = pe.transpose(bank[:, t * P:(t + 1) * P], cprob[:, n % 2, o:o + P], ident[:, :])
                    last.then_inc(unit_done, 1)

            def context_values(n):
                for half in range(2):
                    ring.wait_evacuated(pe, ("cp", n, half))
                bank = ring.take(pe, ("co", n))
                for t in range(CTB):
                    last = pe.matmul(bank[:, 0:D], cprobT[:, n % 2, t * P:(t + 1) * P], ctx_n[:, n % B, t, :],
                                     start=(t == 0), stop=(t == CTB - 1))
                last.then_inc(unit_done, 1)

            def project_qkv(c):
                for k in range(KC):
                    ring.wait_evacuated(pe, ("dT", c, k))
                for s in range(B):
                    bank = ring.take(pe, ("qkv", c, s))
                    for k in range(KC):
                        last = pe.matmul(bank[:, 0:QKV], dT[:, k, s * P:(s + 1) * P], qkv_w[:, k, :],
                                         start=(k == 0), stop=(k == KC - 1))
                    last.then_inc(unit_done, 1)

            def turn_attention(c):
                wait_values(pe, c)
                for k in range(KC):
                    bank = ring.take(pe, ("oT", c, k))
                    for s in range(B):
                        last = pe.transpose(bank[:, s * P:(s + 1) * P], att_o[:, s, k * P:(k + 1) * P], ident[:, :])
                    last.then_inc(unit_done, 1)

            def project_out(c):
                for k in range(KC):
                    ring.wait_evacuated(pe, ("oT", c, k))
                for i in range(2):
                    bank = ring.take(pe, ("po", c, i))
                    for t in range(2):
                        for k in range(KC):
                            last = pe.matmul(bank[:, t * D:(t + 1) * D], dT[:, k, (2 * i + t) * P:(2 * i + t + 1) * P],
                                             proj_w[:, k, :], start=(k == 0), stop=(k == KC - 1))
                    last.then_inc(unit_done, 1)

            def router2(c):
                for k in range(KC):
                    ring.wait_evacuated(pe, ("lT", c, k))
                bank = ring.take(pe, ("rt", c))
                for s in range(B):
                    for k in range(KC):
                        last = pe.matmul(bank[:, s * E:(s + 1) * E], lT[:, k, s * P:(s + 1) * P], router_w[:, k, :],
                                         start=(k == 0), stop=(k == KC - 1))
                last.then_inc(unit_done, 1)

            turn_tokens(("uT", 0), ("c", 0), un)
            pe.wait_ge(ctx_t_loaded, 16 * KC * B)
            pe.wait_ge(ctx_n_loaded, 16 * 2 * B)
            pe.wait_ge(wd_loaded, 48)
            for i in range(NSTEP):
                c, phase = divmod(i, B)
                if i < NT:
                    context_scores(i)
                if phase == 3 and 0 <= c - 2 < TB:
                    project_out(c - 2)
                if 1 <= i <= NT:
                    context_turn(i - 1)
                if 2 <= i <= NT + 1:
                    context_values(i - 2)
                if phase == 2 and 0 <= c - 2 < TB:
                    turn_attention(c - 2)
                if phase == 3 and c + 1 < TB:
                    turn_tokens(("uT", c + 1), ("c", c + 1), un)
                if phase == 3 and 0 <= c - 1 < TB:
                    turn_tokens(("dT", c - 1), ("d", c - 1), dn)
                if phase == 0 and 0 <= c - 2 < TB:
                    project_qkv(c - 2)
                if phase == 0 and 0 <= c - 3 < TB:
                    turn_tokens(("lT", c - 3), ("l", c - 3), l_n)
                if phase == 1 and 0 <= c - 3 < TB:
                    router2(c - 3)

            pe.wait_ge(picks2_ready, 1)
            bank = ring.take(pe, ("rank2", 0))
            pe.matmul(bank[:, 0:NT * E], before[:, :], chosen[:, :, :].rearrange("p t e -> p (t e)"), start=True, stop=False)
            pe.matmul(bank[:, 0:NT * E], ones16[:, :], earlier[:, 0:NT, :].rearrange("p t e -> p (t e)"),
                      start=False, stop=True).then_inc(unit_done, 1)
            pe.wait_ge(hots2_ready, 1)
            slot_sources(("source", 1), NSLOT1)

            def expert_turn(e):
                for k in range(KC):
                    bank = ring.take(pe, ("eT", e, k))
                    for r in range(RT1):
                        s, n = e * RT1 + r, min(P, CAP1 - r * P)
                        if k == 0:
                            pe.wait_ge(gathered2[s % NXG], 16 * (s // NXG + 1))
                        last = pe.transpose(bank[:, r * P:r * P + n], xg2[0:n, s % NXG, k * P:(k + 1) * P], ident[0:n, 0:n])
                    last.then_inc(unit_done, 1)

            def expert_up(e):
                for k in range(KC):
                    ring.wait_evacuated(pe, ("eT", e, k))
                pe.wait_ge(w_loaded[e % NW], 32 * (e // NW + 1))
                for f in range(FC1):
                    bank = ring.take(pe, ("h1", e, f))
                    for k in range(KC):
                        last = pe.matmul(bank[:, 0:CAP1], w1[:, e % NW, k, f * P:(f + 1) * P], eT[:, e % 2, k, :],
                                         start=(k == 0), stop=(k == KC - 1))
                    last.then_inc(unit_done, 1)

            def expert_down(e):
                for f in range(FC1):
                    ring.wait_evacuated(pe, ("h1", e, f))
                for j, (at_expert, parts) in enumerate(down_units):
                    if at_expert != e:
                        continue
                    bank = ring.take(pe, ("h2", j))
                    for f in range(FC1):
                        for on, ex, row0 in parts:
                            last = pe.matmul(bank[on, 0:D], h1[:, ex % 2, f, row0:row0 + on.stop - on.start], w2[:, ex % NW, f, :],
                                             start=(f == 0), stop=(f == FC1 - 1), skip_group_check=True)
                    last.then_inc(unit_done, 1)

            expert_turn(0)
            for e in range(E):
                expert_up(e)
                if e + 1 < E:
                    expert_turn(e + 1)
                expert_down(e)

        @block.sync
        def _(sp):
            for b in range(B):
                sp.dma_start(x[:, TB * b:TB * b + TB, :], a["x"][b].rearrange("(t p) d -> p t d", p=P)).then_inc(x_loaded[b], 16)
                if b == 0:
                    sp.dma_start(cols[:, :], a["cols"]).then_inc(small_loaded, 16)
                    sp.dma_start(rows[:, :], a["rows"]).then_inc(small_loaded, 16)
                    sp.dma_start(mask8[:, :], a["mask"]).then_inc(small_loaded, 16)

            def load_ctx(c):
                if c >= 2:
                    g = (c - 2) // 2 * 3 + (c - 2) % 2 + 1
                    sp.wait_ge(ln_applied, ln_at[g] + 1)
                sp.dma_start(ctx_in[:, c % 2, :, :],
                             a["ctx"][c // 2, (c % 2) * S:(c % 2 + 1) * S, :].rearrange("(t p) d -> p t d", p=P)).then_inc(ctx_loaded[c % 2], 16)

            def store_normalized(b):
                sp.wait_ge(ln_applied, ln_at["h", b] + 1)
                sp.dma_start(h_rows[b * S:(b + 1) * S, :].rearrange("(t p) d -> p t d", p=P), hn[:, 0, :, :]).then_inc(hn_stored, 16)

            load_ctx(0)
            load_ctx(1)
            sp.dma_start(gate_w[:, :, :], a["gate_w"]).then_inc(wb_loaded, 16)
            sp.dma_start(sh_gu[:, :, :], a["sh_gu"]).then_inc(wb_loaded, 16)
            sp.dma_start(sh_dn[:, :], a["sh_dn"]).then_inc(wb_loaded, 16)
            sp.dma_start(qkv_w[:, :, :], a["qkv_w"]).then_inc(wd_loaded, 16)
            sp.dma_start(proj_w[:, :, :], a["proj_w"]).then_inc(wd_loaded, 16)
            sp.dma_start(router_w[:, :, :], a["router_w"]).then_inc(wd_loaded, 16)
            for b in range(B):
                if b + 1 < B:
                    load_ctx(2 * b + 2)
                    load_ctx(2 * b + 3)
                if b:
                    store_normalized(b - 1)
            store_normalized(B - 1)
            ring.wait_done(sp, ("wo", B - 1, 1))
            sp.dma_start(e_gu[:, :, :, :], a["e_gu"]).then_inc(e_loaded, 16)
            sp.dma_start(e_dn[:, :, :], a["e_dn"]).then_inc(e_loaded, 16)
            for s in range(NSLOT0):
                ring.wait_evacuated(sp, ("y", s))
                sp.dma_start(y_rows[s * P:(s + 1) * P, :], ysb[:, s % 3, :]).then_inc(y_stored[s % 3], 16)
                if s % 2 == 0 and s // 2 < KC * B:
                    b, k = divmod(s // 2, KC)
                    sp.dma_start(ctx_t[:, k, b, :], a["ctxT"][:, k, b, :]).then_inc(ctx_t_loaded, 16)
                elif s % 2 == 0 and s // 2 < KC * B + 2 * B:
                    b, half = divmod(s // 2 - KC * B, 2)
                    sp.dma_start(ctx_n[:, b, half * 4:half * 4 + 4, :],
                                 a["ctx"][b, half * 512:half * 512 + 512, :].rearrange("(t p) d -> p t d", p=P)).then_inc(ctx_n_loaded, 16)

            def load_expert(e):
                if e == 0:
                    ring.wait_done(sp, ("co", NT - 1))
                if e >= NW:
                    ring.wait_done(sp, ("h2", last_down(e - NW)))
                sp.dma_start(w1[:, e % NW, :, :], a["w1"][e]).then_inc(w_loaded[e % NW], 16)
                sp.dma_start(w2[:, e % NW, :, :], a["w2"][e]).then_inc(w_loaded[e % NW], 16)

            for c in range(TB):
                if c == TB - 1:
                    for e in range(NW):
                        load_expert(e)
                sp.wait_ge(ln_applied, ln_at["l", c] + 1)
                sp.dma_start(l_rows.rearrange("(s c p) d -> p s c d", s=B, c=TB)[:, :, c, :], l_n[:, :, :]).then_inc(l_stored, 16)
            loaded = NW
            for j, (e, parts) in enumerate(down_units):
                ring.wait_evacuated(sp, ("h2", j))
                for on, ex, row0 in parts:
                    n = on.stop - on.start
                    sp.dma_start(y2_rows[ex * CAP1 + row0:ex * CAP1 + row0 + n, :], y2[on, j % 3, :]).then_inc(y2_stored[j % 3], 16)
                while loaded < E and last_down(loaded - NW) <= j:
                    load_expert(loaded)
                    loaded += 1
            for t in range(NT):
                sp.wait_ge(finished, t + 1)
                sp.dma_start(out[t // TB, t % TB * P:(t % TB + 1) * P, :], x[:, t, :]).then_inc(out_stored, 16)
            sp.wait_ge(out_stored, 16 * NT)

        @block.gpsimd
        def _(pool):
            count = [0]

            def link(ins):
                count[0] += 1
                ins.then_inc(pool_step, 1)
                pool.wait_ge(pool_step, count[0])

            link(pool.memset(ident[:, :], 0.0))
            link(pool.affine_select(out=ident[:, :], in_=ident[:, :], compare_op=ALU.not_equal, fill=1.0, base=0,
                                    pattern=[[-1, P]], channel_multiplier=1))
            pool.memset(ones[:, :], 1.0)
            pool.memset(ones16[:, :], 1.0)
            pool.memset(zero16[:, :], 0.0)
            pool.memset(earlier[:, 0, :], 0.0)
            link(pool.memset(headsel[:, :], 1.0))
            link(pool.affine_select(out=headsel[:, 0:1], in_=headsel[:, 0:1], compare_op=ALU.is_gt, fill=0.0, base=DH0,
                                    pattern=[[0, 1]], channel_multiplier=-1))
            link(pool.affine_select(out=headsel[:, 1:2], in_=headsel[:, 1:2], compare_op=ALU.is_ge, fill=0.0, base=-DH0,
                                    pattern=[[0, 1]], channel_multiplier=1))
            link(pool.affine_select(out=before[:, :], in_=ones16[:, :], compare_op=ALU.is_gt, fill=0.0, base=0,
                                    pattern=[[1, P]], channel_multiplier=-1))
            pool.iota(iota[:, :], pattern=[[1, P]], base=0, channel_multiplier=0, allow_small_or_imprecise_dtypes=True)
            pool.iota(iota16[:, :], pattern=[[1, P]], base=0, channel_multiplier=0, allow_small_or_imprecise_dtypes=True)
            pool.iota(token16[:, :, :], pattern=[[P, NT], [0, 2]], base=0, channel_multiplier=1, allow_small_or_imprecise_dtypes=True)
            pool.iota(thresholds[:, :], pattern=[[P, E]], base=0, channel_multiplier=0, allow_small_or_imprecise_dtypes=True).then_inc(consts_made, 1)

            def add_bias(b):
                pool.wait_ge(ln_applied, ln_at[3 * b] + 1)
                pool.wait_ge(small_loaded, 48)
                xs = x[:, TB * b:TB * b + TB, :]
                pool.tensor_tensor(xs, xs, bc(row("b_out"), 1, TB), ALU.add).then_inc(bias_added, 1)

            def queries_twice(b):
                pool.wait_ge(rq_ready, b + 1)
                if b:
                    ring.wait_done(pool, ("qT", b - 1, H0 - 1))
                pool.tensor_tensor(qdup[:, :, 1, :], qn[:, :, :].rearrange("p t (h e) -> p (t h) e", h=H0),
                                   bc(rq[:, :], 2, DH0), ALU.mult).then_inc(qdup_ready, 1)

            def row_onehots(b):
                pool.wait_ge(rrow_ready, b + 1)
                for t in range(TB * b, TB * b + TB):
                    for k in range(2):
                        last = pool.tensor_scalar(rowhot[:, t, k, :], iota[:, :], rrow[:, t, k:k + 1], None, ALU.is_equal)
                last.then_inc(rowhot_ready, 1)

            add_bias(0)
            for b in range(B):
                queries_twice(b)
                if b + 1 < B:
                    add_bias(b + 1)
                if b:
                    row_onehots(b - 1)
            for t in range(NT):
                ring.wait_evacuated(pool, ("sgu", t))
                if t == 0:
                    ring.wait_done(pool, ("wo", B - 1, 1))
                if t >= 2:
                    ring.wait_done(pool, ("smT", t - 2))
                pool.tensor_tensor(mid[:, t % 2, :], silu[:, t % 2, :], up[:, t % 2, :], ALU.mult).then_inc(shared_mid, 1)
                if t >= 2:
                    add_shared(pool, t - 2)
            for t in (NT - 2, NT - 1):
                add_shared(pool, t)
            pool.wait_ge(slots_ready, 1)
            pool.wait_ge(hn_stored, 16 * B)
            for s in range(NSLOT0):
                if s >= NXG:
                    ring.wait_done(pool, ("xgT", s - NXG))
                pool.indirect_dma_start(xg[:, s % NXG, :], None, h_rows,
                                        bass.IndirectOffsetOnAxis(ap=source[:, s:s + 1], axis=0)).then_inc(gathered[s % NXG], 16)
            for i in range(3):
                pool.wait_ge(y_stored[i], 16 * len(range(i, NSLOT0, 3)))

            def gather_results(n):
                if n >= NYG + B:
                    pool.wait_ge(combined_later, n - NYG - B + 1)
                elif n >= NYG:
                    pool.wait_ge(combined, n - NYG + 1)
                for k in range(2):
                    pool.indirect_dma_start(yg[:, n % NYG, k, :], None, y_rows,
                                            bass.IndirectOffsetOnAxis(ap=slot_u[:, tile_of(n), k:k + 1], axis=0)).then_inc(y_gathered[n % NYG], 16)

            for n in range(B):
                gather_results(n)
            def add_hidden(c):
                pool.wait_ge(ln_applied, ln_at["l", c] + 1)
                pool.tensor_tensor(x[:, c:NT:TB, :], x[:, c:NT:TB, :], hid[:, c % 2, :, :], ALU.add).then_inc(x3_done, 1)

            for n in range(B, NT + 2):
                if n < NT:
                    gather_results(n)
                if n >= B + 2:
                    combine(pool, link, n - 2)
            for c in range(TB):
                attend_values(pool, link, c, VALUES_POOL[c], value_prod, att_done_pool)
                add_hidden(c)
            pool.wait_ge(slots2_ready, 1)
            pool.wait_ge(l_stored, 16 * TB)
            for s in range(NSLOT1):
                if s >= NXG:
                    ring.wait_done(pool, ("eT", (s - NXG) // RT1, KC - 1))
                n = min(P, CAP1 - s % RT1 * P)
                pool.indirect_dma_start(xg2[0:n, s % NXG, :], None, l_rows,
                                        bass.IndirectOffsetOnAxis(ap=source[0:n, s:s + 1], axis=0)).then_inc(gathered2[s % NXG], 16)
            for i in range(3):
                pool.wait_ge(y2_stored[i], 16 * sum(len(parts) for _, parts in down_units[i::3]))
            for t in range(NT):
                if t >= NYG:
                    pool.wait_ge(finished, t - NYG + 1)
                else:
                    pool.wait_ge(combined_later, NT - B)
                for k in range(2):
                    pool.indirect_dma_start(yg[:, t % NYG, k, :], None, y2_rows,
                                            bass.IndirectOffsetOnAxis(ap=slot_u[:, t, k:k + 1], axis=0)).then_inc(y2_gathered[t % NYG], 16)

        @block.scalar
        def _(act):
            act.dma_start(wkv[:, :, :], a["wkv"]).then_inc(wa_loaded, 16)
            act.dma_start(wq[:, :, :], a["wq"]).then_inc(wa_loaded, 16)
            act.dma_start(wout[:, :, :], a["wout"]).then_inc(wa_loaded, 16)
            act.wait_ge(small_loaded, 48)

            def evac_turned(g):
                ring.wait_done(act, ("xT", g, 1))
                n = "ln_l" if g % 3 == 0 else "ln_x"
                if g >= 2:
                    ring.wait_done(act, ("v", g - 2, 1))
                act.activation(xnT[:, g % 2, 1, :], ring.bank(("xT", g, 1)), ACT.Identity, bias=col(n + "_b1"),
                               scale=col(n + "_g1")).then_inc(ring.evacuated(("xT", g, 1)), 1)

            def keys(g):
                b, gg = divmod(g, 3)
                for p in range(NPAIR):
                    bank = ring.bank(("kT", g, p))
                    ring.wait_done(act, ("kT", g, p))
                    if g:
                        ring.wait_done(act, ("ss", g - 1))
                    if gg == 0 and b:
                        ring.wait_done(act, ("s", b - 1, NPAIR - 1, KT0 - 1, 1))
                    act.activation(ksq[:, p, :], bank, ACT.Square)
                    span = slice(gg * S, (gg + 1) * S)
                    act.activation(kstack[0:DH0, 2 * p, span], bank[0:DH0, :], ACT.Copy)
                    act.activation(kstack[DH0:P, 2 * p + 1, span], bank[DH0:P, :], ACT.Copy).then_inc(khi_ready, 1)

            def copies(key, dst):
                ring.wait_done(act, key)
                act.activation(dst, ring.bank(key), ACT.Copy).then_inc(ring.evacuated(key), 1)

            def copies_part(key, dst, n):
                ring.wait_done(act, key)
                act.activation(dst, ring.bank(key)[:, 0:n], ACT.Copy).then_inc(ring.evacuated(key), 1)

            def values(g):
                b, gg = divmod(g, 3)
                if gg == 0 and b:
                    act.wait_ge(pv_done, step(b, 0, 0))
                for i in range(2):
                    copies(("v", g, i), vals[:, gg * TB + 2 * i:gg * TB + 2 * i + 2, :].rearrange("p t d -> p (t d)"))

            def queries(b):
                if b:
                    act.wait_ge(qdup_ready, 2 * b)
                for i in range(2):
                    copies(("q", 3 * b, i), qn[:, 2 * i:2 * i + 2, :].rearrange("p t d -> p (t d)"))

            def query_high(b):
                if b:
                    ring.wait_done(act, ("s", b - 1, NPAIR - 1, KT0 - 1, 1))
                for h in range(H0):
                    ring.wait_done(act, ("qT", b, h))
                    act.activation(qhi[:, h, :], ring.bank(("qT", b, h)), ACT.Copy, scale=gqk[:, :]).then_inc(qhi_ready, 1)

            def exps(b, p, j):
                n = step(b, p, j)
                if n >= 3:
                    act.wait_ge(pv_done, n - 2)
                    act.wait_ge(psums_added, n - 2)
                if p == 0 and j % TB == 0:
                    act.wait_ge(rkey_ready, 3 * b + j // TB + 1)
                for h in range(2):
                    key = ("s", b, p, j, h)
                    ring.wait_done(act, key)
                    act.activation(probs[:, n % 3, h, :], ring.bank(key), ACT.Exp,
                                   bias=lbias[:, :] if j < TB else mbias[:, b, j - TB:j - TB + 1],
                                   scale=rkey[:, b % 2, j, 2 * p + h:2 * p + h + 1]).then_inc(ring.evacuated(key), 1)

            def expert_norm_turned(b):
                for k in range(KC):
                    copies(("hT", b, k), hT[:, k, b * S:(b + 1) * S])

            def router_exp(b):
                key = ("gate", b)
                ring.wait_done(act, key)
                if b:
                    act.wait_ge(picks_ready, b)
                act.activation(rexp[:, :], ring.bank(key)[:, 0:TB * E], ACT.Exp, scale=-1.0).then_inc(ring.evacuated(key), 1)

            evac_turned(0)
            for b in range(B):
                g = 3 * b
                if b == 0:
                    keys(g)
                queries(b)
                values(g)
                if b == 0:
                    evac_turned(g + 1)
                    act.wait_ge(exp_consts_ready, 1)
                evac_turned(g + 2)
                keys(g + 1)
                values(g + 1)
                query_high(b)
                keys(g + 2)
                values(g + 2)
                if b + 1 < B:
                    evac_turned(g + 3)
                for p in range(NPAIR):
                    for j in range(KT0):
                        exps(b, p, j)
                        if j == 6 and p == 0 and b:
                            expert_norm_turned(b - 1)
                        if j == 8 and p == 0 and b:
                            router_exp(b - 1)
                if b + 1 < B:
                    evac_turned(g + 4)
                    keys(g + 3)
            expert_norm_turned(B - 1)
            router_exp(B - 1)

            for i in range(NT + 2):
                if i < NT:
                    key = ("sgu", i)
                    ring.wait_done(act, key)
                    if i >= 2:
                        act.wait_ge(shared_mid, i - 1)
                    act.activation(up[:, i % 2, :], ring.bank(key)[:, M0:2 * M0], ACT.Copy)
                    act.activation(silu[:, i % 2, :], ring.bank(key)[:, 0:M0], ACT.Silu).then_inc(ring.evacuated(key), 1)
                if 1 <= i <= NT:
                    t = i - 1
                    if t >= 2:
                        ring.wait_done(act, ("sy", t - 2))
                    copies_part(("smT", t), midT[:, t % 2, :], P)
                if i >= 2:
                    t = i - 2
                    if t >= 2:
                        act.wait_ge(shared_added, t - 1)
                    copies_part(("sy", t), ysb[:, t % 2, :], D)
            for i in range(NSLOT0 + 3):
                if 1 <= i <= NSLOT0:
                    s = i - 1
                    key = ("gu", s)
                    ring.wait_done(act, key)
                    if s >= 2:
                        ring.wait_evacuated(act, ("gu", s - 2))
                    act.activation(silu[:, s % 2, :], ring.bank(key)[:, 0:M0], ACT.Silu).then_inc(silu_ready, 1)
                if i >= 3:
                    s = i - 3
                    if s >= 3:
                        act.wait_ge(y_stored[s % 3], 16 * (s // 3))
                    if s == 0:
                        act.wait_ge(shared_added, NT)
                    copies_part(("y", s), ysb[:, s % 3, :], D)

            for k in range(KC):
                copies(("uT", 0, k), uT[:, k, :])
            for i in range(NSTEP):
                c, phase = divmod(i, B)
                if i < NT:
                    if i >= 2:
                        ring.wait_done(act, ("cp", i - 2, 1))
                        if i >= 3:
                            act.wait_ge(x2_done, i - 2)
                    act.wait_ge(cmax_ready, i + 1)
                    for half in range(2):
                        key = ("cs", i, half)
                        act.activation(cprob[:, i % 2, half * 512:(half + 1) * 512], ring.bank(key), ACT.Exp,
                                       bias=cmax[:, i % 2, 3:4], scale=CSCALE,
                                       accum_out=csum[:, i % 3, half:half + 1]).then_inc(ring.evacuated(key), 1)
                if 1 <= i <= NT:
                    if i >= 3:
                        ring.wait_done(act, ("co", i - 3))
                    for half in range(2):
                        copies(("cp", i - 1, half), cprobT[:, (i - 1) % 2, half * 512:half * 512 + 512])
                if phase == 2 and 0 <= c - 2 < TB:
                    for k in range(KC):
                        copies(("oT", c - 2, k), dT[:, k, :])
                if phase == 3 and c + 1 < TB:
                    for k in range(KC):
                        ring.wait_done(act, ("cs", i, 1))
                        copies(("uT", c + 1, k), uT[:, k, :])
                if phase == 3 and 0 <= c - 1 < TB:
                    for k in range(KC):
                        key = ("dT", c - 1, k)
                        if c >= 2:
                            ring.wait_done(act, ("po", c - 2, 1))
                        ring.wait_done(act, key)
                        act.activation(dT[:, k, :], ring.bank(key), ACT.Identity, bias=col(f"ln1_b{k}"),
                                       scale=col(f"ln1_w{k}")).then_inc(ring.evacuated(key), 1)
                if phase == 0 and 0 <= c - 2 < TB:
                    if c >= 3:
                        wait_values(act, c - 3)
                    for s in range(B):
                        copies_part(("qkv", c - 2, s), qkv[:, s, :], QKV)
                if phase == 0 and 0 <= c - 3 < TB:
                    for k in range(KC):
                        if c >= 4:
                            ring.wait_done(act, ("rt", c - 4))
                        copies(("lT", c - 3, k), lT[:, k, :])
                if phase == 1 and 0 <= c - 2 < TB:
                    act.wait_ge(att_diff, c - 1)
                    if c >= 3:
                        wait_values(act, c - 3)
                    act.activation(att_e[:, :, :, :].rearrange("p s h k -> p (s h k)"), att_d[:, :, :, :].rearrange("p s h k -> p (s h k)"),
                                   ACT.Exp, scale=DH1 ** -0.5).then_inc(att_exp, 1)
                if phase == 2 and 0 <= c - 3 < TB:
                    act.wait_ge(rl_diff, c - 2)
                    act.activation(rl[:, 1, :, :].rearrange("p s e -> p (s e)"), rl[:, 0, :, :].rearrange("p s e -> p (s e)"),
                                   ACT.Exp).then_inc(rl_exp, 1)

            def expert_turned(e):
                key = ("eT", e, 0)
                if e >= 2:
                    ring.wait_done(act, ("h1", e - 2, FC1 - 1))
                copies_part(key, eT[:, e % 2, 0, :], CAP1)

            expert_turned(0)
            for e in range(E):
                for j in range(FC1):
                    key = ("h1", e, j)
                    if e >= 2:
                        ring.wait_done(act, ("h2", last_down(e - 2)))
                    ring.wait_done(act, key)
                    act.activation(h1[:, e % 2, j, :], ring.bank(key)[:, 0:CAP1], ACT.Gelu_apprx_tanh).then_inc(ring.evacuated(key), 1)
                if e + 1 < E:
                    expert_turned(e + 1)

        @block.vector
        def _(dve):
            count = [0]
            turn = [0]

            def link(ins):
                count[0] += 1
                ins.then_inc(dve_step, 1)
                dve.wait_ge(dve_step, count[0])

            def rsqrt(dst, var, n, scale, floor, add):
                v, t, y = (nwt[:, turn[0], i, 0:n] for i in range(3))
                turn[0] ^= 1
                link(dve.tensor_scalar(v, var, scale, floor, ALU.mult, ALU.add if add else ALU.max))
                link(dve.tensor_scalar(y.bitcast(I32), v.bitcast(I32), -0.5, RSQRT_SEED, ALU.mult, ALU.add))
                for i in range(3):
                    link(dve.tensor_tensor(t, y, y, ALU.mult))
                    link(dve.scalar_tensor_tensor(t, t, -0.5, v, ALU.mult, ALU.mult))
                    last = dve.scalar_tensor_tensor(dst if i == 2 else y, t, 1.5, y, ALU.add, ALU.mult)
                    if i < 2:
                        link(last)
                return last

            def normalize(key):
                i = ln_at[key]
                if isinstance(key, tuple) and key[0] == "l":
                    src = hid[:, key[1] % 2, :, :]
                elif isinstance(key, tuple) and key[0] != "h":
                    src = x[:, key[1]:NT:TB, :]
                elif isinstance(key, tuple):
                    src = x[:, TB * key[1]:TB * key[1] + TB, :]
                elif key % 3 == 0:
                    b = key // 3
                    dve.wait_ge(x_loaded[b], 16)
                    src = x[:, TB * b:TB * b + TB, :]
                else:
                    b, gg = divmod(key, 3)
                    dve.wait_ge(ctx_loaded[gg - 1], 16 * (b + 1))
                    src = ctx_in[:, gg - 1, :, :]
                for t in range(TB):
                    last = dve.bn_stats(st[:, t, :], src[:, t, :])
                link(last)
                for t in range(TB):
                    last = dve.bn_aggr(mv[:, i % 4, t, :], st[:, t, :])
                link(last)
                var, r = mv[:, i % 4, :, 1], rstd[:, i % 4, :]
                if isinstance(key, tuple) and key[0] == "d" or not isinstance(key, tuple) and key % 3 == 0:
                    link(rsqrt(r, var, TB, 1.0, 1e-5, True))
                    t = lnt[:, 0, :]
                    if isinstance(key, tuple):
                        dve.tensor_copy(hid_rstd[:, :], r)
                    link(dve.tensor_tensor(t, r, r, ALU.mult))
                    link(dve.tensor_tensor(t, t, var, ALU.mult))
                    link(rsqrt(lnt[:, 1, :], t, TB, 1.0, 1e-5, True))
                    link(dve.tensor_tensor(r, r, lnt[:, 1, :], ALU.mult))
                else:
                    link(rsqrt(r, var, TB, 1.0, 1e-5, True))
                kind = key[0] if isinstance(key, tuple) else "a"
                if kind == "a":
                    if key >= 2:
                        ring.wait_done(dve, ("xT", key - 2, 1))
                    dst = xn[:, key % 2, :, :]
                elif kind == "h":
                    dst = hn[:, 0, :, :]
                    if key[1]:
                        dve.wait_ge(hn_stored, 16 * key[1])
                        ring.wait_done(dve, ("hT", key[1] - 1, 1))
                else:
                    c = key[1]
                    dst = {"c": un, "d": dn, "l": l_n}[kind]
                    if key == ("c", 0):
                        ring.wait_done(dve, ("y", NSLOT0 - 1))
                    if c:
                        ring.wait_done(dve, ({"c": "uT", "d": "dT", "l": "lT"}[kind], c - 1, KC - 1))
                        if kind == "l":
                            dve.wait_ge(l_stored, 16 * c)
                for t in range(TB):
                    if kind == "l":
                        dve.scalar_tensor_tensor(dst[:, t, :], src[:, t, :], mv[:, i % 4, t, 0:1], row("ln2_w"), ALU.subtract, ALU.mult)
                    else:
                        last = dve.tensor_scalar(dst[:, t, :], src[:, t, :], mv[:, i % 4, t, 0:1], rstd[:, i % 4, t:t + 1],
                                                 ALU.subtract, ALU.mult)
                if kind == "l":
                    turned = dve.tensor_copy(lnt[:, 0, :], lnt[:, 1, :])
                    link(turned)
                    for t in range(TB):
                        last = dve.scalar_tensor_tensor(dst[:, t, :], dst[:, t, :], rstd[:, i % 4, t:t + 1], row("ln2_b"),
                                                        ALU.mult, ALU.add)
                last.then_inc(ln_applied, 1)

            def evac_turned(g):
                key = ("xT", g, 0)
                ring.wait_done(dve, key)
                n = "ln_l" if g % 3 == 0 else "ln_x"
                if g >= 2:
                    ring.wait_done(dve, ("v", g - 2, 1))
                dve.tensor_scalar(xnT[:, g % 2, 0, :], ring.bank(key), col(n + "_g0"), col(n + "_b0"),
                                  ALU.mult, ALU.add).then_inc(ring.evacuated(key), 1)

            def key_low(g):
                gg = g % 3
                span = slice(gg * S, (gg + 1) * S)
                for p in range(NPAIR):
                    bank = ring.bank(("kT", g, p))
                    dve.wait_ge(khi_ready, g * NPAIR + p + 1)
                    dve.tensor_tensor(kstack[DH0:P, 2 * p, span], bank[0:DH0, :],
                                      kstack[0:DH0, 2 * p, span].bitcast(F32), ALU.subtract)
                    dve.tensor_tensor(kstack[0:DH0, 2 * p + 1, span], bank[DH0:P, :],
                                      kstack[DH0:P, 2 * p + 1, span].bitcast(F32),
                                      ALU.subtract).then_inc(ring.evacuated(("kT", g, p)), 1)

            def key_sums(g):
                key = ("ss", g)
                ring.wait_done(dve, key)
                dve.tensor_copy(kss[:, g % 3, :], ring.bank(key)[:, 0:TB * H0]).then_inc(ring.evacuated(key), 1)

            def key_norms(g, n):
                b, gg = divmod(g, 3)
                ring.wait_evacuated(dve, ("ss", g + n - 1))
                dst = rkey[:, b % 2, gg * TB:(gg + n) * TB, :].rearrange("p t h -> p (t h)")
                src = kss[:, gg:gg + n, :].rearrange("p g h -> p (g h)")
                rsqrt(dst, src, n * TB * H0, 1.0 / DH0, 1e-16, False).then_inc(rkey_ready, n)

            def query_norms(b):
                for i in range(2):
                    ring.wait_evacuated(dve, ("q", 3 * b, i))
                link(dve.tensor_tensor(qsq[:, :, :], qn[:, :, :], qn[:, :, :], ALU.mult))
                link(dve.tensor_reduce(ssq[:, :], qsq[:, :, :].rearrange("p t (h e) -> p (t h) e", h=H0), AX.X, ALU.add))
                rsqrt(rq[:, :], ssq[:, :], TB * H0, 1.0 / DH0, 1e-16, False).then_inc(rq_ready, 1)
                dve.wait_ge(rq_ready, b + 1)
                if b:
                    ring.wait_done(dve, ("qT", b - 1, H0 - 1))
                dve.tensor_tensor(qdup[:, :, 0, :], qn[:, :, :].rearrange("p t (h e) -> p (t h) e", h=H0),
                                  bc(rq[:, :], 2, DH0), ALU.mult).then_inc(qdup_ready, 1)

            def query_low(b):
                for h in range(H0):
                    key = ("qT", b, h)
                    dve.wait_ge(qhi_ready, b * H0 + h + 1)
                    dve.scalar_tensor_tensor(qlo[:, h, :], ring.bank(key), gqk[:, 0:1], qhi[:, h, :].bitcast(F32),
                                             ALU.mult, ALU.subtract).then_inc(ring.evacuated(key), 1)

            def add_probs(b, p, j):
                n, m = step(b, p, j), b * NPAIR + p
                for h in range(2):
                    ring.wait_evacuated(dve, ("s", b, p, j, h))
                if j == 0:
                    if m >= 2:
                        ring.wait_done(dve, ("den",) + divmod(m - 2, NPAIR))
                else:
                    dve.wait_ge(psums_added, n)
                src = probs[:, n % 3, :, :].rearrange("p h q -> p (h q)")
                dst = psums[:, m % 2, :]
                if j == 0:
                    dve.tensor_copy(dst, src).then_inc(psums_added, 1)
                else:
                    dve.tensor_tensor(dst, dst, src, ALU.add).then_inc(psums_added, 1)

            def normalize_attention(b, p):
                key, m = ("den", b, p), b * NPAIR + p
                ring.wait_done(dve, key)
                dve.wait_ge(attn_evacuated, m) if m else None
                dve.reciprocal(rden[:, :], ring.bank(key)).then_inc(ring.evacuated(key), 1)
                ring.wait_evacuated(dve, key)
                dve.wait_ge(pv_done, KT0 * (m + 1))
                if b and p == 0:
                    ring.wait_done(dve, ("wo", b - 1, 1))
                dve.tensor_tensor(attnT[:, p, :], acc_psum[:, m % 2, :], rden[:, :], ALU.mult).then_inc(attn_evacuated, 1)

            def add_attention(b):
                dve.wait_ge(bias_added, b + 1)
                for i in range(2):
                    key = ("wo", b, i)
                    ring.wait_done(dve, key)
                    xs = x[:, TB * b + 2 * i:TB * b + 2 * i + 2, :].rearrange("p t d -> p (t d)")
                    dve.tensor_tensor(xs, ring.bank(key), xs, ALU.add).then_inc(ring.evacuated(key), 1)
                for i in range(2):
                    ring.wait_evacuated(dve, ("wo", b, i))

            def choose(b):
                key = ("gate", b)
                ring.wait_evacuated(dve, key)
                flat = score[:, :, :].rearrange("p t e -> p (t e)")
                link(dve.tensor_scalar(flat, rexp[:, :], 1.0, None, ALU.add))
                link(dve.reciprocal(flat, flat))
                for t in range(TB):
                    last = dve.max(top8[:, t, :], score[:, t, :])
                link(last)
                for t in range(TB):
                    last = dve.max_index(idx8[:, t, :], top8[:, t, :], score[:, t, :])
                link(last)
                link(dve.tensor_copy(idxf[:, :, :], idx8[:, :, 0:2]))
                ts = slice(TB * b, TB * b + TB)
                link(dve.tensor_tensor(wtmp[:, :, 0], top8[:, :, 0], top8[:, :, 1], ALU.add))
                link(dve.tensor_scalar(wtmp[:, :, 0], wtmp[:, :, 0], 1e-20, None, ALU.add))
                link(dve.reciprocal(wtmp[:, :, 1], wtmp[:, :, 0]))
                link(dve.scalar_tensor_tensor(weight[:, ts, :], top8[:, :, 0:2], 2.5, bc(wtmp[:, :, 1], 2, 2), ALU.mult, ALU.mult))
                pick_experts(b)

            def pick_experts(b):
                ts = slice(TB * b, TB * b + TB)
                for k in range(2):
                    last = dve.tensor_tensor(pick[:, k, ts, :], bc(iota[:, 0:E], 1, TB), bc(idxf[:, :, k], 2, E), ALU.is_equal)
                link(last)
                link(dve.tensor_tensor(chosen[:, ts, :], pick[:, 0, ts, :], pick[:, 1, ts, :], ALU.add))
                for t in range(TB * b, TB * b + TB):
                    last = dve.tensor_tensor(earlier[:, t + 1, :], earlier[:, t, :], chosen[:, t, :], ALU.add)
                    if t < TB * b + TB - 1:
                        link(last)
                last.then_inc(picks_ready, 1)

            def place_choices(b):
                key = ("rank", b)
                ts = slice(TB * b, TB * b + TB)
                ring.wait_done(dve, key)
                counted = ring.bank(key)[:, 0:TB * E].rearrange("p (t e) -> p t e", e=E)
                for k in range(2):
                    tmp = ptmp[:, k * TB:(k + 1) * TB, :]
                    ins = dve.tensor_tensor(tmp, pick[:, k, ts, :], counted, ALU.mult)
                    if k == 1 and b < B - 1:
                        ins.then_inc(ring.evacuated(key), 1)
                        ring.wait_evacuated(dve, key)
                    else:
                        link(ins)
                    link(dve.tensor_reduce(rank[:, ts, k], tmp, AX.X, ALU.add))
                if b == B - 1:
                    dve.tensor_copy(etiles[:, 0, :], ring.bank(key)[:, TB * E:(TB + 1) * E]).then_inc(ring.evacuated(key), 1)
                link(dve.tensor_copy(rank_i[:, ts, :], rank[:, ts, :]))
                link(dve.tensor_scalar(part_i[:, ts, :], rank_i[:, ts, :], P - 1, None, ALU.bitwise_and))
                link(dve.tensor_copy(rrow[:, ts, :], part_i[:, ts, :]))
                link(dve.tensor_scalar(part_i[:, ts, :], rank_i[:, ts, :], P.bit_length() - 1, None, ALU.arith_shift_right))
                dve.tensor_copy(rtile[:, ts, :], part_i[:, ts, :]).then_inc(rrow_ready, 1)

            dve.wait_ge(small_loaded, 48)
            dve.wait_ge(consts_made, 1)
            normalize(0)
            evac_turned(0)
            normalize(1)
            link(dve.tensor_tensor(gqk[:, :], col("gamma_q"), col("gamma_k"), ALU.mult))
            link(dve.tensor_scalar(gqk[:, :], gqk[:, :], DH0 ** -0.5, None, ALU.mult))
            link(dve.tensor_tensor(gbound[:, 0:DH0], row("gamma_q"), row("gamma_k"), ALU.mult))
            link(dve.tensor_reduce(gbound[:, DH0:DH0 + 1], gbound[:, 0:DH0], AX.X, ALU.max, apply_absolute_value=True))
            link(dve.tensor_scalar(gbound[:, DH0 + 1:DH0 + 2], gbound[:, DH0:DH0 + 1], -(DH0 ** 0.5), 80.0, ALU.mult, ALU.add))
            link(dve.tensor_scalar(lbias[:, :], gbound[:, DH0 + 1:DH0 + 2], 0.0, None, ALU.min))
            flat = mbias[:, :, :].rearrange("p b t -> p (b t)")
            link(dve.tensor_scalar(flat, mask8[:, :].bitcast(U8), BIG, -BIG, ALU.mult, ALU.add))
            dve.tensor_scalar(flat, flat, lbias[:, 0:1], None, ALU.add).then_inc(exp_consts_ready, 1)
            for b in range(B):
                g = 3 * b
                normalize(g + 2)
                if b == 0:
                    key_low(g)
                query_norms(b)
                if b == 0:
                    evac_turned(g + 1)
                evac_turned(g + 2)
                key_sums(g)
                key_low(g + 1)
                query_low(b)
                key_sums(g + 1)
                if b + 1 < B:
                    normalize(g + 3)
                key_low(g + 2)
                key_norms(g, 2)
                if b + 1 < B:
                    evac_turned(g + 3)
                key_sums(g + 2)
                key_norms(g + 2, 1)
                for p in range(NPAIR):
                    for j in range(KT0):
                        add_probs(b, p, j)
                        if j == 1 and p == 0 and b:
                            normalize(("h", b - 1))
                        if j == 10 and p == 0 and b + 1 < B:
                            normalize(g + 4)
                        if j == 4 and p == 1:
                            normalize_attention(b, 0)
                        if j == 7 and p == 1 and b:
                            choose(b - 1)
                        if j == 11 and p == 1 and b:
                            place_choices(b - 1)
                normalize_attention(b, 1)
                if b + 1 < B:
                    evac_turned(g + 4)
                    key_low(g + 3)
                add_attention(b)
            normalize(("h", B - 1))
            choose(B - 1)
            place_choices(B - 1)

            def one_hots(dst, n, places):
                return dve.tensor_tensor(dst.rearrange("p t k j -> p (t k) j"), bc(iota16[:, 0:n], 1, 2 * NT),
                                         bc(places[:, :, :].rearrange("p t k -> p (t k)"), 2, n), ALU.is_equal)

            def tile_onehots(n):
                hot = tilehot[:, :, :, 0:n]
                link(one_hots(hot, n, rtile16))
                return dve.tensor_tensor(hot.rearrange("p t k j -> p (t k) j"), hot.rearrange("p t k j -> p (t k) j"),
                                         bc(token16[:, :, :].rearrange("p t k -> p (t k)"), 2, n), ALU.mult)

            link(dve.tensor_tensor(ecmp[:, 0:E, :], bc(etiles[:, 0, :], 2, E), bc(thresholds[:, :], 1, E), ALU.is_gt))
            link(dve.tensor_reduce(etiles[:, 1, :], ecmp[:, 0:E, :], AX.X, ALU.add))
            link(dve.tensor_tensor_scan(etiles[:, 2, :], etiles[:, 1, :], zero16[:, :], 0.0, ALU.add, ALU.add))
            link(dve.tensor_tensor(etiles[:, 0, :], etiles[:, 2, :], etiles[:, 1, :], ALU.subtract))
            for k in range(2):
                link(dve.tensor_tensor(ptmp[:, :, :], pick[:, k, :, :], bc(etiles[:, 0, :], 1, NT), ALU.mult))
                link(dve.tensor_reduce(dest_f[:, :, k], ptmp[:, :, :], AX.X, ALU.add))
            link(dve.tensor_tensor(rtile[:, :, :], rtile[:, :, :], dest_f[:, :, :], ALU.add))
            ins = dve.tensor_scalar(dest_f[:, :, :], rtile[:, :, :], float(P), None, ALU.mult)
            link(ins)
            row_b = B - 1
            for t in range(TB * row_b, NT):
                for k in range(2):
                    last = dve.tensor_scalar(rowhot[:, t, k, :], iota[:, :], rrow[:, t, k:k + 1], None, ALU.is_equal)
            last.then_inc(rowhot_ready, 1)
            link(dve.tensor_copy(rtile16[:, :, :], rtile[:, :, :]))
            last = tile_onehots(NSLOT0)
            last.then_inc(tilehot_ready, 1)
            link(dve.tensor_tensor(ecmp[:, 0:NSLOT0, :], bc(etiles[:, 2, :], 1, NSLOT0), bc(iota[:, 0:NSLOT0], 2, E), ALU.is_le))
            link(dve.tensor_reduce(eslot[:, 0:NSLOT0], ecmp[:, 0:NSLOT0, :], AX.X, ALU.add))
            dve.tensor_scalar(eslot_i[:, 0:NSLOT0], eslot[:, 0:NSLOT0], float(E - 1), None, ALU.min).then_inc(eslot_ready, 1)
            dve.tensor_tensor(slot_u[:, :, :], dest_f[:, :, :], rrow[:, :, :], ALU.add)
            ring.wait_done(dve, ("source", 0))
            dve.tensor_copy(source[:, 0:NSLOT0], ring.bank(("source", 0))[:, 0:NSLOT0]).then_inc(ring.evacuated(("source", 0)), 1)
            ring.wait_evacuated(dve, ("source", 0))
            link_to = dve.tensor_copy(eslot[:, 0:1], eslot_i[:, 0:1])
            link_to.then_inc(slots_ready, 1)

            def copy_out(key, dst, n):
                ring.wait_done(dve, key)
                dve.tensor_copy(dst, ring.bank(key)[:, 0:n]).then_inc(ring.evacuated(key), 1)

            for i in range(NSLOT0 + 3):
                if i < NSLOT0:
                    if i >= 3:
                        ring.wait_done(dve, ("gu", i - 3))
                    copy_out(("xgT", i), xgT[:, i % 3, :], D)
                if 1 <= i <= NSLOT0:
                    s = i - 1
                    key = ("gu", s)
                    dve.wait_ge(silu_ready, s + 1)
                    if s >= 2:
                        ring.wait_done(dve, ("mT", s - 2))
                    dve.tensor_tensor(mid[:, s % 2, :], silu[:, s % 2, :], ring.bank(key)[:, M0:2 * M0],
                                      ALU.mult).then_inc(ring.evacuated(key), 1)
                if 2 <= i <= NSLOT0 + 1:
                    s = i - 2
                    if s >= 2:
                        ring.wait_done(dve, ("y", s - 2))
                    copy_out(("mT", s), midT[:, s % 2, :], P)

            for n in range(B):
                combine(dve, link, n)
            dve.wait_ge(combined, B)
            normalize(("c", 0))
            link(dve.memset(att_s[:, :, :, :], -BIG))

            def context_max(n):
                if n >= 2:
                    for half in range(2):
                        ring.wait_evacuated(dve, ("cs", n - 2, half))
                for half in range(2):
                    ring.wait_done(dve, ("cs", n, half))
                    last = dve.tensor_reduce(cmax[:, n % 2, half:half + 1], ring.bank(("cs", n, half)), AX.X, ALU.max)
                link(last)
                link(dve.tensor_tensor(cmax[:, n % 2, 2:3], cmax[:, n % 2, 0:1], cmax[:, n % 2, 1:2], ALU.max))
                dve.tensor_scalar(cmax[:, n % 2, 3:4], cmax[:, n % 2, 2:3], -CSCALE, None, ALU.mult).then_inc(cmax_ready, 1)

            def add_context(n):
                t, key = tile_of(n), ("co", n)
                link(dve.tensor_tensor(csum[:, n % 3, 2:3], csum[:, n % 3, 0:1], csum[:, n % 3, 1:2], ALU.add))
                link(dve.reciprocal(csum[:, n % 3, 3:4], csum[:, n % 3, 2:3]))
                ring.wait_done(dve, key)
                dve.scalar_tensor_tensor(x[:, t, :], ring.bank(key)[:, 0:D], csum[:, n % 3, 3:4], x[:, t, :],
                                         ALU.mult, ALU.add).then_inc(ring.evacuated(key), 1)
                ring.wait_evacuated(dve, key)
                dve.tensor_copy(csum[:, n % 3, 2:3], csum[:, n % 3, 3:4]).then_inc(x2_done, 1)

            def attend_scores(c):
                for s in range(B):
                    ring.wait_evacuated(dve, ("qkv", c, s))
                if c:
                    dve.wait_ge(att_diff, c)
                for k in range(B):
                    n = B - k
                    q = qkv[:, k:B, 0:H1 * DH1].rearrange("p s (g r d) -> p s g r d", g=KV1, d=DH1)
                    key = bc(bc(qkv[:, k, H1 * DH1:(H1 + KV1) * DH1].rearrange("p (g d) -> p g d", d=DH1), 2, H1 // KV1), 1, n)
                    pr = prod[:, 0:n, :].rearrange("p s (g r d) -> p s g r d", g=KV1, d=DH1)
                    for s in range(n):
                        last = dve.tensor_tensor(pr[:, s], q[:, s], key[:, s], ALU.mult)
                    link(last)
                    last = dve.tensor_reduce(att_s[:, k:B, :, k], prod[:, 0:n, :].rearrange("p s (h d) -> p s h d", d=DH1), AX.X, ALU.add)
                    link(last)
                link(dve.tensor_reduce(att_m[:, 0, :, :], att_s[:, :, :, :], AX.X, ALU.max))
                if c:
                    dve.wait_ge(att_exp, c)
                dve.tensor_tensor(att_d[:, :, :, :], att_s[:, :, :, :], bc(att_m[:, 0, :, :], 3, B), ALU.subtract).then_inc(att_diff, 1)

            def attend_weights(c):
                dve.wait_ge(att_exp, c + 1)
                link(dve.tensor_reduce(att_m[:, 1, :, :], att_e[:, :, :, :], AX.X, ALU.add))
                link(dve.reciprocal(att_m[:, 1, :, :], att_m[:, 1, :, :]))
                dve.tensor_tensor(att_e[:, :, :, :], att_e[:, :, :, :], bc(att_m[:, 1, :, :], 3, B), ALU.mult).then_inc(att_weights, 1)

            def start_hidden(c):
                i = ln_at["d", c]
                if c >= 2:
                    dve.wait_ge(x3_done, c - 1)
                for s in range(B):
                    last = dve.tensor_scalar(hid[:, c % 2, s, :], x[:, c + s * TB, :], mv[:, i % 4, s, 0:1], hid_rstd[:, s:s + 1],
                                             ALU.subtract, ALU.mult)
                link(last)

            def add_projection(c):
                for i in range(2):
                    key = ("po", c, i)
                    ring.wait_done(dve, key)
                    xs = hid[:, c % 2, 2 * i:2 * i + 2, :]
                    dve.tensor_tensor(xs, ring.bank(key).rearrange("p (t d) -> p t d", t=2), xs, ALU.add).then_inc(ring.evacuated(key), 1)
                for i in range(2):
                    ring.wait_evacuated(dve, ("po", c, i))

            def router_diff(c):
                key = ("rt", c)
                ring.wait_done(dve, key)
                logits = ring.bank(key)[:, 0:B * E].rearrange("p (s e) -> p s e", e=E)
                link(dve.tensor_reduce(rm[:, 0, :], logits, AX.X, ALU.max))
                dve.tensor_tensor(rl[:, 0, :, :], logits, bc(rm[:, 0, :], 2, E), ALU.subtract).then_inc(ring.evacuated(key), 1)
                ring.wait_evacuated(dve, key)
                dve.tensor_copy(rm[:, 1, :], rm[:, 0, :]).then_inc(rl_diff, 1)

            def choose2(c):
                ts = slice(c, NT, TB)
                dve.wait_ge(rl_exp, c + 1)
                link(dve.tensor_reduce(rm[:, 0, :], rl[:, 1, :, :], AX.X, ALU.add))
                link(dve.reciprocal(rm[:, 1, :], rm[:, 0, :]))
                link(dve.tensor_tensor(score[:, :, :], rl[:, 1, :, :], bc(rm[:, 1, :], 2, E), ALU.mult))
                for s in range(B):
                    last = dve.max(top8[:, s, :], score[:, s, :])
                link(last)
                for s in range(B):
                    last = dve.max_index(idx8[:, s, :], top8[:, s, :], score[:, s, :])
                link(last)
                link(dve.tensor_copy(idxf[:, :, :], idx8[:, :, 0:2]))
                dve.tensor_copy(weight2[:, ts, :], top8[:, :, 0:2])
                for k in range(2):
                    last = dve.tensor_tensor(pick[:, k, ts, :], bc(iota[:, 0:E], 1, B), bc(idxf[:, :, k], 2, E), ALU.is_equal)
                link(last)
                link(dve.tensor_tensor(chosen[:, ts, :], pick[:, 0, ts, :], pick[:, 1, ts, :], ALU.add))
                counts = earlier[:, c + 1:NT + 1:TB, :]
                if c:
                    link(dve.tensor_tensor(counts, earlier[:, c:NT:TB, :], chosen[:, ts, :], ALU.add))
                else:
                    link(dve.tensor_copy(counts, chosen[:, ts, :]))

            for i in range(NSTEP):
                c, phase = divmod(i, B)
                if i < NT:
                    context_max(i)
                if phase == 3 and 0 <= c - 2 < TB:
                    add_projection(c - 2)
                if phase == 2 and 0 <= c - 3 < TB:
                    router_diff(c - 3)
                if 2 <= i <= NT + 1:
                    add_context(i - 2)
                if phase == 2 and c + 1 < TB:
                    dve.wait_ge(combined_later, B * (c + 1))
                    normalize(("c", c + 1))
                if phase == 2 and 0 <= c - 3 < TB:
                    choose2(c - 3)
                if phase == 3 and 0 <= c - 2 < TB:
                    normalize(("l", c - 2))
                if phase == 0 and 0 <= c - 2 < TB:
                    attend_scores(c - 2)
                if phase == 1 and 0 <= c - 2 < TB:
                    attend_weights(c - 2)
                    if VALUES_DVE[c - 2]:
                        attend_values(dve, link, c - 2, VALUES_DVE[c - 2], prod, att_done)
                if phase == 1 and 0 <= c - 1 < TB:
                    normalize(("d", c - 1))
                    start_hidden(c - 1)

            for b in range(1, B):
                ins = dve.tensor_tensor(earlier[:, b * TB + 1:(b + 1) * TB + 1, :], earlier[:, b * TB + 1:(b + 1) * TB + 1, :],
                                        bc(earlier[:, b * TB, :], 1, TB), ALU.add)
                if b < B - 1:
                    link(ins)
            ins.then_inc(picks2_ready, 1)
            for k in range(2):
                link(dve.tensor_tensor(ptmp[:, :, :], pick[:, k, :, :], bc(iota[:, 0:E], 1, NT), ALU.mult))
                link(dve.tensor_reduce(dest_f[:, :, k], ptmp[:, :, :], AX.X, ALU.add))
            key = ("rank2", 0)
            ring.wait_done(dve, key)
            counted = ring.bank(key)[:, 0:NT * E].rearrange("p (t e) -> p t e", e=E)
            for k in range(2):
                link(dve.tensor_tensor(ptmp[:, :, :], pick[:, k, :, :], counted, ALU.mult))
                link(dve.tensor_reduce(rank[:, :, k], ptmp[:, :, :], AX.X, ALU.add))
            dve.tensor_copy(etiles[:, 1, :], ring.bank(key)[:, 0:E]).then_inc(ring.evacuated(key), 1)
            link(dve.tensor_scalar(keep[:, :, :], rank[:, :, :], float(CAP1), None, ALU.is_lt))
            link(dve.tensor_copy(rank_i[:, :, :], rank[:, :, :]))
            link(dve.tensor_scalar(part_i[:, :, :], rank_i[:, :, :], P - 1, None, ALU.bitwise_and))
            link(dve.tensor_copy(rrow16[:, :, :], part_i[:, :, :]))
            link(dve.tensor_scalar(part_i[:, :, :], rank_i[:, :, :], P.bit_length() - 1, None, ALU.arith_shift_right))
            link(dve.tensor_copy(rtile[:, :, :], part_i[:, :, :]))
            link(dve.scalar_tensor_tensor(rtile[:, :, :], dest_f[:, :, :], float(RT1), rtile[:, :, :], ALU.mult, ALU.add))
            link(dve.scalar_tensor_tensor(rtile[:, :, :], keep[:, :, :], -1000.0, rtile[:, :, :], ALU.mult, ALU.add))
            link(dve.tensor_scalar(rtile16[:, :, :], rtile[:, :, :], 1000.0, None, ALU.add))
            one_hots(rowhot[:, :, :, :], P, rrow16)
            tile_onehots(NSLOT1).then_inc(hots2_ready, 1)
            link(dve.scalar_tensor_tensor(dest_f[:, :, :], dest_f[:, :, :], float(CAP1), rank[:, :, :], ALU.mult, ALU.add))
            dve.tensor_tensor(slot_u[:, :, :], dest_f[:, :, :], keep[:, :, :], ALU.mult)
            link(dve.tensor_tensor(weight2[:, :, :], weight2[:, :, :], keep[:, :, :], ALU.mult))
            ring.wait_done(dve, ("source", 1))
            dve.tensor_copy(source[:, 0:NSLOT1], ring.bank(("source", 1))[:, 0:NSLOT1]).then_inc(ring.evacuated(("source", 1)), 1)
            ring.wait_evacuated(dve, ("source", 1))
            dve.tensor_copy(eslot[:, 0:1], source[:, 0:1]).then_inc(slots2_ready, 1)

            def expert_turned(e):
                if e >= 2:
                    ring.wait_done(dve, ("h1", e - 2, FC1 - 1))
                copy_out(("eT", e, 1), eT[:, e % 2, 1, :], CAP1)

            expert_turned(0)
            for e in range(E):
                if e + 1 < E:
                    expert_turned(e + 1)
                for j, (at_expert, parts) in enumerate(down_units):
                    if at_expert == e:
                        key = ("h2", j)
                        if j >= 3:
                            dve.wait_ge(y2_stored[j % 3], 16 * stores_before(j))
                        ring.wait_done(dve, key)
                        dve.tensor_copy(y2[:, j % 3, :], ring.bank(key)[:, 0:D]).then_inc(ring.evacuated(key), 1)
            dve.wait_ge(x3_done, TB)
            for t in range(NT):
                dve.wait_ge(y2_gathered[t % NYG], 32 * (t // NYG + 1))
                link(dve.scalar_tensor_tensor(x[:, t, :], yg[:, t % NYG, 0, :], weight2[:, t, 0:1], x[:, t, :], ALU.mult, ALU.add))
                dve.scalar_tensor_tensor(x[:, t, :], yg[:, t % NYG, 1, :], weight2[:, t, 1:2], x[:, t, :], ALU.mult,
                                         ALU.add).then_inc(finished, 1)


def lay_out(inputs):
    f = {k: np.asarray(v) for k, v in inputs.items()}

    def chunks(w):
        return np.ascontiguousarray(w.reshape(-1, P, w.shape[-1]).transpose(1, 0, 2))

    def halves(v):
        return [v[:P], v[P:]]

    gq, gk = f["L0_xattn_q_gamma"], f["L0_xattn_k_gamma"]
    cols = []
    for n in ("L0_xattn_ln_x_g", "L0_xattn_ln_x_b", "L0_xattn_ln_l_g", "L0_xattn_ln_l_b", "L1_ffn_ln1_weight", "L1_ffn_ln1_bias"):
        cols += halves(f[n])
    cols += [np.concatenate([gq, gq]), np.concatenate([gk, gk])]
    rows = np.concatenate([f["L0_xattn_b_out"], f["L1_ffn_ln2_weight"], f["L1_ffn_ln2_bias"], gq, gk])
    wg, wu, wd = f["L0_ffn_w_gate"], f["L0_ffn_w_up"], f["L0_ffn_w_down"]
    gu = np.concatenate([wg, wu], axis=2)
    return {
        "x": f["x"],
        "ctx": f["ctx_1024"],
        "ctxT": np.ascontiguousarray(f["ctx_1024"].transpose(2, 0, 1)).reshape(KC, P, B, SC).transpose(1, 0, 2, 3).copy(),
        "mask": np.ascontiguousarray(f["mask_BxS2_bk0"].reshape(B, CTB, P).transpose(2, 0, 1).reshape(P, B * CTB)).view(np.uint32),
        "cols": np.ascontiguousarray(np.stack(cols, axis=1)),
        "rows": np.ascontiguousarray(np.broadcast_to(rows, (P, NROW))),
        "wq": chunks(f["L0_xattn_W_q"]),
        "wkv": chunks(f["L0_xattn_W_kv"]),
        "wout": chunks(f["L0_xattn_W_out"]),
        "gate_w": chunks(f["L0_ffn_gate_w"].T),
        "sh_gu": chunks(np.concatenate([f["L0_ffn_ws_gate"], f["L0_ffn_ws_up"]], axis=1)),
        "sh_dn": f["L0_ffn_ws_down"],
        "e_gu": np.ascontiguousarray(gu.reshape(E, KC, P, 2 * M0).transpose(2, 1, 0, 3)),
        "e_dn": np.ascontiguousarray(wd.transpose(1, 0, 2)),
        "qkv_w": chunks(f["L1_ffn_qkv_weight"].T),
        "proj_w": chunks(f["L1_ffn_proj_weight"].T),
        "router_w": chunks(f["L1_ffn_router_weight"].T),
        "w1": np.ascontiguousarray(f["L1_ffn_moe_w1"].transpose(0, 2, 1).reshape(E, KC, P, F1).transpose(0, 2, 1, 3)),
        "w2": np.ascontiguousarray(f["L1_ffn_moe_w2"].transpose(0, 2, 1).reshape(E, FC1, P, D).transpose(0, 2, 1, 3)),
    }


def kernel(**inputs):
    import concourse.bacc as bacc
    from concourse.bass_utils import run_bass_kernel_spmd as run

    nc = bacc.Bacc("TRN2", target_bir_lowering=False, num_devices=1)
    arrays = lay_out(inputs)
    a = {n: nc.dram_tensor(f"in_{n}", v.shape, mybir.dt.from_np(v.dtype), kind="ExternalInput").ap() for n, v in arrays.items()}
    out = nc.dram_tensor("out", (B, S, D), F32, kind="ExternalOutput").ap()
    build(nc, a, out)
    r = run(nc, [{f"in_{n}": v for n, v in arrays.items()}], core_ids=[0])
    return r.results[0]["out"]
```

```python
from contextlib import ExitStack

import numpy as np

import concourse.bass as bass
from concourse import mybir

F32 = mybir.dt.float32
F32R = mybir.dt.float32r
F16 = mybir.dt.float16
I32 = mybir.dt.int32
U32 = mybir.dt.uint32
U8 = mybir.dt.uint8
ALU = mybir.AluOpType
ACT = mybir.ActivationFunctionType
AX = mybir.AxisListType

P = 128
B, S, D = 4, 512, 256
KC = D // P
TB = S // P
NT = B * TB
SC = 1024
CTB = SC // P
H0, DH0 = 4, 64
NPAIR = H0 // 2
KT0 = TB + CTB
NG = B * 3
E = 16
M0 = 128
F1 = 512
FC1 = F1 // P
NSLOT0 = (2 * NT * P + E * (P - 1)) // P
CAP1 = -(-(NT * P * 2 * 5) // (E * 4))
RT1 = -(-CAP1 // P)
NSLOT1 = E * RT1
H1, KV1, DH1 = 16, 4, 16
NRING = 6
NXG = 4
GATHER_AHEAD = 2
NXG1 = GATHER_AHEAD * RT1
NYG = 4
NT_DVE = 11
RSQRT_SEED = float(0x5F3759DF)
BIG = 1e30

COLS = ("ln_x_g0", "ln_x_g1", "ln_x_b0", "ln_x_b1", "ln_l_g0", "ln_l_g1", "ln_l_b0", "ln_l_b1",
        "ln1_w0", "ln1_w1", "ln1_b0", "ln1_b1", "gamma_q", "gamma_k")
ROWS = {"b_out": (0, D), "ln2_w": (D, D), "ln2_b": (2 * D, D), "gamma_q": (3 * D, DH0), "gamma_k": (3 * D + DH0, DH0)}
NROW = 3 * D + 2 * DH0
NSTEP = NT + 1
CSCALE = 0.25
QKV = (H1 + 2 * KV1) * DH1
VALUES_DVE = [(), (), (), (1, 3)]
VALUES_POOL = [(0, 1, 2, 3), (0, 1, 2, 3), (0, 1, 2, 3), (0, 2)]
NW = 4


def bc(ap, axis, n):
    a = ap.unsqueeze(axis)
    shape = list(a.shape)
    shape[axis] = n
    return a.broadcast_to(shape)


class BankRing:

    def __init__(self, banks, n, unit_done, evacuated):
        self.banks, self.n, self.unit_done, self.evac = banks, n, unit_done, evacuated
        self.place = {}
        self.uses = [0] * len(banks)
        self.next = 0

    def take(self, pe, key):
        b = self.next
        self.next = (b + 1) % self.n
        self.place[key] = len(self.place), b, self.uses[b]
        if self.uses[b]:
            pe.wait_ge(self.evac[b], self.uses[b])
        self.uses[b] += 1
        return self.banks[b]

    def grow(self):
        self.n = len(self.banks)

    def bank(self, key):
        return self.banks[self.place[key][1]]

    def evacuated(self, key):
        return self.evac[self.place[key][1]]

    def wait_done(self, eng, key):
        eng.wait_ge(self.unit_done, self.place[key][0] + 1)

    def wait_evacuated(self, eng, key):
        _, b, uses = self.place[key]
        eng.wait_ge(self.evac[b], uses + 1)


def build(nc, a, out):
    ctx = ExitStack()
    with ctx:
        def sb(name, shape, dt=F32):
            return ctx.enter_context(nc.sbuf_tensor(name, shape, dt))

        def sem(name):
            return ctx.enter_context(nc.semaphore(name))

        x = sb("x_res", [P, NT, D])
        ident = sb("ident", [P, P])
        ones = sb("ones", [P, P])
        headsel = sb("headsel", [P, 2])
        before = sb("before", [P, P], F16)
        ones16 = sb("ones16", [P, P], F16)
        iota = sb("iota", [P, P])
        iota16 = sb("iota16", [P, P], F16)
        token16 = sb("token16", [P, NT, 2], F16)
        rrow16 = sb("rrow16", [P, NT, 2], F16)
        rtile16 = sb("rtile16", [P, NT, 2], F16)
        thresholds = sb("thresholds", [P, E])
        zero16 = sb("zero16", [P, E])
        cols = sb("cols", [P, len(COLS)])
        rows = sb("rows", [P, NROW])
        mv = sb("mv", [P, 4, TB, 2])
        st = sb("st", [P, TB, 6])
        rstd = sb("rstd", [P, 4, TB])
        nwt = sb("nwt", [P, 2, 3, 48])
        lnt = sb("lnt", [P, 2, TB])
        hid_rstd = sb("hid_rstd", [P, TB])
        kss = sb("kss", [P, 3, TB * H0])
        weight2 = sb("weight2", [P, NT, 2])
        keep = sb("keep", [P, NT, 2])
        mask8 = sb("mask8", [P, B * CTB // 4], U32)
        pick = sb("pick", [P, 2, NT, E])
        weight = sb("weight", [P, NT, 2])
        chosen = sb("chosen", [P, NT, E], F16)
        earlier = sb("earlier", [P, NT + 1, E], F16)
        top8 = sb("top8", [P, TB, 8])
        idx8 = sb("idx8", [P, TB, 8], U32)
        idxf = sb("idxf", [P, TB, 2])
        score = sb("score", [P, TB, E])
        wtmp = sb("wtmp", [P, TB, 2])
        ptmp = sb("ptmp", [P, NT, E])
        rank = sb("rank", [P, NT, 2])
        rank_i = sb("rank_i", [P, NT, 2], I32)
        part_i = sb("part_i", [P, NT, 2], I32)
        rrow = sb("rrow", [P, NT, 2])
        rtile = sb("rtile", [P, NT, 2])
        rowhot = sb("rowhot", [P, NT, 2, P], F16)
        tilehot = sb("tilehot", [P, NT, 2, 48], F16)
        etiles = sb("etiles", [P, 3, E])
        signed16 = sb("signed16", [P, NT, 2], F16)
        ecmp = sb("ecmp", [P, 48, E])
        eslot = sb("eslot", [P, 48])
        eslot_i = sb("eslot_i", [P, 48], I32)
        slot_u = sb("slot_u", [P, NT, 2], U32)
        source = sb("source", [P, 48], U32)
        dest_f = sb("dest_f", [P, NT, 2])

        base = int(nc.sbuf_base) + 64
        arena = nc.sbuf_usable_end

        def place(at, name, shape, dt=F32):
            size = int(np.prod(shape[1:])) * {F16: 2, U8: 1}.get(dt, 4)
            t = nc.alloc_sbuf_tensor_at(name, shape, dt, offset=at[0])
            at[0] += -(-size // 32) * 32
            assert at[0] <= arena, (name, at[0], arena)
            return t

        at = [-(-base // 64) * 64]
        hT_at = at[0]
        hT = place(at, "hT", [P, KC, NT * P])
        gate_w = place(at, "gate_w", [P, KC, E])
        sh_gu = place(at, "sh_gu", [P, KC, 2 * M0])
        sh_dn = place(at, "sh_dn", [P, D])
        qkv_w = place(at, "qkv_w", [P, KC, QKV])
        proj_w = place(at, "proj_w", [P, KC, D])
        router_w = place(at, "router_w", [P, KC, E])
        hn = place(at, "hn", [P, 1, TB, D])
        rexp = place(at, "rexp", [P, TB * E])
        phase_at = at[0]
        wq = place(at, "wq", [P, KC, D])
        wkv = place(at, "wkv", [P, KC, 2 * D])
        wout = place(at, "wout", [P, KC, D])
        xn = place(at, "xn", [P, 2, TB, D])
        xnT = place(at, "xnT", [P, 2, KC, S])
        kstack = place(at, "kstack", [P, H0, KT0 * P], F32R)
        vals = place(at, "vals", [P, KT0, D])
        ksq = place(at, "ksq", [P, NPAIR, S])
        rkey = place(at, "rkey", [P, 2, KT0, H0])
        qn = place(at, "qn", [P, TB, D])
        qsq = place(at, "qsq", [P, TB, D])
        ssq = place(at, "ssq", [P, TB * H0])
        rq = place(at, "rq", [P, TB * H0])
        qdup = place(at, "qdup", [P, TB * H0, 2, DH0])
        qhi = place(at, "qhi", [P, H0, S], F32R)
        qlo = place(at, "qlo", [P, H0, S], F32R)
        gqk = place(at, "gqk", [P, 1])
        gbound = place(at, "gbound", [P, DH0 + 2])
        mbias = place(at, "mbias", [P, B, CTB])
        lbias = place(at, "lbias", [P, 1])
        probs = place(at, "probs", [P, 3, 2, S])
        psums = place(at, "psums", [P, 2, 2 * S])
        rden = place(at, "rden", [P, S])
        attnT = place(at, "attnT", [P, NPAIR, S])
        ctx_in = place(at, "ctx_in", [P, 2, TB, D])
        at = [phase_at]
        yg = place(at, "yg", [P, NYG, 2, D])
        ctx_at = at[0]
        ctx_n = place(at, "ctx_n", [P, B, CTB, D])
        ctx_t = place(at, "ctx_t", [P, KC, B, SC])
        work_at = at[0]
        at = [ctx_at]
        w1 = place(at, "w1", [P, NW, KC, F1])
        w2 = place(at, "w2", [P, NW, FC1, D])
        h1 = place(at, "h1", [P, 2, FC1, CAP1])
        y2 = place(at, "y2", [P, 3, D])
        xg2 = place(at, "xg2", [P, NXG1, D])
        assert at[0] <= work_at - B * QKV * 4
        at = [work_at - B * QKV * 4]
        qkv_last = place(at, "qkv_last", [P, B, QKV])
        at = [ctx_at]
        y_both = place(at, "y_both", [P, NT, 2, D])
        assert at[0] <= work_at
        at = [work_at]
        un = place(at, "un", [P, B, D])
        uT = place(at, "uT", [P, KC, B * P])
        cprob = place(at, "cprob", [P, 2, SC])
        cprobT = place(at, "cprobT", [P, 2, SC])
        csum = place(at, "csum", [P, 3, 4])
        cmax = place(at, "cmax", [P, 2, 4])
        dn = place(at, "dn", [P, B, D])
        dT = place(at, "dT", [P, KC, B * P])
        oT = place(at, "oT", [P, KC, B * P])
        hid = place(at, "hid", [P, 2, B, D])
        l_n = place(at, "l_n", [P, B, D])
        lT = place(at, "lT", [P, KC, B * P])
        qkv = place(at, "qkv", [P, B, QKV])
        prod = place(at, "prod", [P, B, D])
        at = [work_at]
        w1_parts = place(at, "w1_parts", [P, 2, 2, KC * F1], F32R)
        w2_parts = place(at, "w2_parts", [P, 2, 2, FC1 * D], F32R)
        h1_parts = place(at, "h1_parts", [P, 2, 2, FC1, CAP1], F32R)
        eT_parts = place(at, "eT_parts", [P, 2, 2, KC, CAP1], F32R)
        at = [hT_at]
        att_s = place(at, "att_s", [P, B, H1, B])
        att_d = place(at, "att_d", [P, B, H1, B])
        att_e = place(at, "att_e", [P, B, H1, B])
        att_m = place(at, "att_m", [P, 2, B, H1])
        att_o = place(at, "att_o", [P, B, D])
        value_prod = place(at, "value_prod", [P, B, D])
        rl = place(at, "rl", [P, 2, B, E])
        rm = place(at, "rm", [P, 2, B])
        zeros = place(at, "zeros", [P, D])
        dump_row = place(at, "dump_row", [P, NSLOT1])
        srows = place(at, "srows", [P, 3, NSLOT1])
        y_to = place(at, "y_to", [P, E * RT1], U32)
        at = [work_at]
        e_gu = place(at, "e_gu", [P, KC, E, 2 * M0])
        e_dn = place(at, "e_dn", [P, E, D])
        xg = place(at, "xg", [P, NXG, D])
        xgT = place(at, "xgT", [P, 3, D])
        silu = place(at, "silu", [P, 2, M0])
        up = place(at, "up", [P, 2, M0])
        mid = place(at, "mid", [P, 2, M0])
        midT = place(at, "midT", [P, 2, P])
        ysb = place(at, "ysb", [P, 3, D])

        ring_psum = ctx.enter_context(nc.psum_tensor("ring_psum", [P, NRING, 512], F32))
        acc_psum = ctx.enter_context(nc.psum_tensor("acc_psum", [P, 2, 512], F32))

        h_rows = nc.dram_tensor("h_rows", (NT * P, D), F32).ap()
        l_rows = nc.dram_tensor("l_rows", (NT * P, D), F32).ap()
        y_choices = nc.dram_tensor("y_choices", (2 * NT * P + NSLOT1 * P, D), F32).ap()
        y_rows = nc.dram_tensor("y_rows", (NSLOT0 * P, D), F32).ap()

        x_loaded = [sem(f"x_loaded{b}") for b in range(B)]
        ctx_loaded = [sem(f"ctx_loaded{i}") for i in range(2)]
        small_loaded = sem("small_loaded")
        wa_loaded = sem("wa_loaded")
        wb_loaded = sem("wb_loaded")
        consts_made = sem("consts_made")
        dve_step = sem("dve_step")
        pool_step = sem("pool_step")
        unit_done = sem("unit_done")
        evacuated = [sem(f"evacuated{i}") for i in range(NRING + 2)]
        ln_applied = sem("ln_applied")
        bias_added = sem("bias_added")
        khi_ready = sem("khi_ready")
        rkey_ready = sem("rkey_ready")
        rq_ready = sem("rq_ready")
        qdup_ready = sem("qdup_ready")
        qhi_ready = sem("qhi_ready")
        exp_consts_ready = sem("exp_consts_ready")
        pv_done = sem("pv_done")
        psums_added = sem("psums_added")
        attn_evacuated = sem("attn_evacuated")
        hn_stored = sem("hn_stored")
        picks_ready = sem("picks_ready")
        rrow_ready = sem("rrow_ready")
        rowhot_ready = sem("rowhot_ready")
        out_stored = sem("out_stored")
        e_loaded = sem("e_loaded")
        shared_mid = sem("shared_mid")
        shared_added = sem("shared_added")
        tilehot_ready = sem("tilehot_ready")
        eslot_ready = sem("eslot_ready")
        slots_ready = sem("slots_ready")
        gathered = [sem(f"gathered{i}") for i in range(NXG)]
        silu_ready = sem("silu_ready")
        y_stored = [sem(f"y_stored{i}") for i in range(3)]
        y_gathered = [sem(f"y_gathered{i}") for i in range(NYG)]
        combined = sem("combined")
        combined_later = sem("combined_later")
        ctx_n_loaded = sem("ctx_n_loaded")
        ctx_t_loaded = sem("ctx_t_loaded")
        wd_loaded = sem("wd_loaded")
        cmax_ready = sem("cmax_ready")
        x2_done = sem("x2_done")
        att_diff = sem("att_diff")
        att_exp = sem("att_exp")
        att_weights = sem("att_weights")
        att_done = sem("att_done")
        att_done_pool = sem("att_done_pool")
        x3_done = sem("x3_done")
        l_stored = sem("l_stored")
        rl_diff = sem("rl_diff")
        rl_exp = sem("rl_exp")
        picks2_ready = sem("picks2_ready")
        rrow2_ready = sem("rrow2_ready")
        rowhot2_ready = sem("rowhot2_ready")
        hots2_ready = sem("hots2_ready")
        slots2_ready = sem("slots2_ready")
        gathered2 = [sem(f"gathered2_{i}") for i in range(NXG1)]
        w1_high = sem("w1_high")
        w2_high = sem("w2_high")
        w2_low = sem("w2_low")
        h1_high = sem("h1_high")
        h1_low = sem("h1_low")
        w1_low = sem("w1_low")
        eT_high = sem("eT_high")
        w_loaded = [sem(f"w_loaded{i}") for i in range(NW)]
        y2_scattered = [sem(f"y2_scattered{i}") for i in range(3)]
        zeros_made = sem("zeros_made")
        zeros_stored = sem("zeros_stored")
        y_to_ready = sem("y_to_ready")
        y_both_loaded = [sem(f"y_both_loaded{i}") for i in range(NT)]
        finished = sem("finished")

        banks = [ring_psum[:, i, :] for i in range(NRING)] + [acc_psum[:, i, :] for i in range(2)]
        ring = BankRing(banks, NRING, unit_done, evacuated)

        def col(name):
            i = COLS.index(name)
            return cols[:, i:i + 1]

        def row(name):
            o, n = ROWS[name]
            return rows[:, o:o + n]

        ln_order = [0, 1]
        for b in range(B):
            ln_order.append(3 * b + 2)
            if b + 1 < B:
                ln_order.append(3 * b + 3)
            if b:
                ln_order.append(("h", b - 1))
            if b + 1 < B:
                ln_order.append(3 * b + 4)
        ln_order.append(("h", B - 1))
        ln_order.append(("c", 0))
        for i in range(NSTEP):
            c, phase = divmod(i, B)
            if phase == 2 and c + 1 < TB:
                ln_order.append(("c", c + 1))
            if phase == 1 and 0 <= c - 1 < TB:
                ln_order.append(("d", c - 1))
            if phase == 3 and 0 <= c - 2 < TB:
                ln_order.append(("l", c - 2))
        ln_order += [("d", TB - 1), ("l", TB - 2), ("l", TB - 1)]
        ln_at = {k: i for i, k in enumerate(ln_order)}

        def step(b, p, j):
            return (b * NPAIR + p) * KT0 + j

        def tile_of(n):
            return n % B * TB + n // B

        def add_shared(pool, t):
            ring.wait_evacuated(pool, ("sy", t))
            pool.tensor_tensor(x[:, t, :], x[:, t, :], ysb[:, t % 2, :], ALU.add).then_inc(shared_added, 1)

        def combine(eng, link, n):
            t = tile_of(n)
            eng.wait_ge(y_gathered[n % NYG], 32 * (n // NYG + 1))
            if n == 0:
                eng.wait_ge(shared_added, NT)
            both = yg[:, n % NYG, :, :]
            if n < B:
                for k in range(2):
                    last = eng.scalar_tensor_tensor(x[:, t, :], both[:, k, :], weight[:, t, k:k + 1], x[:, t, :], ALU.mult, ALU.add)
                    if k == 0:
                        link(last)
                last.then_inc(combined, 1)
                return
            link(eng.tensor_tensor(both, both, bc(weight[:, t, :], 2, D), ALU.mult))
            link(eng.tensor_tensor(x[:, t, :], x[:, t, :], both[:, 0, :], ALU.add))
            eng.tensor_tensor(x[:, t, :], x[:, t, :], both[:, 1, :], ALU.add).then_inc(combined_later, 1)

        def qkv_of(c):
            return qkv_last if c == TB - 1 else qkv

        def wait_values(eng, c):
            eng.wait_ge(att_done_pool, c + 1)
            if VALUES_DVE[c]:
                eng.wait_ge(att_done, sum(1 for q in VALUES_DVE[:c + 1] if q))

        def attend_values(eng, link, c, queries, product, done):
            eng.wait_ge(att_weights, c + 1)
            if c:
                ring.wait_done(eng, ("oT", c - 1, KC - 1))
            for k in range(queries[-1] + 1):
                v = bc(qkv_of(c)[:, k, (H1 + KV1) * DH1:QKV].rearrange("p (g d) -> p g d", d=DH1), 2, H1 // KV1)
                seen_by = [s for s in queries if s >= k]
                for s in seen_by:
                    dst = att_o if k == 0 else product
                    last = eng.tensor_tensor(dst[:, s, :].rearrange("p (g r d) -> p g r d", g=KV1, d=DH1), v,
                                             bc(att_e[:, s, :, k].rearrange("p (g r) -> p g r", g=KV1), 3, DH1), ALU.mult)
                link(last)
                if k:
                    for s in seen_by:
                        last = eng.tensor_tensor(att_o[:, s, :], att_o[:, s, :], product[:, s, :], ALU.add)
                    if k < queries[-1]:
                        link(last)
            last.then_inc(done, 1)

        assert CAP1 - (RT1 - 1) * P == P // 2 and E % 2 == 0
        down_units = []
        for e in range(E):
            down_units += [(e, [(slice(0, P), e, r * P)]) for r in range(RT1 - 1)]
            if e % 2:
                down_units.append((e, [(slice(0, P // 2), e - 1, (RT1 - 1) * P), (slice(P // 2, P), e, (RT1 - 1) * P)]))

        def last_down(e):
            return max(j for j, (_, parts) in enumerate(down_units) if e in [p[1] for p in parts])

        block = ctx.enter_context(nc.Block())

        @block.tensor
        def _(pe):
            def transposes(g):
                pe.wait_ge(ln_applied, ln_at[g] + 1)
                for k in range(KC):
                    bank = ring.take(pe, ("xT", g, k))
                    for t in range(TB):
                        last = pe.transpose(bank[:, t * P:(t + 1) * P], xn[:, g % 2, t, k * P:(k + 1) * P], ident[:, :])
                    last.then_inc(unit_done, 1)

            def projections(g):
                project_keys(g)
                project_rows(g)

            def project_keys(g):
                for k in range(KC):
                    ring.wait_evacuated(pe, ("xT", g, k))
                for p in range(NPAIR):
                    bank = ring.take(pe, ("kT", g, p))
                    for k in range(KC):
                        last = pe.matmul(bank, wkv[:, k, p * P:(p + 1) * P], xnT[:, g % 2, k, :],
                                         start=(k == 0), stop=(k == KC - 1))
                    last.then_inc(unit_done, 1)

            def project_rows(g):
                if g % 3 == 0:
                    for i in range(2):
                        token_major(("q", g, i), g, i, wq[:, :, :])
                for i in range(2):
                    token_major(("v", g, i), g, i, wkv[:, :, D:2 * D])

            def token_major(key, g, i, w):
                bank = ring.take(pe, key)
                for t in range(2):
                    for k in range(KC):
                        last = pe.matmul(bank[:, t * D:(t + 1) * D],
                                         xnT[:, g % 2, k, (2 * i + t) * P:(2 * i + t + 1) * P], w[:, k, :],
                                         start=(k == 0), stop=(k == KC - 1))
                last.then_inc(unit_done, 1)

            def key_squares(g):
                bank = ring.take(pe, ("ss", g))
                for p in range(NPAIR):
                    pe.wait_ge(khi_ready, g * NPAIR + p + 1)
                    for t in range(TB):
                        c = (t * NPAIR + p) * 2
                        last = pe.matmul(bank[:, c:c + 2], ksq[:, p, t * P:(t + 1) * P], headsel[:, :],
                                         start=True, stop=True)
                last.then_inc(unit_done, 1)

            def query_transposes(b):
                pe.wait_ge(qdup_ready, 2 * (b + 1))
                for h in range(H0):
                    bank = ring.take(pe, ("qT", b, h))
                    for t in range(TB):
                        last = pe.transpose(bank[:, t * P:(t + 1) * P],
                                            qdup[:, t * H0 + h, :, :].rearrange("p a d -> p (a d)"), ident[:, :])
                    last.then_inc(unit_done, 1)

            def scores(b, p, j):
                for h in range(2):
                    hh = 2 * p + h
                    bank = ring.take(pe, ("s", b, p, j, h))
                    pe.matmul(bank, kstack[:, hh, j * P:(j + 1) * P], qhi[:, hh, :], start=True, stop=False)
                    pe.matmul(bank, kstack[:, hh, j * P:(j + 1) * P], qlo[:, hh, :],
                              start=False, stop=True).then_inc(unit_done, 1)

            def weigh(b, p, j):
                n, m = step(b, p, j), b * NPAIR + p
                if j == 0 and m >= 2:
                    pe.wait_ge(attn_evacuated, m - 1)
                for h in range(2):
                    ring.wait_evacuated(pe, ("s", b, p, j, h))
                    last = pe.matmul(acc_psum[h * DH0:(h + 1) * DH0, m % 2, :],
                                     vals[:, j, (2 * p + h) * DH0:(2 * p + h + 1) * DH0], probs[:, n % 3, h, :],
                                     start=(j == 0), stop=(j == KT0 - 1), skip_group_check=True)
                last.then_inc(pv_done, 1)

            def denominators(b, p):
                m = b * NPAIR + p
                pe.wait_ge(psums_added, KT0 * (m + 1))
                bank = ring.take(pe, ("den", b, p))
                for h in range(2):
                    last = pe.matmul(bank[h * DH0:(h + 1) * DH0, :], ones[:, 0:DH0], psums[:, m % 2, h * S:(h + 1) * S],
                                     start=True, stop=True, skip_group_check=True)
                last.then_inc(unit_done, 1)

            def out_projection(b):
                for i in range(2):
                    bank = ring.take(pe, ("wo", b, i))
                    pe.wait_ge(attn_evacuated, NPAIR * (b + 1))
                    for t in range(2):
                        for p in range(NPAIR):
                            last = pe.matmul(bank[:, t * D:(t + 1) * D], attnT[:, p, (2 * i + t) * P:(2 * i + t + 1) * P],
                                             wout[:, p, :], start=(p == 0), stop=(p == NPAIR - 1))
                    last.then_inc(unit_done, 1)

            def expert_norm_transposes(b):
                pe.wait_ge(ln_applied, ln_at["h", b] + 1)
                for k in range(KC):
                    bank = ring.take(pe, ("hT", b, k))
                    for t in range(TB):
                        last = pe.transpose(bank[:, t * P:(t + 1) * P], hn[:, 0, t, k * P:(k + 1) * P], ident[:, :])
                    last.then_inc(unit_done, 1)

            def router(b):
                for k in range(KC):
                    ring.wait_evacuated(pe, ("hT", b, k))
                bank = ring.take(pe, ("gate", b))
                for t in range(TB):
                    for k in range(KC):
                        last = pe.matmul(bank[:, t * E:(t + 1) * E], hT[:, k, (TB * b + t) * P:(TB * b + t + 1) * P],
                                         gate_w[:, k, :], start=(k == 0), stop=(k == KC - 1))
                last.then_inc(unit_done, 1)

            def ranks(b):
                pe.wait_ge(picks_ready, b + 1)
                bank = ring.take(pe, ("rank", b))
                n = TB * E
                pe.matmul(bank[:, 0:n], before[:, :], chosen[:, TB * b:TB * b + TB, :].rearrange("p t e -> p (t e)"),
                          start=True, stop=False)
                last = pe.matmul(bank[:, 0:n], ones16[:, :],
                                 earlier[:, TB * b:TB * b + TB, :].rearrange("p t e -> p (t e)"), start=False, stop=True)
                if b == B - 1:
                    last = pe.matmul(bank[:, n:n + E], ones16[:, :], earlier[:, NT, :], start=True, stop=True)
                last.then_inc(unit_done, 1)

            def shared_up(t):
                bank = ring.take(pe, ("sgu", t))
                for k in range(KC):
                    last = pe.matmul(bank[:, 0:2 * M0], hT[:, k, t * P:(t + 1) * P], sh_gu[:, k, :],
                                     start=(k == 0), stop=(k == KC - 1))
                last.then_inc(unit_done, 1)

            def shared_turn(t):
                pe.wait_ge(shared_mid, t + 1)
                bank = ring.take(pe, ("smT", t))
                pe.transpose(bank[:, 0:P], mid[:, t % 2, :], ident[:, :]).then_inc(unit_done, 1)

            def shared_down(t):
                ring.wait_evacuated(pe, ("smT", t))
                bank = ring.take(pe, ("sy", t))
                pe.matmul(bank[:, 0:D], midT[:, t % 2, :], sh_dn[:, :], start=True, stop=True).then_inc(unit_done, 1)

            def shared_step(i):
                if i < NT:
                    shared_up(i)
                if 1 <= i <= NT:
                    shared_turn(i - 1)
                if i >= 2:
                    shared_down(i - 2)

            pe.wait_ge(consts_made, 1)
            transposes(0)
            pe.wait_ge(wa_loaded, 48)
            for b in range(B):
                g = 3 * b
                if b == 0:
                    project_keys(g)
                project_rows(g)
                if b == 0:
                    transposes(g + 1)
                transposes(g + 2)
                key_squares(g)
                projections(g + 1)
                query_transposes(b)
                key_squares(g + 1)
                projections(g + 2)
                if b + 1 < B:
                    transposes(g + 3)
                key_squares(g + 2)
                for p in range(NPAIR):
                    for j in range(KT0):
                        scores(b, p, j)
                        if j >= 2:
                            weigh(b, p, j - 2)
                        if j == 6 and p == 0 and b:
                            if b == 1:
                                pe.wait_ge(wb_loaded, 48)
                            expert_norm_transposes(b - 1)
                        if j == 8 and p == 0 and b:
                            router(b - 1)
                        if j == 3 and p == 1:
                            denominators(b, 0)
                        if j == 10 and p == 1 and b:
                            ranks(b - 1)
                    weigh(b, p, KT0 - 2)
                    weigh(b, p, KT0 - 1)
                denominators(b, 1)
                if b + 1 < B:
                    transposes(g + 4)
                    project_keys(g + 3)
                else:
                    shared_step(0)
                    shared_step(1)
                out_projection(b)
            ring.grow()
            for i in range(2, 6):
                shared_step(i)
            expert_norm_transposes(B - 1)
            router(B - 1)

            for i in range(6, NT + 2):
                shared_step(i)
                if i == 9:
                    ranks(B - 1)

            def slot_sources(key, n):
                bank = ring.take(pe, key)
                for t in range(NT):
                    for k in range(2):
                        last = pe.matmul(bank[:, 0:n], rowhot[:, t, k, :], tilehot[:, t, k, 0:n],
                                         start=(t == 0 and k == 0), stop=(t == NT - 1 and k == 1))
                last.then_inc(unit_done, 1)

            pe.wait_ge(rowhot_ready, B)
            pe.wait_ge(tilehot_ready, 1)
            slot_sources(("source", 0), NSLOT0)

            expert = {}

            def slot_turn(s):
                pe.wait_ge(gathered[s % NXG], 16 * (s // NXG + 1))
                bank = ring.take(pe, ("xgT", s))
                for k in range(KC):
                    last = pe.transpose(bank[:, k * P:(k + 1) * P], xg[:, s % NXG, k * P:(k + 1) * P], ident[:, :])
                last.then_inc(unit_done, 1)
                expert[s] = pe.value_load(eslot_i[0:1, s:s + 1], min_val=0, max_val=E - 1)

            def slot_up(s):
                ring.wait_evacuated(pe, ("xgT", s))
                bank = ring.take(pe, ("gu", s))
                for k in range(KC):
                    last = pe.matmul(bank[:, 0:2 * M0], xgT[:, s % 3, k * P:(k + 1) * P],
                                     e_gu[:, k, bass.ds(expert[s], 1), :], start=(k == 0), stop=(k == KC - 1))
                last.then_inc(unit_done, 1)

            def slot_mid_turn(s):
                ring.wait_evacuated(pe, ("gu", s))
                bank = ring.take(pe, ("mT", s))
                pe.transpose(bank[:, 0:P], mid[:, s % 2, :], ident[:, :]).then_inc(unit_done, 1)

            def slot_down(s):
                ring.wait_evacuated(pe, ("mT", s))
                bank = ring.take(pe, ("y", s))
                pe.matmul(bank[:, 0:D], midT[:, s % 2, :], e_dn[:, bass.ds(expert[s], 1), :],
                          start=True, stop=True).then_inc(unit_done, 1)

            pe.wait_ge(eslot_ready, 1)
            pe.wait_ge(e_loaded, 32)
            for i in range(NSLOT0 + 3):
                if i < NSLOT0:
                    slot_turn(i)
                if 1 <= i <= NSLOT0:
                    slot_up(i - 1)
                if 2 <= i <= NSLOT0 + 1:
                    slot_mid_turn(i - 2)
                if i >= 3:
                    slot_down(i - 3)

            def turn_tokens(key, ln_key, src):
                pe.wait_ge(ln_applied, ln_at[ln_key] + 1)
                for k in range(KC):
                    bank = ring.take(pe, key + (k,))
                    for s in range(B):
                        last = pe.transpose(bank[:, s * P:(s + 1) * P], src[:, s, k * P:(k + 1) * P], ident[:, :])
                    last.then_inc(unit_done, 1)

            def context_scores(n):
                c, s = divmod(n, B)
                if s == 0:
                    for k in range(KC):
                        ring.wait_evacuated(pe, ("uT", c, k))
                for half in range(2):
                    bank = ring.take(pe, ("cs", n, half))
                    for k in range(KC):
                        last = pe.matmul(bank, uT[:, k, s * P:(s + 1) * P], ctx_t[:, k, s, half * 512:(half + 1) * 512],
                                         start=(k == 0), stop=(k == KC - 1))
                    last.then_inc(unit_done, 1)

            def context_turn(n):
                for half in range(2):
                    ring.wait_evacuated(pe, ("cs", n, half))
                for half in range(2):
                    bank = ring.take(pe, ("cp", n, half))
                    for t in range(4):
                        o = half * 512 + t * P
                        last = pe.transpose(bank[:, t * P:(t + 1) * P], cprob[:, n % 2, o:o + P], ident[:, :])
                    last.then_inc(unit_done, 1)

            def context_values(n):
                for half in range(2):
                    ring.wait_evacuated(pe, ("cp", n, half))
                bank = ring.take(pe, ("co", n))
                for t in range(CTB):
                    last = pe.matmul(bank[:, 0:D], cprobT[:, n % 2, t * P:(t + 1) * P], ctx_n[:, n % B, t, :],
                                     start=(t == 0), stop=(t == CTB - 1))
                last.then_inc(unit_done, 1)

            def project_qkv(c):
                for k in range(KC):
                    ring.wait_evacuated(pe, ("dT", c, k))
                for s in range(B):
                    bank = ring.take(pe, ("qkv", c, s))
                    for k in range(KC):
                        last = pe.matmul(bank[:, 0:QKV], dT[:, k, s * P:(s + 1) * P], qkv_w[:, k, :],
                                         start=(k == 0), stop=(k == KC - 1))
                    last.then_inc(unit_done, 1)

            def turn_attention(c):
                wait_values(pe, c)
                for k in range(KC):
                    bank = ring.take(pe, ("oT", c, k))
                    for s in range(B):
                        last = pe.transpose(bank[:, s * P:(s + 1) * P], att_o[:, s, k * P:(k + 1) * P], ident[:, :])
                    last.then_inc(unit_done, 1)

            def project_out(c):
                for k in range(KC):
                    ring.wait_evacuated(pe, ("oT", c, k))
                for i in range(2):
                    bank = ring.take(pe, ("po", c, i))
                    for t in range(2):
                        for k in range(KC):
                            last = pe.matmul(bank[:, t * D:(t + 1) * D], oT[:, k, (2 * i + t) * P:(2 * i + t + 1) * P],
                                             proj_w[:, k, :], start=(k == 0), stop=(k == KC - 1))
                    last.then_inc(unit_done, 1)

            def router2(c):
                for k in range(KC):
                    ring.wait_evacuated(pe, ("lT", c, k))
                bank = ring.take(pe, ("rt", c))
                for s in range(B):
                    for k in range(KC):
                        last = pe.matmul(bank[:, s * E:(s + 1) * E], lT[:, k, s * P:(s + 1) * P], router_w[:, k, :],
                                         start=(k == 0), stop=(k == KC - 1))
                last.then_inc(unit_done, 1)

            turn_tokens(("uT", 0), ("c", 0), un)
            pe.wait_ge(ctx_t_loaded, 16 * KC * B)
            pe.wait_ge(ctx_n_loaded, 16 * 2 * B)
            pe.wait_ge(wd_loaded, 48)
            for i in range(NSTEP):
                c, phase = divmod(i, B)
                if i < NT:
                    context_scores(i)
                if phase == 3 and 0 <= c - 2 < TB:
                    project_out(c - 2)
                if 1 <= i <= NT:
                    context_turn(i - 1)
                if 2 <= i <= NT + 1:
                    context_values(i - 2)
                if phase == 2 and 0 <= c - 1 < TB:
                    turn_tokens(("dT", c - 1), ("d", c - 1), dn)
                if phase == 2 and 0 <= c - 2 < TB:
                    turn_attention(c - 2)
                if phase == 3 and c + 1 < TB:
                    turn_tokens(("uT", c + 1), ("c", c + 1), un)
                if phase == 3 and 0 <= c - 1 < TB:
                    project_qkv(c - 1)
                if phase == 0 and 0 <= c - 3 < TB:
                    turn_tokens(("lT", c - 3), ("l", c - 3), l_n)
                if phase == 1 and 0 <= c - 3 < TB:
                    router2(c - 3)
            context_values(NT - 1)
            router2(TB - 3)
            turn_tokens(("dT", TB - 1), ("d", TB - 1), dn)
            project_qkv(TB - 1)
            for c in (TB - 2, TB - 1):
                turn_attention(c)
                project_out(c)
            for c in (TB - 2, TB - 1):
                turn_tokens(("lT", c), ("l", c), l_n)
                router2(c)

            pe.wait_ge(picks2_ready, 1)
            bank = ring.take(pe, ("rank2", 0))
            pe.matmul(bank[:, 0:NT * E], before[:, :], chosen[:, :, :].rearrange("p t e -> p (t e)"), start=True, stop=False)
            pe.matmul(bank[:, 0:NT * E], ones16[:, :], earlier[:, 0:NT, :].rearrange("p t e -> p (t e)"),
                      start=False, stop=True).then_inc(unit_done, 1)
            pe.wait_ge(hots2_ready, 1)
            pe.wait_ge(rowhot2_ready, 1)
            slot_sources(("source", 1), NSLOT1)

            def expert_turn(e):
                for k in range(KC):
                    bank = ring.take(pe, ("eT", e, k))
                    for r in range(RT1):
                        s, n = e * RT1 + r, min(P, CAP1 - r * P)
                        if k == 0:
                            pe.wait_ge(gathered2[s % NXG1], 16 * (s // NXG1 + 1))
                        last = pe.transpose(bank[:, r * P:r * P + n], xg2[0:n, s % NXG1, k * P:(k + 1) * P], ident[0:n, 0:n])
                    last.then_inc(unit_done, 1)

            def expert_up(e):
                for k in range(KC):
                    ring.wait_evacuated(pe, ("eT", e, k))
                pe.wait_ge(w1_low, e + 1)
                pe.wait_ge(w_loaded[e % NW], 32 * (e // NW + 1))
                for f in range(FC1):
                    bank = ring.take(pe, ("h1", e, f))
                    n = 0
                    for k in range(KC):
                        for wp, ep in ((0, 0), (0, 1), (1, 0)):
                            last = pe.matmul(bank[:, 0:CAP1], w1_parts[:, e % 2, wp, k * F1 + f * P:k * F1 + (f + 1) * P],
                                             eT_parts[:, e % 2, ep, k, :], start=(n == 0), stop=(n == 3 * KC - 1))
                            n += 1
                    last.then_inc(unit_done, 1)

            def expert_down(e):
                pe.wait_ge(w2_low, e + 1)
                first = True
                for j, (at_expert, parts) in enumerate(down_units):
                    if at_expert != e:
                        continue
                    bank = ring.take(pe, ("h2", j))
                    for f in range(FC1):
                        if first:
                            pe.wait_ge(h1_low, FC1 * e + f + 1)
                        if len(parts) == 1:
                            on, ex, row0 = parts[0]
                            for hp, wp in ((0, 0), (0, 1), (1, 0)):
                                last = pe.matmul(bank[:, 0:D], h1_parts[:, e % 2, hp, f, row0:row0 + P],
                                                 w2_parts[:, e % 2, wp, f * D:(f + 1) * D], start=(f == 0 and hp + wp == 0),
                                                 stop=(f == FC1 - 1 and hp == 1))
                            continue
                        for on, ex, row0 in parts:
                            last = pe.matmul(bank[on, 0:D], h1[:, ex % 2, f, row0:row0 + on.stop - on.start], w2[:, ex % NW, f, :],
                                             start=(f == 0), stop=(f == FC1 - 1), skip_group_check=True)
                    first = False
                    last.then_inc(unit_done, 1)

            expert_turn(0)
            for e in range(E):
                expert_up(e)
                if e + 1 < E:
                    expert_turn(e + 1)
                expert_down(e)

        @block.sync
        def _(sp):
            for b in range(B):
                sp.dma_start(x[:, TB * b:TB * b + TB, :], a["x"][b].rearrange("(t p) d -> p t d", p=P)).then_inc(x_loaded[b], 16)
                if b == 0:
                    sp.dma_start(cols[:, :], a["cols"]).then_inc(small_loaded, 16)
                    sp.dma_start(rows[:, :], a["rows"]).then_inc(small_loaded, 16)
                    sp.dma_start(mask8[:, :], a["mask"]).then_inc(small_loaded, 16)

            def load_ctx(c):
                if c >= 2:
                    g = (c - 2) // 2 * 3 + (c - 2) % 2 + 1
                    sp.wait_ge(ln_applied, ln_at[g] + 1)
                sp.dma_start(ctx_in[:, c % 2, :, :],
                             a["ctx"][c // 2, (c % 2) * S:(c % 2 + 1) * S, :].rearrange("(t p) d -> p t d", p=P)).then_inc(ctx_loaded[c % 2], 16)

            def store_normalized(b):
                sp.wait_ge(ln_applied, ln_at["h", b] + 1)
                sp.dma_start(h_rows[b * S:(b + 1) * S, :].rearrange("(t p) d -> p t d", p=P), hn[:, 0, :, :]).then_inc(hn_stored, 16)

            load_ctx(0)
            load_ctx(1)
            sp.dma_start(gate_w[:, :, :], a["gate_w"]).then_inc(wb_loaded, 16)
            sp.dma_start(sh_gu[:, :, :], a["sh_gu"]).then_inc(wb_loaded, 16)
            sp.dma_start(sh_dn[:, :], a["sh_dn"]).then_inc(wb_loaded, 16)
            sp.dma_start(qkv_w[:, :, :], a["qkv_w"]).then_inc(wd_loaded, 16)
            sp.dma_start(proj_w[:, :, :], a["proj_w"]).then_inc(wd_loaded, 16)
            sp.dma_start(router_w[:, :, :], a["router_w"]).then_inc(wd_loaded, 16)
            for b in range(B):
                if b + 1 < B:
                    load_ctx(2 * b + 2)
                    load_ctx(2 * b + 3)
                if b:
                    store_normalized(b - 1)
            store_normalized(B - 1)
            ring.wait_done(sp, ("wo", B - 1, 1))
            sp.dma_start(e_gu[:, :, :, :], a["e_gu"]).then_inc(e_loaded, 16)
            sp.dma_start(e_dn[:, :, :], a["e_dn"]).then_inc(e_loaded, 16)
            for s in range(NSLOT0):
                ring.wait_evacuated(sp, ("y", s))
                sp.dma_start(y_rows[s * P:(s + 1) * P, :], ysb[:, s % 3, :]).then_inc(y_stored[s % 3], 16)
                if s % 2 == 0 and s // 2 < KC * B:
                    b, k = divmod(s // 2, KC)
                    sp.dma_start(ctx_t[:, k, b, :], a["ctxT"][:, k, b, :]).then_inc(ctx_t_loaded, 16)
                elif s % 2 == 0 and s // 2 < KC * B + 2 * B:
                    b, half = divmod(s // 2 - KC * B, 2)
                    sp.dma_start(ctx_n[:, b, half * 4:half * 4 + 4, :],
                                 a["ctx"][b, half * 512:half * 512 + 512, :].rearrange("(t p) d -> p t d", p=P)).then_inc(ctx_n_loaded, 16)

            sp.wait_ge(zeros_made, 1)
            sp.dma_start(y_choices[0:2 * NT * P, :].rearrange("(t p) d -> p t d", p=P), bc(zeros[:, :], 1, 2 * NT)).then_inc(zeros_stored, 16)

            def load_expert(e):
                if e == 0:
                    ring.wait_done(sp, ("co", NT - 1))
                if e >= NW:
                    ring.wait_done(sp, ("h2", last_down(e - NW)))
                sp.dma_start(w1[:, e % NW, :, :], a["w1"][e]).then_inc(w_loaded[e % NW], 16)
                sp.dma_start(w2[:, e % NW, :, :], a["w2"][e]).then_inc(w_loaded[e % NW], 16)

            for c in range(TB):
                if c == TB - 1:
                    for e in range(NW):
                        load_expert(e)
                sp.wait_ge(ln_applied, ln_at["l", c] + 1)
                sp.dma_start(l_rows.rearrange("(s c p) d -> p s c d", s=B, c=TB)[:, :, c, :], l_n[:, :, :]).then_inc(l_stored, 16)
            loaded = NW
            for j in range(len(down_units)):
                while loaded < E and last_down(loaded - NW) <= j:
                    load_expert(loaded)
                    loaded += 1
            for i in range(3):
                sp.wait_ge(y2_scattered[i], 16 * len(range(i, len(down_units), 3)))
            for t in range(NT):
                sp.dma_start(y_both[:, t, :, :],
                             y_choices[0:2 * NT * P, :].rearrange("(k t p) d -> p t k d", k=2, p=P)[:, t]).then_inc(y_both_loaded[t], 16)
            for t in range(NT):
                sp.wait_ge(finished, t + 1)
                sp.dma_start(out[t // TB, t % TB * P:(t % TB + 1) * P, :], x[:, t, :]).then_inc(out_stored, 16)
            sp.wait_ge(out_stored, 16 * NT)

        @block.gpsimd
        def _(pool):
            count = [0]

            def link(ins):
                count[0] += 1
                ins.then_inc(pool_step, 1)
                pool.wait_ge(pool_step, count[0])

            link(pool.memset(ident[:, :], 0.0))
            link(pool.affine_select(out=ident[:, :], in_=ident[:, :], compare_op=ALU.not_equal, fill=1.0, base=0,
                                    pattern=[[-1, P]], channel_multiplier=1))
            pool.memset(ones[:, :], 1.0)
            pool.memset(ones16[:, :], 1.0)
            pool.memset(zero16[:, :], 0.0)
            pool.memset(earlier[:, 0, :], 0.0)
            link(pool.memset(headsel[:, :], 1.0))
            link(pool.affine_select(out=headsel[:, 0:1], in_=headsel[:, 0:1], compare_op=ALU.is_gt, fill=0.0, base=DH0,
                                    pattern=[[0, 1]], channel_multiplier=-1))
            link(pool.affine_select(out=headsel[:, 1:2], in_=headsel[:, 1:2], compare_op=ALU.is_ge, fill=0.0, base=-DH0,
                                    pattern=[[0, 1]], channel_multiplier=1))
            link(pool.affine_select(out=before[:, :], in_=ones16[:, :], compare_op=ALU.is_gt, fill=0.0, base=0,
                                    pattern=[[1, P]], channel_multiplier=-1))
            pool.iota(iota[:, :], pattern=[[1, P]], base=0, channel_multiplier=0, allow_small_or_imprecise_dtypes=True)
            pool.iota(iota16[:, :], pattern=[[1, P]], base=0, channel_multiplier=0, allow_small_or_imprecise_dtypes=True)
            pool.iota(token16[:, :, :], pattern=[[P, NT], [0, 2]], base=0, channel_multiplier=1, allow_small_or_imprecise_dtypes=True)
            pool.iota(thresholds[:, :], pattern=[[P, E]], base=0, channel_multiplier=0, allow_small_or_imprecise_dtypes=True).then_inc(consts_made, 1)

            def add_bias(b):
                pool.wait_ge(ln_applied, ln_at[3 * b] + 1)
                pool.wait_ge(small_loaded, 48)
                xs = x[:, TB * b:TB * b + TB, :]
                pool.tensor_tensor(xs, xs, bc(row("b_out"), 1, TB), ALU.add).then_inc(bias_added, 1)

            def queries_twice(b):
                pool.wait_ge(rq_ready, b + 1)
                if b:
                    ring.wait_done(pool, ("qT", b - 1, H0 - 1))
                pool.tensor_tensor(qdup[:, :, 1, :], qn[:, :, :].rearrange("p t (h e) -> p (t h) e", h=H0),
                                   bc(rq[:, :], 2, DH0), ALU.mult).then_inc(qdup_ready, 1)

            def row_onehots(b):
                pool.wait_ge(rrow_ready, b + 1)
                for t in range(TB * b, TB * b + TB):
                    for k in range(2):
                        last = pool.tensor_scalar(rowhot[:, t, k, :], iota[:, :], rrow[:, t, k:k + 1], None, ALU.is_equal)
                last.then_inc(rowhot_ready, 1)

            add_bias(0)
            for b in range(B):
                queries_twice(b)
                if b + 1 < B:
                    add_bias(b + 1)
                if b:
                    row_onehots(b - 1)
            for t in range(NT):
                ring.wait_evacuated(pool, ("sgu", t))
                if t >= 2:
                    ring.wait_done(pool, ("smT", t - 2))
                pool.tensor_tensor(mid[:, t % 2, :], silu[:, t % 2, :], up[:, t % 2, :], ALU.mult).then_inc(shared_mid, 1)
                if t >= 2:
                    add_shared(pool, t - 2)
            for t in (NT - 2, NT - 1):
                add_shared(pool, t)
            pool.wait_ge(slots_ready, 1)
            pool.wait_ge(hn_stored, 16 * B)
            for s in range(NSLOT0):
                if s >= NXG:
                    ring.wait_done(pool, ("xgT", s - NXG))
                pool.indirect_dma_start(xg[:, s % NXG, :], None, h_rows,
                                        bass.IndirectOffsetOnAxis(ap=source[:, s:s + 1], axis=0)).then_inc(gathered[s % NXG], 16)
            for i in range(3):
                pool.wait_ge(y_stored[i], 16 * len(range(i, NSLOT0, 3)))

            def gather_results(n):
                if n >= NYG + B:
                    pool.wait_ge(combined_later, n - NYG - B + 1)
                elif n >= NYG:
                    pool.wait_ge(combined, n - NYG + 1)
                for k in range(2):
                    pool.indirect_dma_start(yg[:, n % NYG, k, :], None, y_rows,
                                            bass.IndirectOffsetOnAxis(ap=slot_u[:, tile_of(n), k:k + 1], axis=0)).then_inc(y_gathered[n % NYG], 16)

            for n in range(B):
                gather_results(n)
            pool.iota(dump_row[:, :], pattern=[[P, NSLOT1]], base=2 * NT * P + 1, channel_multiplier=1, allow_small_or_imprecise_dtypes=True)
            pool.memset(zeros[:, :], 0.0).then_inc(zeros_made, 1)

            def add_hidden(c):
                pool.wait_ge(ln_applied, ln_at["l", c] + 1)
                pool.tensor_tensor(x[:, c:NT:TB, :], x[:, c:NT:TB, :], hid[:, c % 2, :, :], ALU.add).then_inc(x3_done, 1)

            for n in range(B, NT + 2):
                if n < NT:
                    gather_results(n)
                if n >= B + 2:
                    combine(pool, link, n - 2)
            for c in range(TB):
                attend_values(pool, link, c, VALUES_POOL[c], value_prod, att_done_pool)
                if c < TB - 2:
                    add_hidden(c)
            add_hidden(TB - 2)
            add_hidden(TB - 1)
            pool.wait_ge(rrow2_ready, 1)
            for t in range(NT_DVE, NT):
                for k in range(2):
                    last = pool.tensor_scalar(rowhot[:, t, k, :], iota[:, :], rrow[:, t, k:k + 1], None, ALU.is_equal)
            last.then_inc(rowhot2_ready, 1)
            pool.wait_ge(slots2_ready, 1)
            pool.wait_ge(l_stored, 16 * TB)

            def gather_rows(e):
                for s in range(e * RT1, (e + 1) * RT1):
                    if s >= NXG1:
                        ring.wait_done(pool, ("eT", (s - NXG1) // RT1, KC - 1))
                    n = min(P, CAP1 - s % RT1 * P)
                    pool.indirect_dma_start(xg2[0:n, s % NXG1, :], None, l_rows,
                                            bass.IndirectOffsetOnAxis(ap=source[0:n, s:s + 1], axis=0)).then_inc(gathered2[s % NXG1], 16)

            for e in range(GATHER_AHEAD):
                gather_rows(e)
            pool.wait_ge(zeros_stored, 16)
            pool.wait_ge(y_to_ready, 1)
            for e in range(E):
                if e + GATHER_AHEAD < E:
                    gather_rows(e + GATHER_AHEAD)
                for j, (at_expert, parts) in enumerate(down_units):
                    if at_expert == e:
                        ring.wait_evacuated(pool, ("h2", j))
                        pool.indirect_dma_start(y_choices, bass.IndirectOffsetOnAxis(ap=y_to[:, j:j + 1], axis=0),
                                                y2[:, j % 3, :], None).then_inc(y2_scattered[j % 3], 16)

        @block.scalar
        def _(act):
            act.dma_start(wkv[:, :, :], a["wkv"]).then_inc(wa_loaded, 16)
            act.dma_start(wq[:, :, :], a["wq"]).then_inc(wa_loaded, 16)
            act.dma_start(wout[:, :, :], a["wout"]).then_inc(wa_loaded, 16)
            act.wait_ge(small_loaded, 48)

            def evac_turned(g):
                ring.wait_done(act, ("xT", g, 1))
                n = "ln_l" if g % 3 == 0 else "ln_x"
                if g >= 2:
                    ring.wait_done(act, ("v", g - 2, 1))
                act.activation(xnT[:, g % 2, 1, :], ring.bank(("xT", g, 1)), ACT.Identity, bias=col(n + "_b1"),
                               scale=col(n + "_g1")).then_inc(ring.evacuated(("xT", g, 1)), 1)

            def keys(g):
                b, gg = divmod(g, 3)
                for p in range(NPAIR):
                    bank = ring.bank(("kT", g, p))
                    ring.wait_done(act, ("kT", g, p))
                    if g:
                        ring.wait_done(act, ("ss", g - 1))
                    if gg == 0 and b:
                        ring.wait_done(act, ("s", b - 1, NPAIR - 1, KT0 - 1, 1))
                    act.activation(ksq[:, p, :], bank, ACT.Square)
                    span = slice(gg * S, (gg + 1) * S)
                    act.activation(kstack[0:DH0, 2 * p, span], bank[0:DH0, :], ACT.Copy)
                    act.activation(kstack[DH0:P, 2 * p + 1, span], bank[DH0:P, :], ACT.Copy).then_inc(khi_ready, 1)

            def copies(key, dst):
                ring.wait_done(act, key)
                act.activation(dst, ring.bank(key), ACT.Copy).then_inc(ring.evacuated(key), 1)

            def copies_part(key, dst, n):
                ring.wait_done(act, key)
                act.activation(dst, ring.bank(key)[:, 0:n], ACT.Copy).then_inc(ring.evacuated(key), 1)

            def values(g):
                b, gg = divmod(g, 3)
                if gg == 0 and b:
                    act.wait_ge(pv_done, step(b, 0, 0))
                for i in range(2):
                    copies(("v", g, i), vals[:, gg * TB + 2 * i:gg * TB + 2 * i + 2, :].rearrange("p t d -> p (t d)"))

            def queries(b):
                if b:
                    act.wait_ge(qdup_ready, 2 * b)
                for i in range(2):
                    copies(("q", 3 * b, i), qn[:, 2 * i:2 * i + 2, :].rearrange("p t d -> p (t d)"))

            def query_high(b):
                if b:
                    ring.wait_done(act, ("s", b - 1, NPAIR - 1, KT0 - 1, 1))
                for h in range(H0):
                    ring.wait_done(act, ("qT", b, h))
                    act.activation(qhi[:, h, :], ring.bank(("qT", b, h)), ACT.Copy, scale=gqk[:, :]).then_inc(qhi_ready, 1)

            def exps(b, p, j):
                n = step(b, p, j)
                if n >= 3:
                    act.wait_ge(pv_done, n - 2)
                    act.wait_ge(psums_added, n - 2)
                if p == 0 and j % TB == 0:
                    act.wait_ge(rkey_ready, 3 * b + j // TB + 1)
                for h in range(2):
                    key = ("s", b, p, j, h)
                    ring.wait_done(act, key)
                    act.activation(probs[:, n % 3, h, :], ring.bank(key), ACT.Exp,
                                   bias=lbias[:, :] if j < TB else mbias[:, b, j - TB:j - TB + 1],
                                   scale=rkey[:, b % 2, j, 2 * p + h:2 * p + h + 1]).then_inc(ring.evacuated(key), 1)

            def expert_norm_turned(b):
                for k in range(KC):
                    copies(("hT", b, k), hT[:, k, b * S:(b + 1) * S])

            def router_exp(b):
                key = ("gate", b)
                ring.wait_done(act, key)
                if b:
                    act.wait_ge(picks_ready, b)
                act.activation(rexp[:, :], ring.bank(key)[:, 0:TB * E], ACT.Exp, scale=-1.0).then_inc(ring.evacuated(key), 1)

            def shared_step(i):
                if i < NT:
                    key = ("sgu", i)
                    ring.wait_done(act, key)
                    if i >= 2:
                        act.wait_ge(shared_mid, i - 1)
                    act.activation(up[:, i % 2, :], ring.bank(key)[:, M0:2 * M0], ACT.Copy)
                    act.activation(silu[:, i % 2, :], ring.bank(key)[:, 0:M0], ACT.Silu).then_inc(ring.evacuated(key), 1)
                if 1 <= i <= NT:
                    t = i - 1
                    if t >= 2:
                        ring.wait_done(act, ("sy", t - 2))
                    copies_part(("smT", t), midT[:, t % 2, :], P)
                if i >= 2:
                    t = i - 2
                    if t >= 2:
                        act.wait_ge(shared_added, t - 1)
                    copies_part(("sy", t), ysb[:, t % 2, :], D)

            evac_turned(0)
            for b in range(B):
                g = 3 * b
                if b == 0:
                    keys(g)
                queries(b)
                values(g)
                if b == 0:
                    evac_turned(g + 1)
                    act.wait_ge(exp_consts_ready, 1)
                evac_turned(g + 2)
                keys(g + 1)
                values(g + 1)
                query_high(b)
                keys(g + 2)
                values(g + 2)
                if b + 1 < B:
                    evac_turned(g + 3)
                for p in range(NPAIR):
                    for j in range(KT0):
                        exps(b, p, j)
                        if j == 6 and p == 0 and b:
                            expert_norm_turned(b - 1)
                        if j == 8 and p == 0 and b:
                            router_exp(b - 1)
                if b + 1 < B:
                    evac_turned(g + 4)
                    keys(g + 3)
            for i in range(6):
                shared_step(i)
            expert_norm_turned(B - 1)
            router_exp(B - 1)

            for i in range(6, NT + 2):
                shared_step(i)
            for i in range(NSLOT0 + 3):
                if 1 <= i <= NSLOT0:
                    s = i - 1
                    key = ("gu", s)
                    ring.wait_done(act, key)
                    if s >= 2:
                        ring.wait_evacuated(act, ("gu", s - 2))
                    act.activation(silu[:, s % 2, :], ring.bank(key)[:, 0:M0], ACT.Silu).then_inc(silu_ready, 1)
                if i >= 3:
                    s = i - 3
                    if s >= 3:
                        act.wait_ge(y_stored[s % 3], 16 * (s // 3))
                    if s == 0:
                        act.wait_ge(shared_added, NT)
                    copies_part(("y", s), ysb[:, s % 3, :], D)

            for k in range(KC):
                copies(("uT", 0, k), uT[:, k, :])
            def attention_exp(c):
                act.wait_ge(att_diff, c + 1)
                if c:
                    wait_values(act, c - 1)
                act.activation(att_e[:, :, :, :].rearrange("p s h k -> p (s h k)"), att_d[:, :, :, :].rearrange("p s h k -> p (s h k)"),
                               ACT.Exp, scale=DH1 ** -0.5).then_inc(att_exp, 1)

            def tokens_turned(c):
                for k in range(KC):
                    key = ("dT", c, k)
                    if c:
                        ring.wait_done(act, ("qkv", c - 1, B - 1))
                    ring.wait_done(act, key)
                    act.activation(dT[:, k, :], ring.bank(key), ACT.Identity, bias=col(f"ln1_b{k}"),
                                   scale=col(f"ln1_w{k}")).then_inc(ring.evacuated(key), 1)

            def attention_turned(c):
                for k in range(KC):
                    if c:
                        ring.wait_done(act, ("po", c - 1, 1))
                    copies(("oT", c, k), oT[:, k, :])

            def qkv_rows(c):
                if 0 < c < TB - 1:
                    wait_values(act, c - 1)
                for s in range(B):
                    copies_part(("qkv", c, s), qkv_of(c)[:, s, :], QKV)

            def routed_turned(c):
                for k in range(KC):
                    if c:
                        ring.wait_done(act, ("rt", c - 1))
                    copies(("lT", c, k), lT[:, k, :])

            def router2_exp(c):
                act.wait_ge(rl_diff, c + 1)
                act.activation(rl[:, 1, :, :].rearrange("p s e -> p (s e)"), rl[:, 0, :, :].rearrange("p s e -> p (s e)"),
                               ACT.Exp).then_inc(rl_exp, 1)

            for i in range(NSTEP):
                c, phase = divmod(i, B)
                if phase == 1 and 0 <= c - 2 < TB:
                    attention_exp(c - 2)
                if i < NT:
                    if i >= 2:
                        ring.wait_done(act, ("cp", i - 2, 1))
                        if i >= 3:
                            act.wait_ge(x2_done, i - 2)
                    act.wait_ge(cmax_ready, i + 1)
                    for half in range(2):
                        key = ("cs", i, half)
                        act.activation(cprob[:, i % 2, half * 512:(half + 1) * 512], ring.bank(key), ACT.Exp,
                                       bias=cmax[:, i % 2, 3:4], scale=CSCALE,
                                       accum_out=csum[:, i % 3, half:half + 1]).then_inc(ring.evacuated(key), 1)
                if 1 <= i <= NT:
                    if i >= 3:
                        ring.wait_done(act, ("co", i - 3))
                    for half in range(2):
                        copies(("cp", i - 1, half), cprobT[:, (i - 1) % 2, half * 512:half * 512 + 512])
                if phase == 2 and 0 <= c - 1 < TB:
                    tokens_turned(c - 1)
                if phase == 2 and 0 <= c - 2 < TB:
                    attention_turned(c - 2)
                if phase == 3 and c + 1 < TB:
                    for k in range(KC):
                        ring.wait_done(act, ("cs", i, 1))
                        copies(("uT", c + 1, k), uT[:, k, :])
                if phase == 3 and 0 <= c - 1 < TB:
                    qkv_rows(c - 1)
                if phase == 0 and 0 <= c - 3 < TB:
                    routed_turned(c - 3)
                if phase == 2 and 0 <= c - 3 < TB:
                    router2_exp(c - 3)
            tokens_turned(TB - 1)
            qkv_rows(TB - 1)
            attention_exp(TB - 2)
            router2_exp(TB - 3)
            attention_exp(TB - 1)
            attention_turned(TB - 2)
            attention_turned(TB - 1)
            for c in (TB - 2, TB - 1):
                routed_turned(c)
                router2_exp(c)

            def weights_high(e):
                if e >= 2:
                    ring.wait_done(act, ("h1", e - 2, FC1 - 1))
                act.wait_ge(w_loaded[e % NW], 32 * (e // NW + 1))
                act.activation(w1_parts[:, e % 2, 0, :], w1[:, e % NW, :, :].rearrange("p k f -> p (k f)"), ACT.Copy).then_inc(w1_high, 1)

            def expert_turned(e):
                if e >= 2:
                    ring.wait_done(act, ("h1", e - 2, FC1 - 1))
                for k in range(KC):
                    ring.wait_done(act, ("eT", e, k))
                    act.activation(eT_parts[:, e % 2, 0, k, :], ring.bank(("eT", e, k))[:, 0:CAP1], ACT.Copy).then_inc(eT_high, 1)

            weights_high(0)
            expert_turned(0)
            for e in range(E):
                if e >= 2:
                    ring.wait_done(act, ("h2", last_down(e - 2)))
                act.activation(w2_parts[:, e % 2, 0, :], w2[:, e % NW, :, :].rearrange("p f d -> p (f d)"), ACT.Copy).then_inc(w2_high, 1)
                for j in range(FC1):
                    key = ("h1", e, j)
                    ring.wait_done(act, key)
                    act.activation(h1[:, e % 2, j, :], ring.bank(key)[:, 0:CAP1], ACT.Gelu_apprx_tanh).then_inc(ring.evacuated(key), 1)
                    ring.wait_evacuated(act, key)
                    act.activation(h1_parts[:, e % 2, 0, j, :], h1[:, e % 2, j, :], ACT.Copy).then_inc(h1_high, 1)
                if e + 1 < E:
                    expert_turned(e + 1)
                    weights_high(e + 1)

        @block.vector
        def _(dve):
            count = [0]
            turn = [0]

            def link(ins):
                count[0] += 1
                ins.then_inc(dve_step, 1)
                dve.wait_ge(dve_step, count[0])

            def rsqrt(dst, var, n, scale, floor, add):
                v, t, y = (nwt[:, turn[0], i, 0:n] for i in range(3))
                turn[0] ^= 1
                link(dve.tensor_scalar(v, var, scale, floor, ALU.mult, ALU.add if add else ALU.max))
                link(dve.tensor_scalar(y.bitcast(I32), v.bitcast(I32), -0.5, RSQRT_SEED, ALU.mult, ALU.add))
                for i in range(3):
                    link(dve.tensor_tensor(t, y, y, ALU.mult))
                    link(dve.scalar_tensor_tensor(t, t, -0.5, v, ALU.mult, ALU.mult))
                    last = dve.scalar_tensor_tensor(dst if i == 2 else y, t, 1.5, y, ALU.add, ALU.mult)
                    if i < 2:
                        link(last)
                return last

            def normalize(key):
                i = ln_at[key]
                if isinstance(key, tuple) and key[0] == "l":
                    src = hid[:, key[1] % 2, :, :]
                elif isinstance(key, tuple) and key[0] != "h":
                    src = x[:, key[1]:NT:TB, :]
                elif isinstance(key, tuple):
                    src = x[:, TB * key[1]:TB * key[1] + TB, :]
                elif key % 3 == 0:
                    b = key // 3
                    dve.wait_ge(x_loaded[b], 16)
                    src = x[:, TB * b:TB * b + TB, :]
                else:
                    b, gg = divmod(key, 3)
                    dve.wait_ge(ctx_loaded[gg - 1], 16 * (b + 1))
                    src = ctx_in[:, gg - 1, :, :]
                if key != ("c", 0):
                    for t in range(TB):
                        last = dve.bn_stats(st[:, t, :], src[:, t, :])
                    link(last)
                for t in range(TB):
                    last = dve.bn_aggr(mv[:, i % 4, t, :], st[:, t, :])
                link(last)
                var, r = mv[:, i % 4, :, 1], rstd[:, i % 4, :]
                if isinstance(key, tuple) and key[0] == "d" or not isinstance(key, tuple) and key % 3 == 0:
                    link(rsqrt(r, var, TB, 1.0, 1e-5, True))
                    t = lnt[:, 0, :]
                    if isinstance(key, tuple):
                        dve.tensor_copy(hid_rstd[:, :], r)
                    link(dve.tensor_tensor(t, r, r, ALU.mult))
                    link(dve.tensor_tensor(t, t, var, ALU.mult))
                    link(rsqrt(lnt[:, 1, :], t, TB, 1.0, 1e-5, True))
                    link(dve.tensor_tensor(r, r, lnt[:, 1, :], ALU.mult))
                else:
                    link(rsqrt(r, var, TB, 1.0, 1e-5, True))
                kind = key[0] if isinstance(key, tuple) else "a"
                if kind == "a":
                    if key >= 2:
                        ring.wait_done(dve, ("xT", key - 2, 1))
                    dst = xn[:, key % 2, :, :]
                elif kind == "h":
                    dst = hn[:, 0, :, :]
                    if key[1]:
                        dve.wait_ge(hn_stored, 16 * key[1])
                        ring.wait_done(dve, ("hT", key[1] - 1, 1))
                else:
                    c = key[1]
                    dst = {"c": un, "d": dn, "l": l_n}[kind]
                    if key == ("c", 0):
                        ring.wait_done(dve, ("y", NSLOT0 - 1))
                    if c:
                        ring.wait_done(dve, ({"c": "uT", "d": "dT", "l": "lT"}[kind], c - 1, KC - 1))
                        if kind == "l":
                            dve.wait_ge(l_stored, 16 * c)
                for t in range(TB):
                    if kind == "l":
                        last = dve.scalar_tensor_tensor(dst[:, t, :], src[:, t, :], mv[:, i % 4, t, 0:1], row("ln2_w"), ALU.subtract, ALU.mult)
                    else:
                        last = dve.tensor_scalar(dst[:, t, :], src[:, t, :], mv[:, i % 4, t, 0:1], rstd[:, i % 4, t:t + 1],
                                                 ALU.subtract, ALU.mult)
                if kind == "l":
                    link(last)
                    for t in range(TB):
                        last = dve.scalar_tensor_tensor(dst[:, t, :], dst[:, t, :], rstd[:, i % 4, t:t + 1], row("ln2_b"),
                                                        ALU.mult, ALU.add)
                last.then_inc(ln_applied, 1)

            def evac_turned(g):
                key = ("xT", g, 0)
                ring.wait_done(dve, key)
                n = "ln_l" if g % 3 == 0 else "ln_x"
                if g >= 2:
                    ring.wait_done(dve, ("v", g - 2, 1))
                dve.tensor_scalar(xnT[:, g % 2, 0, :], ring.bank(key), col(n + "_g0"), col(n + "_b0"),
                                  ALU.mult, ALU.add).then_inc(ring.evacuated(key), 1)

            def key_low(g):
                gg = g % 3
                span = slice(gg * S, (gg + 1) * S)
                for p in range(NPAIR):
                    bank = ring.bank(("kT", g, p))
                    dve.wait_ge(khi_ready, g * NPAIR + p + 1)
                    dve.tensor_tensor(kstack[DH0:P, 2 * p, span], bank[0:DH0, :],
                                      kstack[0:DH0, 2 * p, span].bitcast(F32), ALU.subtract)
                    dve.tensor_tensor(kstack[0:DH0, 2 * p + 1, span], bank[DH0:P, :],
                                      kstack[DH0:P, 2 * p + 1, span].bitcast(F32),
                                      ALU.subtract).then_inc(ring.evacuated(("kT", g, p)), 1)

            def key_sums(g):
                key = ("ss", g)
                ring.wait_done(dve, key)
                dve.tensor_copy(kss[:, g % 3, :], ring.bank(key)[:, 0:TB * H0]).then_inc(ring.evacuated(key), 1)

            def key_norms(g, n):
                b, gg = divmod(g, 3)
                ring.wait_evacuated(dve, ("ss", g + n - 1))
                dst = rkey[:, b % 2, gg * TB:(gg + n) * TB, :].rearrange("p t h -> p (t h)")
                src = kss[:, gg:gg + n, :].rearrange("p g h -> p (g h)")
                rsqrt(dst, src, n * TB * H0, 1.0 / DH0, 1e-16, False).then_inc(rkey_ready, n)

            def query_norms(b):
                for i in range(2):
                    ring.wait_evacuated(dve, ("q", 3 * b, i))
                link(dve.tensor_tensor(qsq[:, :, :], qn[:, :, :], qn[:, :, :], ALU.mult))
                link(dve.tensor_reduce(ssq[:, :], qsq[:, :, :].rearrange("p t (h e) -> p (t h) e", h=H0), AX.X, ALU.add))
                rsqrt(rq[:, :], ssq[:, :], TB * H0, 1.0 / DH0, 1e-16, False).then_inc(rq_ready, 1)
                dve.wait_ge(rq_ready, b + 1)
                if b:
                    ring.wait_done(dve, ("qT", b - 1, H0 - 1))
                dve.tensor_tensor(qdup[:, :, 0, :], qn[:, :, :].rearrange("p t (h e) -> p (t h) e", h=H0),
                                  bc(rq[:, :], 2, DH0), ALU.mult).then_inc(qdup_ready, 1)

            def query_low(b):
                for h in range(H0):
                    key = ("qT", b, h)
                    dve.wait_ge(qhi_ready, b * H0 + h + 1)
                    dve.scalar_tensor_tensor(qlo[:, h, :], ring.bank(key), gqk[:, 0:1], qhi[:, h, :].bitcast(F32),
                                             ALU.mult, ALU.subtract).then_inc(ring.evacuated(key), 1)

            def add_probs(b, p, j):
                n, m = step(b, p, j), b * NPAIR + p
                for h in range(2):
                    ring.wait_evacuated(dve, ("s", b, p, j, h))
                if j == 0:
                    if m >= 2:
                        ring.wait_done(dve, ("den",) + divmod(m - 2, NPAIR))
                else:
                    dve.wait_ge(psums_added, n)
                src = probs[:, n % 3, :, :].rearrange("p h q -> p (h q)")
                dst = psums[:, m % 2, :]
                if j == 0:
                    dve.tensor_copy(dst, src).then_inc(psums_added, 1)
                else:
                    dve.tensor_tensor(dst, dst, src, ALU.add).then_inc(psums_added, 1)

            def normalize_attention(b, p):
                key, m = ("den", b, p), b * NPAIR + p
                ring.wait_done(dve, key)
                dve.wait_ge(attn_evacuated, m) if m else None
                dve.reciprocal(rden[:, :], ring.bank(key)).then_inc(ring.evacuated(key), 1)
                ring.wait_evacuated(dve, key)
                dve.wait_ge(pv_done, KT0 * (m + 1))
                if b and p == 0:
                    ring.wait_done(dve, ("wo", b - 1, 1))
                dve.tensor_tensor(attnT[:, p, :], acc_psum[:, m % 2, :], rden[:, :], ALU.mult).then_inc(attn_evacuated, 1)

            def add_attention(b):
                dve.wait_ge(bias_added, b + 1)
                for i in range(2):
                    key = ("wo", b, i)
                    ring.wait_done(dve, key)
                    xs = x[:, TB * b + 2 * i:TB * b + 2 * i + 2, :].rearrange("p t d -> p (t d)")
                    dve.tensor_tensor(xs, ring.bank(key), xs, ALU.add).then_inc(ring.evacuated(key), 1)
                for i in range(2):
                    ring.wait_evacuated(dve, ("wo", b, i))

            def choose(b):
                key = ("gate", b)
                ring.wait_evacuated(dve, key)
                flat = score[:, :, :].rearrange("p t e -> p (t e)")
                link(dve.tensor_scalar(flat, rexp[:, :], 1.0, None, ALU.add))
                link(dve.reciprocal(flat, flat))
                for t in range(TB):
                    last = dve.max(top8[:, t, :], score[:, t, :])
                link(last)
                for t in range(TB):
                    last = dve.max_index(idx8[:, t, :], top8[:, t, :], score[:, t, :])
                link(last)
                link(dve.tensor_copy(idxf[:, :, :], idx8[:, :, 0:2]))
                ts = slice(TB * b, TB * b + TB)
                link(dve.tensor_tensor(wtmp[:, :, 0], top8[:, :, 0], top8[:, :, 1], ALU.add))
                link(dve.tensor_scalar(wtmp[:, :, 0], wtmp[:, :, 0], 1e-20, None, ALU.add))
                link(dve.reciprocal(wtmp[:, :, 1], wtmp[:, :, 0]))
                link(dve.scalar_tensor_tensor(weight[:, ts, :], top8[:, :, 0:2], 2.5, bc(wtmp[:, :, 1], 2, 2), ALU.mult, ALU.mult))
                pick_experts(b)

            def pick_experts(b):
                ts = slice(TB * b, TB * b + TB)
                for k in range(2):
                    last = dve.tensor_tensor(pick[:, k, ts, :], bc(iota[:, 0:E], 1, TB), bc(idxf[:, :, k], 2, E), ALU.is_equal)
                link(last)
                link(dve.tensor_tensor(chosen[:, ts, :], pick[:, 0, ts, :], pick[:, 1, ts, :], ALU.add))
                for t in range(TB * b, TB * b + TB):
                    last = dve.tensor_tensor(earlier[:, t + 1, :], earlier[:, t, :], chosen[:, t, :], ALU.add)
                    if t < TB * b + TB - 1:
                        link(last)
                last.then_inc(picks_ready, 1)

            def place_choices(b):
                key = ("rank", b)
                ts = slice(TB * b, TB * b + TB)
                ring.wait_done(dve, key)
                counted = ring.bank(key)[:, 0:TB * E].rearrange("p (t e) -> p t e", e=E)
                for k in range(2):
                    tmp = ptmp[:, k * TB:(k + 1) * TB, :]
                    ins = dve.tensor_tensor(tmp, pick[:, k, ts, :], counted, ALU.mult)
                    if k == 1 and b < B - 1:
                        ins.then_inc(ring.evacuated(key), 1)
                        ring.wait_evacuated(dve, key)
                    else:
                        link(ins)
                    link(dve.tensor_reduce(rank[:, ts, k], tmp, AX.X, ALU.add))
                if b == B - 1:
                    dve.tensor_copy(etiles[:, 0, :], ring.bank(key)[:, TB * E:(TB + 1) * E]).then_inc(ring.evacuated(key), 1)
                link(dve.tensor_copy(rank_i[:, ts, :], rank[:, ts, :]))
                link(dve.tensor_scalar(part_i[:, ts, :], rank_i[:, ts, :], P - 1, None, ALU.bitwise_and))
                link(dve.tensor_copy(rrow[:, ts, :], part_i[:, ts, :]))
                link(dve.tensor_scalar(part_i[:, ts, :], rank_i[:, ts, :], P.bit_length() - 1, None, ALU.arith_shift_right))
                dve.tensor_copy(rtile[:, ts, :], part_i[:, ts, :]).then_inc(rrow_ready, 1)

            normalize(0)
            dve.wait_ge(small_loaded, 48)
            dve.wait_ge(consts_made, 1)
            evac_turned(0)
            normalize(1)
            link(dve.tensor_tensor(gqk[:, :], col("gamma_q"), col("gamma_k"), ALU.mult))
            link(dve.tensor_scalar(gqk[:, :], gqk[:, :], DH0 ** -0.5, None, ALU.mult))
            link(dve.tensor_tensor(gbound[:, 0:DH0], row("gamma_q"), row("gamma_k"), ALU.mult))
            link(dve.tensor_reduce(gbound[:, DH0:DH0 + 1], gbound[:, 0:DH0], AX.X, ALU.max, apply_absolute_value=True))
            link(dve.tensor_scalar(gbound[:, DH0 + 1:DH0 + 2], gbound[:, DH0:DH0 + 1], -(DH0 ** 0.5), 80.0, ALU.mult, ALU.add))
            link(dve.tensor_scalar(lbias[:, :], gbound[:, DH0 + 1:DH0 + 2], 0.0, None, ALU.min))
            flat = mbias[:, :, :].rearrange("p b t -> p (b t)")
            link(dve.tensor_scalar(flat, mask8[:, :].bitcast(U8), BIG, -BIG, ALU.mult, ALU.add))
            dve.tensor_scalar(flat, flat, lbias[:, 0:1], None, ALU.add).then_inc(exp_consts_ready, 1)
            for b in range(B):
                g = 3 * b
                normalize(g + 2)
                if b == 0:
                    key_low(g)
                query_norms(b)
                if b == 0:
                    evac_turned(g + 1)
                evac_turned(g + 2)
                key_sums(g)
                key_low(g + 1)
                query_low(b)
                key_sums(g + 1)
                if b + 1 < B:
                    normalize(g + 3)
                key_low(g + 2)
                key_norms(g, 2)
                if b + 1 < B:
                    evac_turned(g + 3)
                key_sums(g + 2)
                key_norms(g + 2, 1)
                for p in range(NPAIR):
                    for j in range(KT0):
                        add_probs(b, p, j)
                        if j == 1 and p == 0 and b:
                            normalize(("h", b - 1))
                        if j == 10 and p == 0 and b + 1 < B:
                            normalize(g + 4)
                        if j == 4 and p == 1:
                            normalize_attention(b, 0)
                        if j == 7 and p == 1 and b:
                            choose(b - 1)
                        if j == 11 and p == 1 and b:
                            place_choices(b - 1)
                normalize_attention(b, 1)
                if b + 1 < B:
                    evac_turned(g + 4)
                    key_low(g + 3)
                add_attention(b)
            normalize(("h", B - 1))
            choose(B - 1)
            place_choices(B - 1)

            def one_hots(dst, n, places, tiles=NT):
                return dve.tensor_tensor(dst.rearrange("p t k j -> p (t k) j"), bc(iota16[:, 0:n], 1, 2 * tiles),
                                         bc(places[:, 0:tiles, :].rearrange("p t k -> p (t k)"), 2, n), ALU.is_equal)

            def tile_onehots(n, tokens):
                hot = tilehot[:, :, :, 0:n]
                link(one_hots(hot, n, rtile16))
                return dve.tensor_tensor(hot.rearrange("p t k j -> p (t k) j"), hot.rearrange("p t k j -> p (t k) j"),
                                         bc(tokens[:, :, :].rearrange("p t k -> p (t k)"), 2, n), ALU.mult)

            link(dve.tensor_tensor(ecmp[:, 0:E, :], bc(etiles[:, 0, :], 2, E), bc(thresholds[:, :], 1, E), ALU.is_gt))
            link(dve.tensor_reduce(etiles[:, 1, :], ecmp[:, 0:E, :], AX.X, ALU.add))
            link(dve.tensor_tensor_scan(etiles[:, 2, :], etiles[:, 1, :], zero16[:, :], 0.0, ALU.add, ALU.add))
            link(dve.tensor_tensor(etiles[:, 0, :], etiles[:, 2, :], etiles[:, 1, :], ALU.subtract))
            for k in range(2):
                link(dve.tensor_tensor(ptmp[:, :, :], pick[:, k, :, :], bc(etiles[:, 0, :], 1, NT), ALU.mult))
                link(dve.tensor_reduce(dest_f[:, :, k], ptmp[:, :, :], AX.X, ALU.add))
            link(dve.tensor_tensor(rtile[:, :, :], rtile[:, :, :], dest_f[:, :, :], ALU.add))
            ins = dve.tensor_scalar(dest_f[:, :, :], rtile[:, :, :], float(P), None, ALU.mult)
            link(ins)
            for t in range(TB * (B - 1), NT):
                for k in range(2):
                    last = dve.tensor_scalar(rowhot[:, t, k, :], iota[:, :], rrow[:, t, k:k + 1], None, ALU.is_equal)
            last.then_inc(rowhot_ready, 1)
            link(dve.tensor_copy(rtile16[:, :, :], rtile[:, :, :]))
            last = tile_onehots(NSLOT0, token16)
            last.then_inc(tilehot_ready, 1)
            link(dve.tensor_tensor(ecmp[:, 0:NSLOT0, :], bc(etiles[:, 2, :], 1, NSLOT0), bc(iota[:, 0:NSLOT0], 2, E), ALU.is_le))
            link(dve.tensor_reduce(eslot[:, 0:NSLOT0], ecmp[:, 0:NSLOT0, :], AX.X, ALU.add))
            dve.tensor_scalar(eslot_i[:, 0:NSLOT0], eslot[:, 0:NSLOT0], float(E - 1), None, ALU.min).then_inc(eslot_ready, 1)
            dve.tensor_tensor(slot_u[:, :, :], dest_f[:, :, :], rrow[:, :, :], ALU.add)
            ring.wait_done(dve, ("source", 0))
            dve.tensor_copy(source[:, 0:NSLOT0], ring.bank(("source", 0))[:, 0:NSLOT0]).then_inc(ring.evacuated(("source", 0)), 1)
            ring.wait_evacuated(dve, ("source", 0))
            dve.tensor_copy(eslot[:, 0:1], eslot_i[:, 0:1]).then_inc(slots_ready, 1)

            def copy_out(key, dst, n):
                ring.wait_done(dve, key)
                dve.tensor_copy(dst, ring.bank(key)[:, 0:n]).then_inc(ring.evacuated(key), 1)

            for i in range(NSLOT0 + 3):
                if i < NSLOT0:
                    if i >= 3:
                        ring.wait_done(dve, ("gu", i - 3))
                    copy_out(("xgT", i), xgT[:, i % 3, :], D)
                if 1 <= i <= NSLOT0:
                    s = i - 1
                    key = ("gu", s)
                    dve.wait_ge(silu_ready, s + 1)
                    if s >= 2:
                        ring.wait_done(dve, ("mT", s - 2))
                    dve.tensor_tensor(mid[:, s % 2, :], silu[:, s % 2, :], ring.bank(key)[:, M0:2 * M0],
                                      ALU.mult).then_inc(ring.evacuated(key), 1)
                if 2 <= i <= NSLOT0 + 1:
                    s = i - 2
                    if s >= 2:
                        ring.wait_done(dve, ("y", s - 2))
                    copy_out(("mT", s), midT[:, s % 2, :], P)

            for n in range(B):
                combine(dve, link, n)
                dve.wait_ge(combined, n + 1)
                last = dve.bn_stats(st[:, n, :], x[:, tile_of(n), :])
            link(last)
            normalize(("c", 0))
            link(dve.memset(att_s[:, :, :, :], -BIG))

            def context_max(n):
                if n >= 2:
                    for half in range(2):
                        ring.wait_evacuated(dve, ("cs", n - 2, half))
                for half in range(2):
                    ring.wait_done(dve, ("cs", n, half))
                    last = dve.tensor_reduce(cmax[:, n % 2, half:half + 1], ring.bank(("cs", n, half)), AX.X, ALU.max)
                link(last)
                link(dve.tensor_tensor(cmax[:, n % 2, 2:3], cmax[:, n % 2, 0:1], cmax[:, n % 2, 1:2], ALU.max))
                dve.tensor_scalar(cmax[:, n % 2, 3:4], cmax[:, n % 2, 2:3], -CSCALE, None, ALU.mult).then_inc(cmax_ready, 1)

            def add_context(n):
                t, key = tile_of(n), ("co", n)
                link(dve.tensor_tensor(csum[:, n % 3, 2:3], csum[:, n % 3, 0:1], csum[:, n % 3, 1:2], ALU.add))
                link(dve.reciprocal(csum[:, n % 3, 3:4], csum[:, n % 3, 2:3]))
                ring.wait_done(dve, key)
                dve.scalar_tensor_tensor(x[:, t, :], ring.bank(key)[:, 0:D], csum[:, n % 3, 3:4], x[:, t, :],
                                         ALU.mult, ALU.add).then_inc(ring.evacuated(key), 1)
                ring.wait_evacuated(dve, key)
                dve.tensor_copy(csum[:, n % 3, 2:3], csum[:, n % 3, 3:4]).then_inc(x2_done, 1)

            def attend_scores(c):
                for s in range(B):
                    ring.wait_evacuated(dve, ("qkv", c, s))
                if c:
                    dve.wait_ge(att_diff, c)
                for k in range(B):
                    n = B - k
                    q = qkv_of(c)[:, k:B, 0:H1 * DH1].rearrange("p s (g r d) -> p s g r d", g=KV1, d=DH1)
                    key = bc(bc(qkv_of(c)[:, k, H1 * DH1:(H1 + KV1) * DH1].rearrange("p (g d) -> p g d", d=DH1), 2, H1 // KV1), 1, n)
                    pr = prod[:, 0:n, :].rearrange("p s (g r d) -> p s g r d", g=KV1, d=DH1)
                    for s in range(n):
                        last = dve.tensor_tensor(pr[:, s], q[:, s], key[:, s], ALU.mult)
                    link(last)
                    last = dve.tensor_reduce(att_s[:, k:B, :, k], prod[:, 0:n, :].rearrange("p s (h d) -> p s h d", d=DH1), AX.X, ALU.add)
                    link(last)
                link(dve.tensor_reduce(att_m[:, 0, :, :], att_s[:, :, :, :], AX.X, ALU.max))
                if c:
                    dve.wait_ge(att_exp, c)
                dve.tensor_tensor(att_d[:, :, :, :], att_s[:, :, :, :], bc(att_m[:, 0, :, :], 3, B), ALU.subtract).then_inc(att_diff, 1)

            def attend_weights(c):
                dve.wait_ge(att_exp, c + 1)
                link(dve.tensor_reduce(att_m[:, 1, :, :], att_e[:, :, :, :], AX.X, ALU.add))
                link(dve.reciprocal(att_m[:, 1, :, :], att_m[:, 1, :, :]))
                dve.tensor_tensor(att_e[:, :, :, :], att_e[:, :, :, :], bc(att_m[:, 1, :, :], 3, B), ALU.mult).then_inc(att_weights, 1)

            def start_hidden(c):
                i = ln_at["d", c]
                if c >= 2:
                    dve.wait_ge(x3_done, c - 1)
                for s in range(B):
                    last = dve.tensor_scalar(hid[:, c % 2, s, :], x[:, c + s * TB, :], mv[:, i % 4, s, 0:1], hid_rstd[:, s:s + 1],
                                             ALU.subtract, ALU.mult)
                link(last)

            def add_projection(c):
                for i in range(2):
                    key = ("po", c, i)
                    ring.wait_done(dve, key)
                    xs = hid[:, c % 2, 2 * i:2 * i + 2, :]
                    dve.tensor_tensor(xs, ring.bank(key).rearrange("p (t d) -> p t d", t=2), xs, ALU.add).then_inc(ring.evacuated(key), 1)
                for i in range(2):
                    ring.wait_evacuated(dve, ("po", c, i))

            def router_diff(c):
                key = ("rt", c)
                ring.wait_done(dve, key)
                logits = ring.bank(key)[:, 0:B * E].rearrange("p (s e) -> p s e", e=E)
                link(dve.tensor_reduce(rm[:, 0, :], logits, AX.X, ALU.max))
                dve.tensor_tensor(rl[:, 0, :, :], logits, bc(rm[:, 0, :], 2, E), ALU.subtract).then_inc(ring.evacuated(key), 1)
                ring.wait_evacuated(dve, key)
                dve.tensor_copy(rm[:, 1, :], rm[:, 0, :]).then_inc(rl_diff, 1)

            def choose2(c):
                ts = slice(c, NT, TB)
                dve.wait_ge(rl_exp, c + 1)
                link(dve.tensor_reduce(rm[:, 0, :], rl[:, 1, :, :], AX.X, ALU.add))
                link(dve.reciprocal(rm[:, 1, :], rm[:, 0, :]))
                link(dve.tensor_tensor(score[:, :, :], rl[:, 1, :, :], bc(rm[:, 1, :], 2, E), ALU.mult))
                for s in range(B):
                    last = dve.max(top8[:, s, :], score[:, s, :])
                link(last)
                for s in range(B):
                    last = dve.max_index(idx8[:, s, :], top8[:, s, :], score[:, s, :])
                link(last)
                link(dve.tensor_copy(idxf[:, :, :], idx8[:, :, 0:2]))
                dve.tensor_copy(weight2[:, ts, :], top8[:, :, 0:2])
                dve.tensor_copy(dest_f[:, ts, :], idx8[:, :, 0:2])
                for k in range(2):
                    last = dve.tensor_tensor(pick[:, k, ts, :], bc(iota[:, 0:E], 1, B), bc(idxf[:, :, k], 2, E), ALU.is_equal)
                link(last)
                link(dve.tensor_tensor(chosen[:, ts, :], pick[:, 0, ts, :], pick[:, 1, ts, :], ALU.add))
                counts = earlier[:, c + 1:NT + 1:TB, :]
                if c:
                    link(dve.tensor_tensor(counts, earlier[:, c:NT:TB, :], chosen[:, ts, :], ALU.add))
                else:
                    link(dve.tensor_copy(counts, chosen[:, ts, :]))

            for i in range(NSTEP):
                c, phase = divmod(i, B)
                if phase == 1 and 0 <= c - 2 < TB:
                    attend_weights(c - 2)
                if i < NT:
                    context_max(i)
                if phase == 3 and 0 <= c - 2 < TB:
                    add_projection(c - 2)
                if phase == 2 and 0 <= c - 3 < TB:
                    router_diff(c - 3)
                if 2 <= i <= NT + 1:
                    add_context(i - 2)
                if phase == 2 and c + 1 < TB:
                    dve.wait_ge(combined_later, B * (c + 1))
                    normalize(("c", c + 1))
                if phase == 2 and 0 <= c - 3 < TB:
                    choose2(c - 3)
                if phase == 3 and 0 <= c - 2 < TB:
                    normalize(("l", c - 2))
                if phase == 0 and 0 <= c - 2 < TB - 2:
                    attend_scores(c - 2)
                if phase == 1 and 0 <= c - 1 < TB:
                    normalize(("d", c - 1))
                    start_hidden(c - 1)
            add_context(NT - 1)
            normalize(("d", TB - 1))
            attend_scores(TB - 2)
            router_diff(TB - 3)
            start_hidden(TB - 1)
            attend_weights(TB - 2)
            choose2(TB - 3)
            attend_scores(TB - 1)
            attend_weights(TB - 1)
            attend_values(dve, link, TB - 1, VALUES_DVE[TB - 1], prod, att_done)
            add_projection(TB - 2)
            normalize(("l", TB - 2))
            add_projection(TB - 1)
            normalize(("l", TB - 1))
            router_diff(TB - 2)
            choose2(TB - 2)
            dve.tensor_scalar(signed16[:, :, 0], token16[:, :, 0], 1.0, None, ALU.add)
            dve.tensor_scalar(signed16[:, :, 1], token16[:, :, 1], -1.0, -1.0, ALU.mult, ALU.add)
            router_diff(TB - 1)
            choose2(TB - 1)

            for b in range(1, B):
                ins = dve.tensor_tensor(earlier[:, b * TB + 1:(b + 1) * TB + 1, :], earlier[:, b * TB + 1:(b + 1) * TB + 1, :],
                                        bc(earlier[:, b * TB, :], 1, TB), ALU.add)
                if b < B - 1:
                    link(ins)
            ins.then_inc(picks2_ready, 1)
            key = ("rank2", 0)
            ring.wait_done(dve, key)
            counted = ring.bank(key)[:, 0:NT * E].rearrange("p (t e) -> p t e", e=E)
            for k in range(2):
                link(dve.tensor_tensor(ptmp[:, :, :], pick[:, k, :, :], counted, ALU.mult))
                link(dve.tensor_reduce(rank[:, :, k], ptmp[:, :, :], AX.X, ALU.add))
            dve.tensor_copy(etiles[:, 1, :], ring.bank(key)[:, 0:E]).then_inc(ring.evacuated(key), 1)
            link(dve.tensor_scalar(keep[:, :, :], rank[:, :, :], float(CAP1), None, ALU.is_lt))
            link(dve.tensor_copy(rank_i[:, :, :], rank[:, :, :]))
            link(dve.tensor_scalar(part_i[:, :, :], rank_i[:, :, :], P - 1, None, ALU.bitwise_and))
            dve.tensor_copy(rrow[:, NT_DVE:NT, :], part_i[:, NT_DVE:NT, :]).then_inc(rrow2_ready, 1)
            link(dve.tensor_copy(rrow16[:, :, :], part_i[:, :, :]))
            link(dve.tensor_scalar(part_i[:, :, :], rank_i[:, :, :], P.bit_length() - 1, None, ALU.arith_shift_right))
            link(dve.tensor_copy(rtile[:, :, :], part_i[:, :, :]))
            link(dve.scalar_tensor_tensor(rtile[:, :, :], dest_f[:, :, :], float(RT1), rtile[:, :, :], ALU.mult, ALU.add))
            link(dve.scalar_tensor_tensor(rtile[:, :, :], keep[:, :, :], -1000.0, rtile[:, :, :], ALU.mult, ALU.add))
            link(dve.tensor_scalar(rtile16[:, :, :], rtile[:, :, :], 1000.0, None, ALU.add))
            one_hots(rowhot[:, 0:NT_DVE, :, :], P, rrow16, NT_DVE)
            tile_onehots(NSLOT1, signed16).then_inc(hots2_ready, 1)
            link(dve.tensor_tensor(weight2[:, :, :], weight2[:, :, :], keep[:, :, :], ALU.mult))
            ring.wait_done(dve, ("source", 1))
            signed, token, to = (srows[:, i, :] for i in range(3))
            dve.tensor_copy(signed, ring.bank(("source", 1))[:, 0:NSLOT1]).then_inc(ring.evacuated(("source", 1)), 1)
            ring.wait_evacuated(dve, ("source", 1))
            link(dve.scalar_tensor_tensor(token, signed, -1.0, signed, ALU.mult, ALU.max))
            link(dve.tensor_scalar(source[:, 0:NSLOT1], token, -1.0, 0.0, ALU.add, ALU.max))
            dve.tensor_copy(eslot[:, 0:1], source[:, 0:1]).then_inc(slots2_ready, 1)
            link(dve.tensor_scalar(to, signed, 0.0, float(NT * P), ALU.is_lt, ALU.mult))
            link(dve.tensor_tensor(token, token, to, ALU.add))
            link(dve.tensor_scalar(to, signed, 0.0, None, ALU.is_equal))
            link(dve.tensor_tensor(to, to, dump_row[:, :], ALU.mult))
            link(dve.scalar_tensor_tensor(to, token, -1.0, to, ALU.add, ALU.add))
            for j, (_, parts) in enumerate(down_units):
                for on, ex, row0 in parts:
                    s = ex * RT1 + row0 // P
                    last = dve.tensor_copy(y_to[on, j:j + 1], to[0:on.stop - on.start, s:s + 1])
            last.then_inc(y_to_ready, 1)

            def weights_low(e):
                dve.wait_ge(w1_high, e + 1)
                dve.tensor_tensor(w1_parts[:, e % 2, 1, :], w1[:, e % NW, :, :].rearrange("p k f -> p (k f)"),
                                  w1_parts[:, e % 2, 0, :], ALU.subtract).then_inc(w1_low, 1)

            def expert_turned(e):
                for k in range(KC):
                    key = ("eT", e, k)
                    dve.wait_ge(eT_high, KC * e + k + 1)
                    dve.tensor_tensor(eT_parts[:, e % 2, 1, k, :], ring.bank(key)[:, 0:CAP1], eT_parts[:, e % 2, 0, k, :],
                                      ALU.subtract).then_inc(ring.evacuated(key), 1)

            weights_low(0)
            expert_turned(0)
            for e in range(E):
                dve.wait_ge(w2_high, e + 1)
                dve.tensor_tensor(w2_parts[:, e % 2, 1, :], w2[:, e % NW, :, :].rearrange("p f d -> p (f d)"),
                                  w2_parts[:, e % 2, 0, :], ALU.subtract).then_inc(w2_low, 1)
                for j in range(FC1):
                    dve.wait_ge(h1_high, FC1 * e + j + 1)
                    dve.tensor_tensor(h1_parts[:, e % 2, 1, j, :], h1[:, e % 2, j, :], h1_parts[:, e % 2, 0, j, :],
                                      ALU.subtract).then_inc(h1_low, 1)
                if e + 1 < E:
                    expert_turned(e + 1)
                    weights_low(e + 1)
                for j, (at_expert, parts) in enumerate(down_units):
                    if at_expert == e:
                        key = ("h2", j)
                        if j >= 3:
                            dve.wait_ge(y2_scattered[j % 3], 16 * (j // 3))
                        ring.wait_done(dve, key)
                        dve.tensor_copy(y2[:, j % 3, :], ring.bank(key)[:, 0:D]).then_inc(ring.evacuated(key), 1)
            dve.wait_ge(x3_done, TB)
            for t in range(NT):
                dve.wait_ge(y_both_loaded[t], 16)
                link(dve.scalar_tensor_tensor(x[:, t, :], y_both[:, t, 0, :], weight2[:, t, 0:1], x[:, t, :], ALU.mult, ALU.add))
                dve.scalar_tensor_tensor(x[:, t, :], y_both[:, t, 1, :], weight2[:, t, 1:2], x[:, t, :], ALU.mult,
                                         ALU.add).then_inc(finished, 1)


def lay_out(inputs):
    f = {k: np.asarray(v) for k, v in inputs.items()}

    def chunks(w):
        return np.ascontiguousarray(w.reshape(-1, P, w.shape[-1]).transpose(1, 0, 2))

    def halves(v):
        return [v[:P], v[P:]]

    gq, gk = f["L0_xattn_q_gamma"], f["L0_xattn_k_gamma"]
    cols = []
    for n in ("L0_xattn_ln_x_g", "L0_xattn_ln_x_b", "L0_xattn_ln_l_g", "L0_xattn_ln_l_b", "L1_ffn_ln1_weight", "L1_ffn_ln1_bias"):
        cols += halves(f[n])
    cols += [np.concatenate([gq, gq]), np.concatenate([gk, gk])]
    rows = np.concatenate([f["L0_xattn_b_out"], f["L1_ffn_ln2_weight"], f["L1_ffn_ln2_bias"], gq, gk])
    wg, wu, wd = f["L0_ffn_w_gate"], f["L0_ffn_w_up"], f["L0_ffn_w_down"]
    gu = np.concatenate([wg, wu], axis=2)
    return {
        "x": f["x"],
        "ctx": f["ctx_1024"],
        "ctxT": np.ascontiguousarray(f["ctx_1024"].transpose(2, 0, 1)).reshape(KC, P, B, SC).transpose(1, 0, 2, 3).copy(),
        "mask": np.ascontiguousarray(f["mask_BxS2_bk0"].reshape(B, CTB, P).transpose(2, 0, 1).reshape(P, B * CTB)).view(np.uint32),
        "cols": np.ascontiguousarray(np.stack(cols, axis=1)),
        "rows": np.ascontiguousarray(np.broadcast_to(rows, (P, NROW))),
        "wq": chunks(f["L0_xattn_W_q"]),
        "wkv": chunks(f["L0_xattn_W_kv"]),
        "wout": chunks(f["L0_xattn_W_out"]),
        "gate_w": chunks(f["L0_ffn_gate_w"].T),
        "sh_gu": chunks(np.concatenate([f["L0_ffn_ws_gate"], f["L0_ffn_ws_up"]], axis=1)),
        "sh_dn": f["L0_ffn_ws_down"],
        "e_gu": np.ascontiguousarray(gu.reshape(E, KC, P, 2 * M0).transpose(2, 1, 0, 3)),
        "e_dn": np.ascontiguousarray(wd.transpose(1, 0, 2)),
        "qkv_w": chunks(f["L1_ffn_qkv_weight"].T),
        "proj_w": chunks(f["L1_ffn_proj_weight"].T),
        "router_w": chunks(f["L1_ffn_router_weight"].T),
        "w1": np.ascontiguousarray(f["L1_ffn_moe_w1"].transpose(0, 2, 1).reshape(E, KC, P, F1).transpose(0, 2, 1, 3)),
        "w2": np.ascontiguousarray(f["L1_ffn_moe_w2"].transpose(0, 2, 1).reshape(E, FC1, P, D).transpose(0, 2, 1, 3)),
    }


def kernel(**inputs):
    import concourse.bacc as bacc
    from concourse.bass_utils import run_bass_kernel_spmd as run

    nc = bacc.Bacc("TRN2", target_bir_lowering=False, num_devices=1)
    arrays = lay_out(inputs)
    a = {n: nc.dram_tensor(f"in_{n}", v.shape, mybir.dt.from_np(v.dtype), kind="ExternalInput").ap() for n, v in arrays.items()}
    out = nc.dram_tensor("out", (B, S, D), F32, kind="ExternalOutput").ap()
    build(nc, a, out)
    r = run(nc, [{f"in_{n}": v for n, v in arrays.items()}], core_ids=[0])
    return r.results[0]["out"]
```
